# Optimizing a Trainium2 kernel written in Bass

```python
import numpy as np
import jax
import jax.numpy as jnp

def _softmax(x, axis=-1):
    return jax.nn.softmax(x, axis=axis)

def _gelu(x):
    return jax.nn.gelu(x, approximate=True)

def _silu(x):
    return jax.nn.silu(x)

def _sigmoid(x):
    return jax.nn.sigmoid(x)

def _layernorm(x, axis=-1, eps=1e-05):
    m = jnp.mean(x, axis=axis, keepdims=True)
    v = jnp.var(x, axis=axis, keepdims=True)
    return (x - m) / jnp.sqrt(v + eps)

def _scatter_add(tgt, idx, src, axis=0):
    return tgt.at[idx].add(src)

def _segment_sum(src, seg, n):
    return jax.ops.segment_sum(src, seg, n)
kernel_name = 'mk_seq_preln_d2_jaxref_r8_997d31'

def setup_inputs(seed: int=0):
    np.random.seed(seed)
    _w = jnp.asarray

    def _L0_attn_setup():
        import jax, jax.numpy as jnp
        import numpy as np
        D_MODEL = 256
        N_HEADS = 16
        HEAD_DIM = D_MODEL // N_HEADS
        B, T = (2, 256)
        key = jax.random.key(seed)
        ks = jax.random.split(key, 9)
        s = 0.02
        x = jax.random.normal(ks[0], (B, T, D_MODEL), dtype=jnp.float32)
        Wq = jax.random.normal(ks[1], (N_HEADS, D_MODEL, HEAD_DIM), dtype=jnp.float32) * s
        bq = jax.random.normal(ks[2], (N_HEADS, HEAD_DIM), dtype=jnp.float32) * s
        Wk = jax.random.normal(ks[3], (N_HEADS, D_MODEL, HEAD_DIM), dtype=jnp.float32) * s
        bk = jax.random.normal(ks[4], (N_HEADS, HEAD_DIM), dtype=jnp.float32) * s
        Wv = jax.random.normal(ks[5], (N_HEADS, D_MODEL, HEAD_DIM), dtype=jnp.float32) * s
        bv = jax.random.normal(ks[6], (N_HEADS, HEAD_DIM), dtype=jnp.float32) * s
        Wo = jax.random.normal(ks[7], (D_MODEL, D_MODEL), dtype=jnp.float32) * s
        bo = jax.random.normal(ks[8], (D_MODEL,), dtype=jnp.float32) * s
        return {'x': x, 'Wq': Wq, 'bq': bq, 'Wk': Wk, 'bk': bk, 'Wv': Wv, 'bv': bv, 'Wo': Wo, 'bo': bo}
    _L0_attn_in = _L0_attn_setup()

    def _L0_ffn_setup():
        import jax, jax.numpy as jnp
        import numpy as np
        TOP_K = 8
        NUM_GROUPS = 8
        key = jax.random.key(seed)
        ks = jax.random.split(key, 6)
        T_B, T_S, H, I, E, G = (1, 256, 256, 96, 32, NUM_GROUPS)
        hidden_states = jax.random.normal(ks[0], (T_B, T_S, H), dtype=jnp.float32)
        gate_weight = jax.random.normal(ks[1], (E, H), dtype=jnp.float32) * 0.02
        gate_up_proj = jax.random.normal(ks[2], (E, 2 * I, H), dtype=jnp.float32) * 0.02
        down_proj = jax.random.normal(ks[3], (E, H, I), dtype=jnp.float32) * 0.02
        merge_groups = jax.random.randint(ks[4], (E,), 0, G, dtype=jnp.int64)
        merge_groups = merge_groups.at[:G].set(jnp.arange(G, dtype=jnp.int64))
        dominant_experts = jax.random.randint(ks[5], (G,), 0, E, dtype=jnp.int64)
        return {'hidden_states': hidden_states, 'gate_weight': gate_weight, 'gate_up_proj': gate_up_proj, 'down_proj': down_proj, 'merge_groups': merge_groups, 'dominant_experts': dominant_experts}
    _L0_ffn_in = _L0_ffn_setup()

    def _L1_attn_setup():
        import jax, jax.numpy as jnp
        import numpy as np
        import math
        E = 256
        H = 16
        D = E // H

        def _alibi_slopes(n):

            def pow2_slopes(n):
                start = 2 ** (-2 ** (-(math.log2(n) - 3)))
                return [start * start ** i for i in range(n)]
            if math.log2(n).is_integer():
                return pow2_slopes(n)
            c = 2 ** math.floor(math.log2(n))
            return pow2_slopes(c) + _alibi_slopes(2 * c)[::2][:n - c]

        def _alibi_bias(seq_len):
            slopes = jnp.asarray(_alibi_slopes(H), dtype=jnp.float32)
            pos = jnp.arange(seq_len)
            rel = jnp.abs(pos[None, :] - pos[:, None]).astype(jnp.float32)
            return -slopes[:, None, None] * rel[None, :, :]
        key = jax.random.key(seed)
        ks = jax.random.split(key, 5)
        B, S = (2, 256)
        scale = 1.0 / math.sqrt(E)
        x = jax.random.normal(ks[0], (B, S, E), dtype=jnp.float32)
        Wq = jax.random.normal(ks[1], (E, E), dtype=jnp.float32) * scale
        Wk = jax.random.normal(ks[2], (E, E), dtype=jnp.float32) * scale
        Wv = jax.random.normal(ks[3], (E, E), dtype=jnp.float32) * scale
        Wo = jax.random.normal(ks[4], (E, E), dtype=jnp.float32) * scale
        z = jnp.zeros((E,), dtype=jnp.float32)
        return {'x': x, 'Wq': Wq, 'bq': z, 'Wk': Wk, 'bk': z, 'Wv': Wv, 'bv': z, 'Wo': Wo, 'bo': z}
    _L1_attn_in = _L1_attn_setup()

    def _L1_ffn_setup():
        import jax, jax.numpy as jnp
        import numpy as np
        K = 2

        def gelu(v):
            return jax.nn.gelu(v, approximate=False)
        key = jax.random.key(seed)
        ks = jax.random.split(key, 10)
        B, S, D, H, E = (4, 256, 256, 128, 8)
        SH = 2 * H
        u = lambda k_, shape, b: jax.random.uniform(k_, shape, jnp.float32, -b, b)
        return {'x': jax.random.normal(ks[0], (B, S, D), jnp.float32), 'gate_w': u(ks[1], (D, E), 1.0 / D), 'w1': u(ks[2], (E, D, H), 1.0 / D), 'b1': u(ks[3], (E, H), 1.0 / np.sqrt(D)), 'w2': u(ks[4], (E, H, D), 1.0 / H), 'b2': u(ks[5], (E, D), 1.0 / np.sqrt(H)), 'shared_w1': u(ks[6], (D, SH), 1.0 / D), 'shared_b1': u(ks[7], (SH,), 1.0 / np.sqrt(D)), 'shared_w2': u(ks[8], (SH, D), 1.0 / SH), 'shared_b2': u(ks[9], (D,), 1.0 / np.sqrt(SH))}
    _L1_ffn_in = _L1_ffn_setup()
    _d = {'L0_attn_x': _L0_attn_in['x'], 'L0_attn_Wq': _L0_attn_in['Wq'], 'L0_attn_bq': _L0_attn_in['bq'], 'L0_attn_Wk': _L0_attn_in['Wk'], 'L0_attn_bk': _L0_attn_in['bk'], 'L0_attn_Wv': _L0_attn_in['Wv'], 'L0_attn_bv': _L0_attn_in['bv'], 'L0_attn_Wo': _L0_attn_in['Wo'], 'L0_attn_bo': _L0_attn_in['bo'], 'L0_ffn_gate_weight': _L0_ffn_in['gate_weight'], 'L0_ffn_gate_up_proj': _L0_ffn_in['gate_up_proj'], 'L0_ffn_down_proj': _L0_ffn_in['down_proj'], 'L0_ffn_merge_groups': _L0_ffn_in['merge_groups'], 'L0_ffn_dominant_experts': _L0_ffn_in['dominant_experts'], 'L1_attn_Wq': _L1_attn_in['Wq'], 'L1_attn_bq': _L1_attn_in['bq'], 'L1_attn_Wk': _L1_attn_in['Wk'], 'L1_attn_bk': _L1_attn_in['bk'], 'L1_attn_Wv': _L1_attn_in['Wv'], 'L1_attn_bv': _L1_attn_in['bv'], 'L1_attn_Wo': _L1_attn_in['Wo'], 'L1_attn_bo': _L1_attn_in['bo'], 'L1_ffn_gate_w': _L1_ffn_in['gate_w'], 'L1_ffn_w1': _L1_ffn_in['w1'], 'L1_ffn_b1': _L1_ffn_in['b1'], 'L1_ffn_w2': _L1_ffn_in['w2'], 'L1_ffn_b2': _L1_ffn_in['b2'], 'L1_ffn_shared_w1': _L1_ffn_in['shared_w1'], 'L1_ffn_shared_b1': _L1_ffn_in['shared_b1'], 'L1_ffn_shared_w2': _L1_ffn_in['shared_w2'], 'L1_ffn_shared_b2': _L1_ffn_in['shared_b2']}
    _x0 = _d['L0_attn_x']
    _d['L0_attn_x'] = jax.random.normal(jax.random.fold_in(jax.random.key(seed), 1), (1, 2048, 256), dtype=_x0.dtype)
    del _x0
    return _d

def reference(L0_attn_x, L0_attn_Wq, L0_attn_bq, L0_attn_Wk, L0_attn_bk, L0_attn_Wv, L0_attn_bv, L0_attn_Wo, L0_attn_bo, L0_ffn_gate_weight, L0_ffn_gate_up_proj, L0_ffn_down_proj, L0_ffn_merge_groups, L0_ffn_dominant_experts, L1_attn_Wq, L1_attn_bq, L1_attn_Wk, L1_attn_bk, L1_attn_Wv, L1_attn_bv, L1_attn_Wo, L1_attn_bo, L1_ffn_gate_w, L1_ffn_w1, L1_ffn_b1, L1_ffn_w2, L1_ffn_b2, L1_ffn_shared_w1, L1_ffn_shared_b1, L1_ffn_shared_w2, L1_ffn_shared_b2):

    def _L0_attn_ref(x, Wq, bq, Wk, bk, Wv, bv, Wo, bo):
        import jax, jax.numpy as jnp
        import numpy as np
        D_MODEL = 256
        N_HEADS = 16
        HEAD_DIM = D_MODEL // N_HEADS
        B, T = (2, 256)
        Bn, Tn, C = x.shape
        H, _, D = Wq.shape
        scale = D ** (-0.5)
        q = jnp.einsum('btc,hcd->bhtd', x, Wq) + bq[None, :, None, :]
        k = jnp.einsum('btc,hcd->bhtd', x, Wk) + bk[None, :, None, :]
        v = jnp.einsum('btc,hcd->bhtd', x, Wv) + bv[None, :, None, :]
        scores = jnp.einsum('bhtd,bhsd->bhts', q, k) * scale
        neg = jnp.finfo(scores.dtype).min
        causal = jnp.triu(jnp.full((Tn, Tn), neg, dtype=scores.dtype), k=1)
        probs = jax.nn.softmax(scores + causal, axis=-1)
        y = jnp.einsum('bhts,bhsd->bhtd', probs, v)
        y = y.transpose(0, 2, 1, 3).reshape(Bn, Tn, H * D)
        return y @ Wo + bo

    def _L0_ffn_ref(hidden_states, gate_weight, gate_up_proj, down_proj, merge_groups, dominant_experts):
        import jax, jax.numpy as jnp
        import numpy as np
        TOP_K = 8
        NUM_GROUPS = 8
        B, S, H = hidden_states.shape
        G = dominant_experts.shape[0]
        x = hidden_states.reshape(-1, H)
        logits = jnp.einsum('th,eh->te', x, gate_weight)
        probs = jax.nn.softmax(logits.astype(jnp.float32), axis=-1).astype(logits.dtype)
        top_val, top_idx = jax.lax.top_k(probs, TOP_K)
        top_val = top_val / jnp.sum(top_val, axis=-1, keepdims=True)
        sel_group = merge_groups[top_idx]
        onehot = jax.nn.one_hot(sel_group, G, dtype=top_val.dtype)
        w_tg = jnp.einsum('tk,tkg->tg', top_val, onehot)
        gu = gate_up_proj[dominant_experts]
        dn = down_proj[dominant_experts]
        h = jnp.einsum('th,goh->tgo', x, gu)
        gate, up = jnp.split(h, 2, axis=-1)
        act = jax.nn.silu(gate) * up
        y = jnp.einsum('tgi,ghi->tgh', act, dn)
        out = jnp.einsum('tg,tgh->th', w_tg, y)
        return out.reshape(B, S, H)

    def _L1_attn_ref(x, Wq, bq, Wk, bk, Wv, bv, Wo, bo):
        import jax, jax.numpy as jnp
        import numpy as np
        import math
        E = 256
        H = 16
        D = E // H

        def _alibi_slopes(n):

            def pow2_slopes(n):
                start = 2 ** (-2 ** (-(math.log2(n) - 3)))
                return [start * start ** i for i in range(n)]
            if math.log2(n).is_integer():
                return pow2_slopes(n)
            c = 2 ** math.floor(math.log2(n))
            return pow2_slopes(c) + _alibi_slopes(2 * c)[::2][:n - c]

        def _alibi_bias(seq_len):
            slopes = jnp.asarray(_alibi_slopes(H), dtype=jnp.float32)
            pos = jnp.arange(seq_len)
            rel = jnp.abs(pos[None, :] - pos[:, None]).astype(jnp.float32)
            return -slopes[:, None, None] * rel[None, :, :]
        B, S, _ = x.shape

        def proj(W, b):
            return (x @ W.T + b).reshape(B, S, H, D).transpose(0, 2, 1, 3)
        q = proj(Wq, bq)
        k = proj(Wk, bk)
        v = proj(Wv, bv)
        scores = jnp.einsum('bhqd,bhkd->bhqk', q, k) / math.sqrt(D)
        causal = jnp.triu(jnp.ones((S, S), dtype=bool), k=1)
        scores = jnp.where(causal[None, None], -jnp.inf, scores)
        scores = scores + _alibi_bias(S)[None]
        probs = jax.nn.softmax(scores, axis=-1)
        out = jnp.einsum('bhqk,bhkd->bhqd', probs, v)
        out = out.transpose(0, 2, 1, 3).reshape(B, S, E)
        return out @ Wo.T + bo

    def _L1_ffn_ref(x, gate_w, w1, b1, w2, b2, shared_w1, shared_b1, shared_w2, shared_b2):
        import jax, jax.numpy as jnp
        import numpy as np
        K = 2

        def gelu(v):
            return jax.nn.gelu(v, approximate=False)
        B, S, D = x.shape
        E = gate_w.shape[1]
        xf = x.reshape(-1, D)
        logits = xf @ gate_w
        top_logits, top_idx = jax.lax.top_k(logits, K)
        top_gates = jax.nn.softmax(top_logits, axis=-1)
        gates = jnp.sum(jax.nn.one_hot(top_idx, E, dtype=xf.dtype) * top_gates[..., None], axis=1)
        h = gelu(jnp.einsum('nd,edh->neh', xf, w1) + b1)
        out_e = jnp.einsum('neh,ehd->ned', h, w2) + b2
        routed = jnp.einsum('ne,ned->nd', gates, out_e)
        shared = gelu(xf @ shared_w1 + shared_b1) @ shared_w2 + shared_b2
        return (routed + shared).reshape(B, S, D)
    x = L0_attn_x
    x = x + _L0_attn_ref(_layernorm(x, axis=-1), L0_attn_Wq, L0_attn_bq, L0_attn_Wk, L0_attn_bk, L0_attn_Wv, L0_attn_bv, L0_attn_Wo, L0_attn_bo)
    x = x + _L0_ffn_ref(_layernorm(x, axis=-1), L0_ffn_gate_weight, L0_ffn_gate_up_proj, L0_ffn_down_proj, L0_ffn_merge_groups, L0_ffn_dominant_experts)
    x = x + _L1_attn_ref(_layernorm(x, axis=-1), L1_attn_Wq, L1_attn_bq, L1_attn_Wk, L1_attn_bk, L1_attn_Wv, L1_attn_bv, L1_attn_Wo, L1_attn_bo)
    x = x + _L1_ffn_ref(_layernorm(x, axis=-1), L1_ffn_gate_w, L1_ffn_w1, L1_ffn_b1, L1_ffn_w2, L1_ffn_b2, L1_ffn_shared_w1, L1_ffn_shared_b1, L1_ffn_shared_w2, L1_ffn_shared_b2)
    return x

_drawn_inputs = setup_inputs


def setup_inputs(seed=0):
    import zlib

    import numpy as np

    out = dict(_drawn_inputs(seed))
    spreads = {'L1_attn_bq': (0.0, 1.578),
     'L1_attn_bk': (0.0, 2.0),
     'L1_attn_bv': (0.0, 0.419),
     'L1_attn_bo': (0.0, 0.426)}
    factors = {'L0_attn_Wq': 8.0,
     'L0_attn_bq': 8.0,
     'L0_attn_Wk': 8.0,
     'L0_attn_bk': 64.0,
     'L0_attn_Wv': 6.015,
     'L0_attn_bv': 6.152,
     'L0_attn_Wo': 4.054,
     'L0_ffn_gate_weight': 8.0,
     'L0_ffn_gate_up_proj': 8.0,
     'L0_ffn_down_proj': 8.0,
     'L1_ffn_w1': 50.873,
     'L1_ffn_b1': 52.473,
     'L1_ffn_w2': 36.345,
     'L1_ffn_shared_w1': 51.254,
     'L1_ffn_shared_b1': 53.994,
     'L1_ffn_shared_w2': 37.522,
     'L0_attn_bo': 3.132,
     'L1_ffn_gate_w': 4.547,
     'L1_ffn_b2': 7.901,
     'L1_ffn_shared_b2': 7.908}
    for name, (base, spread) in spreads.items():
        noise = np.random.default_rng([zlib.crc32(name.encode()), seed]).standard_normal(out[name].shape)
        drawn = base * np.exp(spread * noise) if base else spread * noise
        out[name] = jnp.asarray(drawn.astype(out[name].dtype))
    for name, factor in factors.items():
        out[name] = (out[name] * factor).astype(out[name].dtype)
    return out
```

```python
from contextlib import ExitStack

import concourse.bass as bass
from concourse import mybir

F32 = mybir.dt.float32
BF16 = mybir.dt.bfloat16
I32 = mybir.dt.int32
U32 = mybir.dt.uint32
ALU = mybir.AluOpType
ACT = mybir.ActivationFunctionType
AX = mybir.AxisListType

P = 128
T = 2048
D = 256
KD = D // P
NT = T // P
TB = 512
NB = T // TB
TPB = TB // P
H = 16
HD = D // H
G = 4
NG = H // G
EPS = 1e-5
NEG = -3.0e38

R_SLOPE = 0
R_POS = 6
R_QK = 12
R_MAX = R_QK + 6 * HD
KA = R_MAX
KB = R_MAX + 3
Q_PARTS = (0, 0, 0, 1, 1, 2)
K_PARTS = (0, 1, 2, 0, 1, 0)

E0 = 32
G0 = 8
I0 = 96
M0 = G0 * I0 // P
E1 = 8
H1 = 128
M1 = E1 + 2
MMAX = max(M0, M1)

ACC_BANKS = (0, 1)
TR_BANK = 2
SIDE_BANK = 3
HID_BANKS = (4, 5, 6, 7)
O_BANK = 4
A_BANKS = (5, 6, 7)


def pass_a_items():
    blocks = []
    for b in range(NB):
        items = []
        for i in range(TPB * b, TPB * b + TPB):
            keys = (i + 1) * P
            for c in range(keys // TB):
                items += [(i, h, 1, c * TB, TB) for h in range(G)]
            w = keys % TB
            if w:
                n = min(G, TB // w)
                items += [(i, h, n, keys - w, w) for h in range(0, G, n)]
        blocks.append(items)
    return blocks


def pass_b_units():
    return [(b, j, TB - max(0, j - TPB * b) * P) for b in range(NB) for j in range(TPB * (b + 1))]


UNITS = pass_b_units()
NU = len(UNITS)
A_BLOCKS = pass_a_items()
A_STEPS = [s for b in range(NB) for s in [("max", it) for it in A_BLOCKS[b]] + [("row", b)]]
NA = len(A_STEPS)
assert NA % len(A_BANKS) == 0 and NU % 2 == 0


def a_cost(step):
    return step[1][2] * step[1][4] if step[0] == "max" else 0


LEAD = 66 * P * G


def head_length():
    cost, n = 0, 0
    while cost < LEAD:
        cost += a_cost(A_STEPS[n])
        n += 1
    return n


NHEAD = head_length()


def slots():
    todo = [(0, s) for s in A_STEPS[NHEAD:]] + [(1, s) for s in A_STEPS[:NHEAD]]
    out, at, done_a, done_b = [], 0, 0, 0
    for u, (_, _, w) in enumerate(UNITS):
        done_b += w * G
        mine = []
        while at < len(todo) and (done_a < done_b or u == NU - 1):
            if todo[at][1][0] == "row" and mine and u < NU - 1:
                break
            mine.append((todo[at][0], at, todo[at][1]))
            done_a += a_cost(todo[at][1])
            at += 1
        out.append(mine)
    assert at == len(todo)
    return out


SLOTS = slots()


ACC_ORDER = [("out", p) for p in range(4)]
for _b in range(NB):
    ACC_ORDER += [("out", p) for p in (2 * _b + 4, 2 * _b + 5) if p < NT // 2]
    ACC_ORDER += [("down", 2 * _b), ("down", 2 * _b + 1)]


def two_layers(nc, x, wq0, bq0, wk0, bk0, wv0, bv0, wo0, bo0, router0, gate_up0, down0, merge0, dominant0,
               wq1, bq1, wk1, bk1, wv1, bv1, wo1, bo1, router1, w1, b1, w2, b2, sw1, sb1, sw2, sb2,
               slope_parts, expert_of_row, out):
    with ExitStack() as ctx:
        def sb(name, shape, dt=F32):
            return ctx.enter_context(nc.sbuf_tensor(name, shape, dt))

        def sem(name):
            return ctx.enter_context(nc.semaphore(name))

        def sems(name, n):
            return [sem(f"{name}{i}") for i in range(n)]

        psum = ctx.enter_context(nc.psum_tensor("psum", [P, 8, TB], F32))

        xs = sb("xs", [P, NT, D])
        xT = sb("xT", [P, KD, T])
        yT = xT
        q_stack = sb("q_stack", [P, 2, NB, G, TB], BF16)
        k_stack = sb("k_stack", [P, 2, G, T], BF16)
        v_stage = sb("v_stage", [P, 2, NT, G, HD, 2])
        work = sb("work", [P, 8192])
        v_all = work[:, 0:NT * D].rearrange("p (i c) -> p i c", i=NT)
        probs = work[:, 4096:8192].rearrange("p (s k c) -> p s k c", s=4, k=2)
        qk_f = work[:, 4096:5120].rearrange("p (s c) -> p s c", s=2)
        qk_p = work[:, 5120:8192].bitcast(BF16).rearrange("p (s r c) -> p s r c", s=4, r=3)
        hidden = work[:, 0:MMAX * TB].rearrange("p (m c) -> p m c", m=MMAX)
        act_out = work[:, 5120:5120 + 2 * TB].rearrange("p (s c) -> p s c", s=2)
        act_up = work[:, 6144:6144 + 2 * TB].rearrange("p (s c) -> p s c", s=2)
        w_attn = sb("w_attn", [P, 4, KD, D])
        w_mix = sb("w_mix", [P, 5120])
        gate_w = w_mix[:, 0:KD * G0 * I0].rearrange("p (k c) -> p k c", k=KD)
        up_w = w_mix[:, 1536:1536 + KD * G0 * I0].rearrange("p (k c) -> p k c", k=KD)
        down_w = w_mix[:, 3072:3072 + M0 * D].rearrange("p (m c) -> p m c", m=M0)
        w1_s = w_mix[:, 0:KD * E1 * H1].rearrange("p (k e c) -> p k e c", k=KD, e=E1)
        sw1_s = w_mix[:, 2048:2048 + KD * D].rearrange("p (k c) -> p k c", k=KD)
        w2_s = w_mix[:, 2560:2560 + M1 * D].rearrange("p (m c) -> p m c", m=M1)
        area = sb("area", [P, 2560])
        xn = area[:, 0:2 * TPB * D].rearrange("p (s q c) -> p s q c", s=2, q=TPB)
        y_n = area[:, 0:2 * TB].rearrange("p (s c) -> p s c", s=2)
        o_t = area[:, 1024:1024 + TB]
        mt = area[0:G * TPB, 1536:1536 + 2 * P].rearrange("p (s c) -> p s c", s=2)
        mr = area[0:G * TPB, 1792:1792 + 2 * P].rearrange("p (s c) -> p s c", s=2)
        mrow = area[0:G * TPB, 2048:2048 + 3 * P].bitcast(BF16).rearrange("p (s r c) -> p s r c", s=2, r=3)
        stats = sb("stats", [P, TPB, 6])
        mv = sb("mv", [P, TPB, 2])
        lnt = sb("lnt", [P, 4, TPB])
        rstd = sb("rstd", [P, TPB])
        ident = sb("ident", [P, P])
        ident_bf = sb("ident_bf", [P, P], BF16)
        tri = sb("tri", [P, P], BF16)
        zeros = sb("zeros", [G * TPB, P])
        spare = sb("spare", [1, 16])
        bcol = sb("bcol", [P, 2, 2, KD])
        bcol4 = sb("bcol4", [P, 2, 2, KD])
        brow = sb("brow", [P, 5, D])
        hb = sb("hb", [P, M1])
        b2_s = sb("b2_s", [E1, D])
        r0_s = sb("r0_s", [P, KD, E0])
        r1_s = sb("r1_s", [P, KD, E1])
        dom = sb("dom", [1, G0], I32)
        merge_i = sb("merge_i", [3 * E0, 1], I32)
        merge_f = sb("merge_f", [3 * E0, 1])
        erow = sb("erow", [3 * E1, 1])
        slope_c = sb("slope_c", [3 * H, 1])
        spread0 = sb("spread0", [3 * E0, G0 * I0], BF16)
        spread1 = sb("spread1", [3 * E1, E1 * H1], BF16)
        iota8 = sb("iota8", [P, TPB, E1])
        qk_r = sb("qk_r", [P, 2, TB])
        mx = sb("mx", [P, G, NT, NB])
        nmax = sb("nmax", [P, G, TPB])
        o_r = sb("o_r", [P, TB // 32])
        o_n = sb("o_n", [P, TB])
        rt = sb("rt", [P, 6, TPB, E0])
        rmax = sb("rmax", [P, TPB, 8])
        ridx = sb("ridx", [P, TPB, 8], U32)
        rsmall = sb("rsmall", [P, 8, TPB])
        gparts = sb("gparts", [P, TPB, 3 * E0], BF16)
        gT = sb("gT", [3 * E0, TB], BF16)
        gTf = work[0:E1, 7168:7168 + TB]
        iota_g = work[0:3 * E0, 0:G0 * I0].rearrange("p (g c) -> p g c", g=G0)
        iota_e = work[0:3 * E1, 1024:1024 + E1 * H1].rearrange("p (e c) -> p e c", e=E1)
        slope_q = k_stack[0:3 * H, 0, 0, :]
        slope_k = k_stack[0:3 * H, 0, 1, :]
        zero_rows = k_stack[0:3 * H, 0, 2, :]
        pos_hi = k_stack[0:1, 1, 0, :]
        pos_lo = k_stack[0:1, 1, 1, :]

        q_parts = nc.dram_tensor("q_parts", [3, NG, NB, G, HD, TB], BF16, kind="Internal").ap()
        k_parts = nc.dram_tensor("k_parts", [3, D, T], BF16, kind="Internal").ap()
        slopes_q = nc.dram_tensor("slopes_q", [2, 3, H, TB], BF16, kind="Internal").ap()
        slopes_k = nc.dram_tensor("slopes_k", [2, 3, H, T], BF16, kind="Internal").ap()
        positions = nc.dram_tensor("positions", [2, T], BF16, kind="Internal").ap()

        x_in = sems("x_in", NB)
        wattn_in = sems("wattn_in", 2)
        wmix_in = sems("wmix_in", 2)
        small_in = sem("small_in")
        dom_in = sem("dom_in")
        const_pool = sem("const_pool")
        const_dve = sem("const_dve")
        table_out = sem("table_out")
        fixed_in = sem("fixed_in")
        ln_stat = sems("ln_stat", 4)
        ln_var = sems("ln_var", 4)
        ln_root = sems("ln_root", 4)
        ln_xn = sems("ln_xn", 4)
        ln_tr = sems("ln_tr", 4)
        ln_xT = sems("ln_xT", 4)
        pj_mm = sems("pj_mm", 2)
        pj_act = sems("pj_act", 2)
        pj_dve = sems("pj_dve", 2)
        pj_cut = sems("pj_cut", 2)
        pj_parts = sems("pj_parts", 2)
        pj_out = [sems(f"pj_out{l}_", 4) for l in range(2)]
        pj_v = sems("pj_v", 2)
        xb_done = sems("xb_done", 3)
        at_stack = sems("at_stack", 2)
        at_ones = sems("at_ones", 2)
        at_vst = sems("at_vst", 2)
        at_score = sems("at_score", 2)
        at_exp = sems("at_exp", 2)
        at_pv = sems("at_pv", 2)
        at_ofree = sems("at_ofree", 2)
        at_dve = sems("at_dve", 2)
        at_yn = sems("at_yn", 2)
        at_y = [sems(f"at_y{l}_", 2) for l in range(2)]
        a_mm = sems("a_mm", 2)
        a_max = sems("a_max", 2)
        a_nm = sems("a_nm", 2)
        a_cut = sems("a_cut", 2)
        a_split = sems("a_split", 2)
        a_row = [sems(f"a_row{l}_", 2) for l in range(2)]
        acc_mm = sems("acc_mm", 2)
        x_add = sems("x_add", 2)
        side_mm = sems("side_mm", 2)
        side_free = sems("side_free", 2)
        r_dve = sems("r_dve", 2)
        r_soft = sems("r_soft", 2)
        r_exp = sems("r_exp", 2)
        r_gates = sems("r_gates", 2)
        hid_mm = sems("hid_mm", 2)
        hid_act = sems("hid_act", 2)
        hid_up = sems("hid_up", 2)
        hid_done = sems("hid_done", 2)
        down_mm = sems("down_mm", 2)
        x_out = sem("x_out")

        SMALL = 19
        MIX_DMAS = 3 * G0 + sum(I0 * g % P + I0 > P for g in range(G0))
        CONST_POOL = 14
        CONST_DVE = 8
        A_W = ((wq0, wk0, wv0, wo0), (wq1, wk1, wv1, wo1))
        SIDE = (2 + M0, 3 + E1)
        GATE_ITEMS = (2, 3)

        block = ctx.enter_context(nc.Block())

        @block.sync
        def _(sp):
            xv = x.rearrange("a (i p) c -> p (a i) c", p=P)
            for b in range(NB):
                sp.dma_start(xs[:, b * TPB:(b + 1) * TPB, :], xv[:, b * TPB:(b + 1) * TPB, :]).then_inc(x_in[b], 16)

            def load_attn(l):
                for n, w in enumerate(A_W[l]):
                    sp.dma_start(w_attn[:, n, :, :], w.rearrange("(k p) c -> p k c", p=P)).then_inc(wattn_in[l], 16)

            load_attn(0)
            sp.wait_ge(const_dve, CONST_DVE)
            sp.wait_ge(const_pool, CONST_POOL)
            for l, (tq, tk) in enumerate(((zero_rows, zero_rows), (slope_q, slope_k))):
                sp.dma_start(slopes_q[l].rearrange("r h t -> (r h) t"), tq[:, 0:TB]).then_inc(table_out, 16)
                sp.dma_start(slopes_k[l].rearrange("r h t -> (r h) t"), tk).then_inc(table_out, 16)
            sp.dma_start(positions[0:1, :], pos_hi).then_inc(table_out, 16)
            sp.dma_start(positions[1:2, :], pos_lo).then_inc(table_out, 16)
            sp.wait_ge(table_out, 16 * 6)
            for par in range(2):
                for r in range(3):
                    for h in range(G):
                        sp.dma_start(k_stack[R_SLOPE + 2 * r:R_SLOPE + 2 * r + 2, par, h, :], positions).then_inc(fixed_in, 16)
                        sp.dma_start(q_stack[R_POS + 2 * r:R_POS + 2 * r + 2, par, :, h, :],
                                     positions.rearrange("a (b t) -> a b t", b=NB)).then_inc(fixed_in, 16)

            def load_mix(l):
                if l == 0:
                    sp.wait_ge(dom_in, 16)
                    for g in range(G0):
                        e = sp.value_load(dom[0:1, g:g + 1], min_val=0, max_val=E0 - 1)
                        gu = gate_up0[bass.ds(e, 1), :, :].rearrange("a (k p) o -> p (a k) o", p=P)
                        sp.dma_start(gate_w[:, :, I0 * g:I0 * g + I0], gu[:, :, 0:I0]).then_inc(wmix_in[0], 16)
                        sp.dma_start(up_w[:, :, I0 * g:I0 * g + I0], gu[:, :, I0:2 * I0]).then_inc(wmix_in[0], 16)
                        dn = down0[bass.ds(e, 1), :, :].rearrange("a i c -> (a i) c")
                        r0 = I0 * g
                        n = min(I0, P - r0 % P)
                        sp.dma_start(down_w[r0 % P:r0 % P + n, r0 // P, :], dn[0:n, :]).then_inc(wmix_in[0], 16)
                        if n < I0:
                            sp.dma_start(down_w[0:I0 - n, r0 // P + 1, :], dn[n:I0, :]).then_inc(wmix_in[0], 16)
                else:
                    for k in range(KD):
                        sp.dma_start(w1_s[:, k, :, :], w1[:, k * P:(k + 1) * P, :].rearrange("e p c -> p e c")).then_inc(wmix_in[1], 16)
                    sp.dma_start(sw1_s, sw1.rearrange("(k p) c -> p k c", p=P)).then_inc(wmix_in[1], 16)
                    sp.dma_start(w2_s[:, 0:E1, :], w2.rearrange("e p c -> p e c")).then_inc(wmix_in[1], 16)
                    sp.dma_start(w2_s[:, E1:M1, :], sw2.rearrange("(k p) c -> p k c", p=P)).then_inc(wmix_in[1], 16)

            def load_stack(l, par, group):
                hs = bass.ds(group * G, G)
                for r in range(3):
                    sq = slopes_q[l, r, hs, :].rearrange("(a b h) t -> a b (h t)", a=1, b=1).broadcast_to([2, NB, G * TB])
                    sp.dma_start(q_stack[R_SLOPE + 2 * r:R_SLOPE + 2 * r + 2, par, :, :, :].rearrange("a b h t -> a b (h t)"), sq)\
                        .then_inc(at_stack[l], 16)
                    sk = slopes_k[l, r, hs, :].rearrange("(a h) t -> a (h t)", a=1).broadcast_to([2, G * T])
                    sp.dma_start(k_stack[R_POS + 2 * r:R_POS + 2 * r + 2, par, :, :].rearrange("a h t -> a (h t)"), sk)\
                        .then_inc(at_stack[l], 16)
                for n in range(6):
                    rows = slice(R_QK + HD * n, R_QK + HD * n + HD)
                    qv = q_parts[Q_PARTS[n], bass.ds(group, 1)].rearrange("g b h d t -> d (g b h) t")
                    kv = k_parts[K_PARTS[n]].rearrange("(h d) t -> d h t", d=HD)
                    sp.dma_start(q_stack[rows, par, :, :, :].rearrange("d b h t -> d (b h) t"), qv).then_inc(at_stack[l], 16)
                    sp.dma_start(k_stack[rows, par, :, :], kv[:, hs, :]).then_inc(at_stack[l], 16)

            def store_max(l, n, b, par):
                sp.wait_ge(a_split[l], n + 3)
                for r in range(3):
                    dst = q_stack[R_MAX + r:R_MAX + r + 1, par, b, :, :].rearrange("a h c -> a (h c)")
                    sp.dma_start(dst, mrow[:, b % 2, r, :]).then_inc(a_row[l][b % 2], 16)

            def store_y(l, n, b, half, it):
                sp.wait_ge(at_yn[l], n + 1)
                sp.dma_start(yT[64 * half:64 * half + 64, bass.ds(it, 1), b * TB:(b + 1) * TB],
                             y_n[0:P:2, b % 2:b % 2 + 1, :]).then_inc(at_y[l][b % 2], 16)

            for l in range(2):
                for n in range(4 * NB):
                    b, which, m = n // 4, n % 4 // 2, n % 2
                    sp.wait_ge(pj_parts[l], n + 1)
                    if which:
                        sp.dma_start(k_parts[:, m * P:(m + 1) * P, b * TB:(b + 1) * TB].rearrange("r p t -> p r t"),
                                     qk_p[:, n % 4, :, :]).then_inc(pj_out[l][n % 4], 16)
                    else:
                        for g in range(2):
                            sp.dma_start(q_parts[:, 2 * m + g, b].rearrange("r h d t -> (h d) r t"),
                                         qk_p[64 * g:64 * g + 64, n % 4, :, :]).then_inc(pj_out[l][n % 4], 16)
                for n in range(4):
                    sp.wait_ge(pj_out[l][n], 16 * (2, 2, 1, 1)[n] * NB)
                load_stack(l, 0, 0)
                if l == 0:
                    load_mix(0)
                else:
                    sp.wait_ge(down_mm[0], NT // 2)
                    load_mix(1)
                for par in range(2):
                    sp.sem_inc(a_row[l][par], 48)
                    sp.sem_inc(at_y[l][par], 16)
                for off, k, (kind, what) in [(0, k, s) for k, s in enumerate(A_STEPS[:NHEAD])]:
                    if kind == "row":
                        store_max(l, what, what, 0)
                with sp.Fori(0, NG // 2) as it:
                    for half in range(2):
                        grp = it * 2 + half
                        load_stack(l, 1 - half, it * 2 + 1 if half == 0 else (1 - it) * 2)
                        for u, (b, j, w) in enumerate(UNITS):
                            for off, k, (kind, what) in SLOTS[u]:
                                if kind == "row":
                                    store_max(l, (grp + off) * NB + what, what, (half + off) % 2)
                            if b and j == 1:
                                store_y(l, grp * NB + b - 1, b - 1, half, it)
                        store_y(l, grp * NB + NB - 1, NB - 1, half, it)
                if l == 0:
                    sp.wait_ge(acc_mm[0], NT // 2)
                    load_attn(1)
            for b in range(NB):
                sp.wait_ge(x_add[1], ACC_ORDER.index(("down", 2 * b + 1)) + 1)
                sp.dma_start(out.rearrange("a (i p) c -> p (a i) c", p=P)[:, b * TPB:(b + 1) * TPB, :],
                             xs[:, b * TPB:(b + 1) * TPB, :]).then_inc(x_out, 16)
            sp.wait_ge(x_out, 16 * NB)

        @block.gpsimd
        def _(pool):
            pool.memset(ident[:, :], 0.0).then_inc(const_pool, 1)
            pool.memset(tri[:, :], 0.0).then_inc(const_pool, 1)
            pool.memset(zeros[:, :], 0.0).then_inc(const_pool, 1)
            pool.wait_ge(const_pool, 3)
            pool.affine_select(out=ident[:, :], in_=ident[:, :], compare_op=ALU.not_equal, fill=1.0, base=0,
                               pattern=[[-1, P]], channel_multiplier=1).then_inc(const_pool, 1)
            pool.affine_select(out=tri[:, :], in_=tri[:, :], compare_op=ALU.is_ge, fill=NEG, base=0,
                               pattern=[[-1, P]], channel_multiplier=1).then_inc(const_pool, 1)
            pool.iota(pos_hi.rearrange("p (a c) -> p a c", c=8), pattern=[[8, T // 8], [0, 8]], base=0,
                      channel_multiplier=0, allow_small_or_imprecise_dtypes=True).then_inc(const_pool, 1)
            pool.iota(pos_lo.rearrange("p (a c) -> p a c", c=8), pattern=[[0, T // 8], [1, 8]], base=0,
                      channel_multiplier=0, allow_small_or_imprecise_dtypes=True).then_inc(const_pool, 1)
            pool.iota(iota8[:, :, :], pattern=[[0, TPB], [1, E1]], base=0, channel_multiplier=0,
                      allow_small_or_imprecise_dtypes=True).then_inc(const_pool, 1)
            pool.memset(zero_rows, 0.0).then_inc(const_pool, 1)
            pool.memset(v_stage[:, :, :, :, :, :], 1.0).then_inc(const_pool, 1)
            pool.iota(iota_g, pattern=[[1, G0], [0, I0]], base=0, channel_multiplier=0,
                      allow_small_or_imprecise_dtypes=True).then_inc(const_pool, 1)
            pool.iota(iota_e, pattern=[[1, E1], [0, H1]], base=0, channel_multiplier=0,
                      allow_small_or_imprecise_dtypes=True).then_inc(const_pool, 1)
            pool.wait_ge(const_pool, 12)
            pool.tensor_copy(ident_bf[:, :], ident[:, :]).then_inc(const_pool, 1)
            pool.memset(o_n[:, :], 0.0).then_inc(const_pool, 1)

            def add_row(n, row, b, after, value):
                pool.wait_ge(after, value)
                xv = xs[:, b * TPB:(b + 1) * TPB, :]
                pool.tensor_tensor(xv, xv, brow[:, row:row + 1, :].broadcast_to([P, TPB, D]), ALU.add).then_inc(xb_done[n], 1)

            def stage_v(l, par, group_col, count):
                pool.tensor_copy(v_stage[:, par, :, :, :, 0],
                                 v_all[:, :, bass.ds(group_col, G * HD)].rearrange("p i (h d) -> p i h d", d=HD)).then_inc(at_vst[l], 1)

            def split_max(l, step, grp, b):
                pool.wait_ge(a_max[l], step + 1)
                pool.wait_ge(a_row[l][b % 2], 48 * (grp * 2 + b // 2 + 1))
                s = b % 2
                n = grp * NB + b
                base = n * 4
                pool.tensor_tensor(mrow[:, s, 0, :], mt[:, s, :], zeros[0:G * TPB, :], ALU.add).then_inc(a_cut[l], 1)
                pool.wait_ge(a_cut[l], base + 1)
                pool.tensor_tensor(mr[:, s, :], mt[:, s, :], mrow[:, s, 0, :], ALU.subtract).then_inc(a_cut[l], 1)
                pool.wait_ge(a_cut[l], base + 2)
                pool.tensor_tensor(mrow[:, s, 1, :], mr[:, s, :], zeros[0:G * TPB, :], ALU.add).then_inc(a_cut[l], 1)
                pool.wait_ge(a_cut[l], base + 3)
                pool.tensor_tensor(mr[:, s, :], mr[:, s, :], mrow[:, s, 1, :], ALU.subtract).then_inc(a_cut[l], 1)
                pool.wait_ge(a_cut[l], base + 4)
                pool.tensor_tensor(mrow[:, s, 2, :], mr[:, s, :], zeros[0:G * TPB, :], ALU.add).then_inc(a_split[l], 1)

            for l in range(2):
                if l == 0:
                    pool.wait_ge(small_in, 16 * SMALL)
                for b in range(NB):
                    add_row(l, 2 * l + 1, b, ln_xn[2 * l], TPB * (b + 1))
                pool.wait_ge(pj_v[l], NT)
                stage_v(l, 0, 0, 1)
                pool.sem_inc(a_split[l], 2)
                for n, (kind, what) in enumerate(A_STEPS[:NHEAD]):
                    if kind == "row":
                        split_max(l, n, 0, what)
                with pool.Fori(0, NG // 2) as it:
                    for half in range(2):
                        grp = it * 2 + half
                        for u, (b, j, w) in enumerate(UNITS):
                            if (b, j) == (1, 0):
                                pool.wait_ge(at_pv[l], grp * NU + 2)
                                pool.tensor_tensor(spare[:, half:half + 1], zeros[0:1, 0:1], zeros[0:1, 0:1], ALU.add)
                                stage_v(l, 1 - half, (it * 2 + 1 if half == 0 else (1 - it) * 2) * (G * HD), 0)
                            for off, k, (kind, what) in SLOTS[u]:
                                if kind == "row":
                                    split_max(l, grp * NA + NHEAD + k, grp + off, what)
                if l == 1:
                    for b in range(NB):
                        add_row(2, 4, b, ln_xn[3], TPB * (b + 1))

        @block.scalar
        def _(act):
            for l, (bq, bk, bv, bo) in enumerate(((bq0, bk0, bv0, bo0), (bq1, bk1, bv1, bo1))):
                for n, v in enumerate((bq, bk)):
                    act.dma_start(bcol[:, l, n, :], v).then_inc(small_in, 16)
                for n, v in enumerate((bv, bo)):
                    act.dma_start(brow[:, 2 * l + n, :], v.rearrange("(a c) -> a c", a=1).broadcast_to([P, D])).then_inc(small_in, 16)
            act.dma_start(brow[:, 4, :], sb2.rearrange("(a c) -> a c", a=1).broadcast_to([P, D])).then_inc(small_in, 16)
            act.dma_start(hb[:, 0:E1], b1).then_inc(small_in, 16)
            act.dma_start(hb[:, E1:M1], sb1).then_inc(small_in, 16)
            act.dma_start(b2_s[:, :], b2).then_inc(small_in, 16)
            act.dma_start(r0_s[:, :, :], router0.rearrange("(k p) e -> p k e", p=P)).then_inc(small_in, 16)
            act.dma_start(r1_s[:, :, :], router1.rearrange("(k p) e -> p k e", p=P)).then_inc(small_in, 16)
            for r in range(3):
                act.dma_start(merge_i[r * E0:(r + 1) * E0, :], merge0.rearrange("(e a) -> e a", a=1)).then_inc(small_in, 16)
            act.dma_start(erow[:, :], expert_of_row).then_inc(small_in, 16)
            act.dma_start(slope_c[:, :], slope_parts).then_inc(small_in, 16)
            act.dma_start(dom[:, :], dominant0.rearrange("(a g) -> a g", a=1)).then_inc(dom_in, 16)

            def ln_block(n, b):
                act.wait_ge(ln_var[n], b + 1)
                act.activation(lnt[:, 1, :], lnt[:, 0, :], ACT.Sqrt).then_inc(ln_root[n], 1)

            def ln_evac(n, b):
                for k in range(KD):
                    act.wait_ge(ln_tr[n], KD * b + k + 1)
                    act.activation(xT[:, k, b * TB:(b + 1) * TB], psum[:, TR_BANK, :], ACT.Copy).then_inc(ln_xT[n], 1)

            def project(l, b):
                for n in range(4):
                    which, m = n // 2, n % 2
                    item = 6 * b + n
                    count = 4 * b + n
                    bank = psum[:, HID_BANKS[item % 4], :]
                    bias = (bcol4 if which == 0 else bcol)[:, l, which, m:m + 1]
                    scale = 0.25 if which == 0 else 1.0
                    act.wait_ge(pj_mm[l], item + 1)
                    if count >= 2:
                        act.wait_ge(pj_dve[l], count - 1)
                    if count >= 4:
                        act.wait_ge(pj_out[l][n], 16 * (2, 2, 1, 1)[n] * b)
                    act.activation(qk_p[:, count % 4, 0, :], bank, ACT.Identity, bias=bias, scale=scale).then_inc(pj_act[l], 1)
                    act.activation(qk_f[:, count % 2, :], bank, ACT.Identity, bias=bias, scale=scale).then_inc(pj_act[l], 1)

            act.wait_ge(const_dve, CONST_DVE)
            for l in range(2):
                ln_block(2 * l, 0)
                ln_evac(2 * l, 0)
                for b in range(NB):
                    if b + 1 < NB:
                        ln_block(2 * l, b + 1)
                        ln_evac(2 * l, b + 1)
                    project(l, b)
                with act.Fori(0, NG // 2) as it:
                    for half in range(2):
                        grp = it * 2 + half
                        for u, (b, j, w) in enumerate(UNITS):
                            for hh in range(2):
                                act.wait_ge(at_score[l], grp * (2 * NU) + 2 * u + hh + 1)
                                if hh == 0:
                                    act.wait_ge(at_pv[l], grp * NU + u + 1)
                                act.activation(probs[:, (2 * u + hh) % 4, :, 0:w], psum[:, 2 * hh:2 * hh + 2, 0:w], ACT.Exp).then_inc(at_exp[l], 1)

                def hidden_rows(b):
                    if l == 0:
                        for m in range(M0):
                            n = M0 * b + m
                            act.wait_ge(hid_mm[0], n + 1)
                            if n >= 2:
                                act.wait_ge(hid_up[0], n - 1)
                            act.activation(act_out[:, n % 2, :], psum[:, HID_BANKS[2 * (n % 2)], :], ACT.Silu).then_inc(hid_act[0], 1)
                    else:
                        for m in range(M1):
                            n = M1 * b + m
                            act.wait_ge(hid_mm[1], n + 1)
                            bank = psum[:, HID_BANKS[n % 4], :]
                            if m < E1:
                                q = E1 * b + m
                                if q >= 2:
                                    act.wait_ge(hid_done[1], q - 1)
                                act.activation(act_out[:, q % 2, :], bank, ACT.Gelu, bias=hb[:, m:m + 1]).then_inc(hid_act[1], 1)
                            else:
                                act.activation(hidden[:, m, :], bank, ACT.Gelu, bias=hb[:, m:m + 1]).then_inc(hid_act[1], 1)

                def route(b):
                    if l == 0:
                        act.wait_ge(side_free[0], GATE_ITEMS[0] * b + 1)
                        act.activation(rt[:, 1, :, :], rt[:, 0, :, :], ACT.Exp).then_inc(r_exp[l], 1)
                    else:
                        act.wait_ge(r_soft[1], b + 1)
                        act.activation(rsmall[:, 1, :], rsmall[:, 0, :], ACT.Exp).then_inc(r_exp[l], 1)

                ln_block(2 * l + 1, 0)
                ln_evac(2 * l + 1, 0)
                route(0)
                for b in range(NB):
                    if b + 1 < NB:
                        ln_block(2 * l + 1, b + 1)
                    hidden_rows(b)
                    if b + 1 < NB:
                        ln_evac(2 * l + 1, b + 1)
                        route(b + 1)

        @block.tensor
        def _(pe):
            def transpose_rows(n, b):
                pe.wait_ge(ln_xn[n], TPB * (b + 1))
                for k in range(KD):
                    item = KD * b + k
                    if item:
                        pe.wait_ge(ln_xT[n], item)
                    for q in range(TPB):
                        last = pe.transpose(psum[:, TR_BANK, q * P:(q + 1) * P], xn[:, b % 2, q, k * P:(k + 1) * P], ident[:, :])
                    last.then_inc(ln_tr[n], 1)

            def bank_free(l, item):
                old = item - 4
                if old >= 0:
                    b, n = divmod(old, 6)
                    if n < 4:
                        pe.wait_ge(pj_act[l], 2 * (4 * b + n + 1))
                    else:
                        pe.wait_ge(pj_v[l], TPB * b + 2 * (n - 4) + 2)

            def project(l, b):
                if b == 0:
                    pe.wait_ge(wattn_in[l], 64)
                pe.wait_ge(ln_xT[2 * l], KD * (b + 1))
                for n in range(6):
                    item = 6 * b + n
                    bank_free(l, item)
                    bank = psum[:, HID_BANKS[item % 4], :]
                    if n < 4:
                        which, m = n // 2, n % 2
                        for k in range(KD):
                            last = pe.matmul(bank, w_attn[:, which, k, m * P:(m + 1) * P], xT[:, k, b * TB:(b + 1) * TB],
                                             start=(k == 0), stop=(k == KD - 1))
                    else:
                        for q in range(2):
                            i = TPB * b + 2 * (n - 4) + q
                            for k in range(KD):
                                last = pe.matmul(bank[:, q * D:(q + 1) * D], xT[:, k, i * P:(i + 1) * P], w_attn[:, 2, k, :],
                                                 start=(k == 0), stop=(k == KD - 1))
                    last.then_inc(pj_mm[l], 1)

            def a_step_mm(l, n, par, step, first):
                kind, what = step
                slot = psum[:, A_BANKS[first % 3], :]
                if n is not None:
                    pe.wait_ge(a_max[l], n)
                if kind == "row":
                    last = pe.transpose(slot[0:G * TPB, 0:P], nmax[:, :, :].rearrange("p h i -> p (h i)"), ident[:, :])
                    last.then_inc(a_mm[l], 1)
                    return
                i, h0, nh, s0, w = what
                for h in range(nh):
                    diag = s0 + w == (i + 1) * P
                    dst = slot[:, h * w:(h + 1) * w]
                    last = pe.matmul(dst, q_stack[0:KA, par, i // TPB, h0 + h, i % TPB * P:(i % TPB + 1) * P], k_stack[0:KA, par, h0 + h, s0:s0 + w],
                                     start=True, stop=not diag)
                    if diag:
                        last = pe.matmul(dst[:, w - P:w], ident_bf[:, :], tri[:, :], start=False, stop=True)
                last.then_inc(a_mm[l], 1)

            def scores(l, grp, par, u):
                b, j, w = UNITS[u]
                if j == 0:
                    pe.wait_ge(a_row[l][b % 2], 48 * (grp * 2 + b // 2 + 2))
                for hh in range(2):
                    if u:
                        pe.wait_ge(at_exp[l], grp * (2 * NU) + 2 * u + hh - 1)
                    for q in range(2):
                        h = 2 * hh + q
                        diag = j >= TPB * b
                        last = pe.matmul(psum[:, h, 0:w], k_stack[0:KB, par, h, j * P:(j + 1) * P], q_stack[0:KB, par, b, h, TB - w:TB],
                                         start=True, stop=not diag)
                        if diag:
                            last = pe.matmul(psum[:, h, 0:P], tri[:, :], ident_bf[:, :], start=False, stop=True)
                    last.then_inc(at_score[l], 1)

            def values(l, grp, par, u):
                b, j, w = UNITS[u]
                if j == 0:
                    pe.wait_ge(at_ofree[l], grp * NB + b + 1)
                    if b == 0:
                        pe.wait_ge(at_vst[l], grp + 1)
                pe.wait_ge(at_exp[l], grp * (2 * NU) + 2 * u + 2)
                for h in range(G):
                    last = pe.matmul(psum[32 * h:32 * h + 32, O_BANK, TB - w:TB], v_stage[:, par, j, h, :, :].rearrange("p d a -> p (d a)"),
                                     probs[:, (2 * u + h // 2) % 4, h % 2, 0:w], start=(j == 0), stop=(j == TPB * (b + 1) - 1),
                                     skip_group_check=True)
                last.then_inc(at_pv[l], 1)

            def out_pair(l, pair):
                n = ACC_ORDER.index(("out", pair))
                if n >= 2:
                    pe.wait_ge(x_add[l], n - 1)
                for q in range(2):
                    i = 2 * pair + q
                    for k in range(KD):
                        last = pe.matmul(psum[:, ACC_BANKS[n % 2], q * D:(q + 1) * D], yT[:, k, i * P:(i + 1) * P], w_attn[:, 3, k, :],
                                         start=(k == 0), stop=(k == KD - 1))
                last.then_inc(acc_mm[l], 1)


            def logits(l, b):
                pe.wait_ge(ln_xT[2 * l + 1], KD * (b + 1))
                if b:
                    pe.wait_ge(hid_done[l], (M0 if l == 0 else E1) * b)
                ne, w = (E0, r0_s) if l == 0 else (E1, r1_s)
                for q in range(TPB):
                    i = TPB * b + q
                    for k in range(KD):
                        last = pe.matmul(psum[:, SIDE_BANK, q * ne:(q + 1) * ne], xT[:, k, i * P:(i + 1) * P], w[:, k, :],
                                         start=(k == 0), stop=(k == KD - 1))
                last.then_inc(side_mm[l], 1)

            def gate_rows(l, b):
                ne = 3 * (E0 if l == 0 else E1)
                pe.wait_ge(r_gates[l], b + 1)
                pe.wait_ge(side_free[l], GATE_ITEMS[l] * b + 1)
                bank = psum[:, SIDE_BANK, :].bitcast(BF16)
                for q in range(TPB):
                    last = pe.transpose(bank[0:ne, q * P:(q + 1) * P], gparts[:, q, 0:ne], ident_bf[:, :])
                last.then_inc(side_mm[l], 1)
                if l == 1:
                    pe.wait_ge(side_free[l], GATE_ITEMS[l] * b + 2)
                    for q in range(TPB):
                        last = pe.transpose(psum[0:E1, SIDE_BANK, q * P:(q + 1) * P], rt[:, 5, q, 0:E1], ident[:, :])
                    last.then_inc(side_mm[l], 1)

            def spread(l, b, m):
                if m == 0:
                    pe.wait_ge(side_free[l], GATE_ITEMS[l] * (b + 1))
                else:
                    pe.wait_ge(hid_done[l], (M0 if l == 0 else E1) * b + m)
                lhs = spread0[:, m * P:(m + 1) * P] if l == 0 else spread1[:, m * P:(m + 1) * P]
                ne = 3 * (E0 if l == 0 else E1)
                pe.matmul(psum[:, SIDE_BANK, :], lhs, gT[0:ne, :], start=True, stop=True).then_inc(side_mm[l], 1)

            def hidden_mm(l, b, m):
                xb = lambda k: xT[:, k, b * TB:(b + 1) * TB]
                if l == 0:
                    n = M0 * b + m
                    if n >= 2:
                        pe.wait_ge(hid_act[0], n - 1)
                        pe.wait_ge(hid_up[0], n - 1)
                    for s, w in enumerate((gate_w, up_w)):
                        for k in range(KD):
                            last = pe.matmul(psum[:, HID_BANKS[2 * (n % 2) + s], :], w[:, k, m * P:(m + 1) * P], xb(k),
                                             start=(k == 0), stop=(k == KD - 1))
                else:
                    n = M1 * b + m
                    if n >= 4:
                        pe.wait_ge(hid_act[1], n - 3)
                    for k in range(KD):
                        w = w1_s[:, k, m, :] if m < E1 else sw1_s[:, k, (m - E1) * P:(m - E1 + 1) * P]
                        last = pe.matmul(psum[:, HID_BANKS[n % 4], :], w, xb(k), start=(k == 0), stop=(k == KD - 1))
                last.then_inc(hid_mm[l], 1)

            def down_pair(l, b, s):
                pair = 2 * b + s
                pe.wait_ge(x_add[l], ACC_ORDER.index(("down", pair)) - 1)
                mm = M0 if l == 0 else M1
                w = down_w if l == 0 else w2_s
                for q in range(2):
                    c0 = (2 * s + q) * P
                    dst = psum[:, ACC_BANKS[pair % 2], q * D:(q + 1) * D]
                    if l == 1:
                        pe.matmul(dst, gTf[:, c0:c0 + P], b2_s[:, :], start=True, stop=False)
                    for m in range(mm):
                        last = pe.matmul(dst, hidden[:, m, c0:c0 + P], w[:, m, :], start=(m == 0 and l == 0), stop=(m == mm - 1))
                last.then_inc(down_mm[l], 1)

            pe.wait_ge(const_pool, CONST_POOL)
            pe.wait_ge(const_dve, CONST_DVE)
            for l in range(2):
                transpose_rows(2 * l, 0)
                for b in range(NB):
                    if b + 1 < NB:
                        transpose_rows(2 * l, b + 1)
                    project(l, b)
                pe.wait_ge(pj_act[l], 8 * NB)
                pe.wait_ge(pj_v[l], NT)
                if l == 0:
                    pe.wait_ge(fixed_in, 16 * 48)
                per_load = 18 * 16
                pe.wait_ge(at_stack[l], per_load)
                pe.sem_inc(at_pv[l], 2)
                rows = 0
                for n, step in enumerate(A_STEPS[:NHEAD]):
                    if step[0] == "row":
                        rows += 1
                        pe.wait_ge(a_nm[l], rows)
                    a_step_mm(l, n - 2 if n >= 3 else None, 0, step, n)
                with pe.Fori(0, NG // 2) as it:
                    for half in range(2):
                        grp = it * 2 + half
                        scores(l, grp, half, 0)
                        for u in range(NU):
                            if u + 1 < NU:
                                scores(l, grp, half, u + 1)
                            for off, k, step in SLOTS[u]:
                                if step[0] == "row":
                                    pe.wait_ge(a_nm[l], (grp + off) * NB + step[1] + 1)
                                elif off == 1 and k == NA - NHEAD:
                                    pe.wait_ge(at_stack[l], (grp + 2) * per_load)
                                a_step_mm(l, grp * NA + (NHEAD + k - 2), (half + off) % 2, step, NHEAD + k)
                            values(l, grp, half, u)
                for par in range(2):
                    pe.wait_ge(at_y[l][par], 16 + 8 * NB * NG)
                pe.wait_ge(a_max[l], NHEAD + NA * NG)
                out_pair(l, 0)
                out_pair(l, 1)
                out_pair(l, 2)
                out_pair(l, 3)
                pe.wait_ge(wmix_in[l], 16 * (MIX_DMAS if l == 0 else 5))
                transpose_rows(2 * l + 1, 0)
                logits(l, 0)
                for b in range(NB):
                    mm = M0 if l == 0 else M1
                    me = M0 if l == 0 else E1
                    hidden_mm(l, b, 0)
                    hidden_mm(l, b, 1)
                    gate_rows(l, b)
                    for m in range(mm):
                        if m < me:
                            spread(l, b, m)
                        if m + 2 < mm:
                            hidden_mm(l, b, m + 2)
                    if b + 1 < NB:
                        if b + 2 < NB:
                            out_pair(l, 2 * b + 4)
                            out_pair(l, 2 * b + 5)
                        transpose_rows(2 * l + 1, b + 1)
                        logits(l, b + 1)
                    pe.wait_ge(hid_done[l], me * (b + 1))
                    if l == 1:
                        pe.wait_ge(hid_act[1], M1 * (b + 1))
                    down_pair(l, b, 0)
                    down_pair(l, b, 1)

        @block.vector
        def _(dve):
            V = nc.vector

            def layer_norm(n, b):
                if n == 0:
                    dve.wait_ge(x_in[b], 16)
                else:
                    kind, l = ("out", n // 2) if n % 2 else ("down", n // 2 - 1)
                    dve.wait_ge(x_add[l], ACC_ORDER.index((kind, 2 * b + 1)) + 1)
                for q in range(TPB):
                    V.bn_stats(stats[:, q, :], xs[:, b * TPB + q, :]).then_inc(ln_stat[n], 1)
                base = b * 13
                for q in range(TPB):
                    dve.wait_ge(ln_stat[n], base + q + 1)
                    V.bn_aggr(mv[:, q, :], stats[:, q, :]).then_inc(ln_stat[n], 1)
                dve.wait_ge(ln_stat[n], base + 8)
                V.tensor_scalar(lnt[:, 0, :], mv[:, :, 1], EPS, None, ALU.add).then_inc(ln_var[n], 1)
                dve.wait_ge(ln_root[n], b + 1)
                V.reciprocal(rstd[:, :], lnt[:, 1, :]).then_inc(ln_stat[n], 1)
                dve.wait_ge(ln_stat[n], base + 9)
                V.tensor_tensor(lnt[:, 2, :], rstd[:, :], rstd[:, :], ALU.mult).then_inc(ln_stat[n], 1)
                dve.wait_ge(ln_stat[n], base + 10)
                V.tensor_tensor(lnt[:, 3, :], lnt[:, 2, :], lnt[:, 0, :], ALU.mult).then_inc(ln_stat[n], 1)
                dve.wait_ge(ln_stat[n], base + 11)
                V.tensor_scalar(lnt[:, 2, :], lnt[:, 3, :], -0.5, 1.5, ALU.mult, ALU.add).then_inc(ln_stat[n], 1)
                dve.wait_ge(ln_stat[n], base + 12)
                V.tensor_tensor(lnt[:, 3, :], lnt[:, 2, :], rstd[:, :], ALU.mult).then_inc(ln_stat[n], 1)
                dve.wait_ge(ln_stat[n], base + 13)
                if b >= 2:
                    dve.wait_ge(ln_tr[n], KD * (b - 1))
                for q in range(TPB):
                    V.tensor_scalar(xn[:, b % 2, q, :], xs[:, b * TPB + q, :], mv[:, q, 0:1], lnt[:, 3, q:q + 1],
                                    ALU.subtract, ALU.mult).then_inc(ln_xn[n], 1)

            def project(l, b):
                for n in range(4):
                    count = 4 * b + n
                    s, r = count % 4, count % 2
                    dve.wait_ge(pj_act[l], 2 * count + 2)
                    V.tensor_tensor(qk_r[:, 0, :], qk_f[:, r, :], qk_p[:, s, 0, :], ALU.subtract).then_inc(pj_dve[l], 1)
                    dve.wait_ge(pj_dve[l], count + 1)
                    V.tensor_copy(qk_p[:, s, 1, :], qk_r[:, 0, :]).then_inc(pj_cut[l], 1)
                    dve.wait_ge(pj_cut[l], count + 1)
                    V.tensor_tensor(qk_p[:, s, 2, :], qk_r[:, 0, :], qk_p[:, s, 1, :], ALU.subtract).then_inc(pj_parts[l], 1)
                    dve.wait_ge(pj_parts[l], count + 1)
                for n in range(2):
                    item = 6 * b + 4 + n
                    dve.wait_ge(pj_mm[l], item + 1)
                    for q in range(2):
                        i = TPB * b + 2 * n + q
                        V.tensor_tensor(v_all[:, i, :], psum[:, HID_BANKS[item % 4], q * D:(q + 1) * D], brow[:, 2 * l, :],
                                        ALU.add).then_inc(pj_v[l], 1)

            def a_step_max(l, n, step, blk):
                kind, what = step
                first, count = n
                slot = psum[:, A_BANKS[first % 3], :]
                if kind == "max":
                    i, h0, nh, s0, w = what
                    dve.wait_ge(a_mm[l], count + 1)
                    V.tensor_reduce(mx[:, h0:h0 + nh, i, s0 // TB], slot[:, 0:nh * w].rearrange("p (h c) -> p h c", h=nh),
                                    AX.X, ALU.max).then_inc(a_max[l], 1)
                else:
                    dve.wait_ge(a_max[l], count)
                    V.tensor_reduce(nmax[:, :, :], mx[:, :, what * TPB:(what + 1) * TPB, :], AX.X, ALU.max,
                                    negate=True).then_inc(a_nm[l], 1)
                    dve.wait_ge(a_mm[l], count + 1)
                    dve.wait_ge(a_split[l], blk + 1)
                    V.tensor_copy(mt[:, what % 2, :], slot[0:G * TPB, 0:P]).then_inc(a_max[l], 1)

            def output(l, grp, b):
                n = grp * NB + b
                dve.wait_ge(at_pv[l], 2 + grp * NU + sum(1 for v in UNITS if v[0] <= b))
                V.transpose(o_t, psum[:, O_BANK, :]).then_inc(at_ofree[l], 1)
                dve.wait_ge(at_ofree[l], n + 2)
                ov = o_t.rearrange("p (k d a) -> p k d a", d=HD, a=2)
                nv = o_n[:, :].rearrange("p (k d a) -> p k d a", d=HD, a=2)
                V.reciprocal(o_r[:, :], ov[:, :, 0, 1]).then_inc(at_dve[l], 1)
                dve.wait_ge(at_dve[l], 2 * n + 1)
                V.tensor_tensor(nv[:, :, :, 0], ov[:, :, :, 0], o_r[:, :].rearrange("p (k a) -> p k a", a=1).broadcast_to([P, TB // 32, HD]),
                                ALU.mult).then_inc(at_dve[l], 1)
                dve.wait_ge(at_dve[l], 2 * n + 2)
                dve.wait_ge(at_y[l][b % 2], 16 * (grp * 2 + b // 2 + 1))
                V.transpose(y_n[:, b % 2, :], o_n[:, :]).then_inc(at_yn[l], 1)

            def add_acc(l, kind, pair):
                n = ACC_ORDER.index((kind, pair))
                if kind == "out":
                    dve.wait_ge(acc_mm[l], pair + 1)
                    dve.wait_ge(xb_done[l], NB)
                else:
                    dve.wait_ge(down_mm[l], pair + 1)
                    if l == 1:
                        dve.wait_ge(xb_done[2], pair // 2 + 1)
                xv = xs[:, 2 * pair:2 * pair + 2, :]
                V.tensor_tensor(xv, psum[:, ACC_BANKS[n % 2], :].rearrange("p (i c) -> p i c", i=2), xv, ALU.add).then_inc(x_add[l], 1)

            def bc(a, w):
                return a.rearrange("p (q a) -> p q a", a=1).broadcast_to([P, TPB, w])

            def step(l, ins):
                count[l] += 1
                ins.then_inc(r_dve[l], 1)
                dve.wait_ge(r_dve[l], count[l])

            count = [0, 0]

            def cut_gates(l, b, src, ne):
                rest = rt[:, 4, :, 0:ne]
                gp = lambda r: gparts[:, :, r * ne:(r + 1) * ne]
                step(l, V.tensor_copy(gp(0), src))
                step(l, V.tensor_tensor(rest, src, gp(0), ALU.subtract))
                step(l, V.tensor_copy(gp(1), rest))
                step(l, V.tensor_tensor(rest, rest, gp(1), ALU.subtract))
                V.tensor_copy(gp(2), rest).then_inc(r_gates[l], 1)

            def route0(b):
                lg = psum[:, SIDE_BANK, 0:TPB * E0].rearrange("p (q e) -> p q e", q=TPB)
                dve.wait_ge(side_mm[0], SIDE[0] * b + 1)
                step(0, V.tensor_reduce(rsmall[:, 0, :], lg, AX.X, ALU.max))
                V.tensor_tensor(rt[:, 0, :, :], lg, bc(rsmall[:, 0, :], E0), ALU.subtract).then_inc(side_free[0], 1)
                dve.wait_ge(r_exp[0], b + 1)
                for q in range(TPB):
                    V.max(rmax[:, q, :], rt[:, 1, q, :]).then_inc(r_dve[0], 1)
                count[0] += TPB
                dve.wait_ge(r_dve[0], count[0])
                for q in range(TPB):
                    V.match_replace(rt[:, 2, q, :], rmax[:, q, :], rt[:, 1, q, :], 0.0).then_inc(r_dve[0], 1)
                count[0] += TPB
                dve.wait_ge(r_dve[0], count[0])
                step(0, V.tensor_reduce(rsmall[:, 1, :], rmax[:, :, :], AX.X, ALU.add))
                step(0, V.reciprocal(rsmall[:, 2, :], rsmall[:, 1, :]))
                step(0, V.tensor_tensor(rt[:, 3, :, :], rt[:, 1, :, :], rt[:, 2, :, :], ALU.subtract))
                step(0, V.tensor_tensor(rt[:, 5, :, :], rt[:, 3, :, :], bc(rsmall[:, 2, :], E0), ALU.mult))
                if b:
                    dve.wait_ge(side_mm[0], SIDE[0] * (b - 1) + 2)
                cut_gates(0, b, rt[:, 5, :, :], E0)

            def route1(b):
                lg = rt[:, 0, :, 0:E1]
                dve.wait_ge(side_mm[1], SIDE[1] * b + 1)
                V.tensor_copy(lg, psum[:, SIDE_BANK, 0:TPB * E1].rearrange("p (q e) -> p q e", q=TPB)).then_inc(side_free[1], 1)
                dve.wait_ge(side_free[1], GATE_ITEMS[1] * b + 1)
                for q in range(TPB):
                    V.max(rmax[:, q, :], lg[:, q, :]).then_inc(r_dve[1], 1)
                count[1] += TPB
                dve.wait_ge(r_dve[1], count[1])
                V.tensor_tensor(rsmall[:, 0, :], rmax[:, :, 1], rmax[:, :, 0], ALU.subtract).then_inc(r_soft[1], 1)
                for q in range(TPB):
                    V.max_index(ridx[:, q, :], rmax[:, q, :], lg[:, q, :]).then_inc(r_dve[1], 1)
                count[1] += TPB
                dve.wait_ge(r_dve[1], count[1])
                step(1, V.tensor_copy(rsmall[:, 4, :], ridx[:, :, 0]))
                step(1, V.tensor_copy(rsmall[:, 5, :], ridx[:, :, 1]))
                dve.wait_ge(r_exp[1], b + 1)
                step(1, V.tensor_scalar(rsmall[:, 2, :], rsmall[:, 1, :], 1.0, None, ALU.add))
                step(1, V.reciprocal(rsmall[:, 3, :], rsmall[:, 2, :]))
                step(1, V.tensor_tensor(rsmall[:, 6, :], rsmall[:, 1, :], rsmall[:, 3, :], ALU.mult))
                first, second = rt[:, 1, :, 0:E1], rt[:, 2, :, 0:E1]
                step(1, V.tensor_tensor(first, iota8[:, :, :], bc(rsmall[:, 4, :], E1), ALU.is_equal))
                step(1, V.tensor_tensor(second, iota8[:, :, :], bc(rsmall[:, 5, :], E1), ALU.is_equal))
                step(1, V.tensor_tensor(first, first, bc(rsmall[:, 3, :], E1), ALU.mult))
                step(1, V.tensor_tensor(second, second, bc(rsmall[:, 6, :], E1), ALU.mult))
                if b:
                    dve.wait_ge(side_mm[1], SIDE[1] * (b - 1) + 3)
                step(1, V.tensor_tensor(rt[:, 5, :, 0:E1], first, second, ALU.add))
                cut_gates(1, b, rt[:, 5, :, 0:E1], E1)

            def mixture(l, b):
                me = M0 if l == 0 else E1
                ne = 3 * (E0 if l == 0 else E1)
                n0 = SIDE[l] * b + 1
                if b:
                    dve.wait_ge(side_mm[l], SIDE[l] * b)
                dve.wait_ge(side_mm[l], n0 + 1)
                V.tensor_copy(gT[0:ne, :], psum[:, SIDE_BANK, :].bitcast(BF16)[0:ne, 0:TB]).then_inc(side_free[l], 1)
                if l == 1:
                    dve.wait_ge(side_mm[1], n0 + 2)
                    V.tensor_copy(gTf, psum[0:E1, SIDE_BANK, :]).then_inc(side_free[1], 1)
                first = n0 + (1 if l == 0 else 2)
                for m in range(me):
                    q = me * b + m
                    if l == 0:
                        dve.wait_ge(hid_act[0], q + 1)
                        V.tensor_tensor(act_up[:, q % 2, :], psum[:, HID_BANKS[2 * (q % 2) + 1], :], act_out[:, q % 2, :],
                                        ALU.mult).then_inc(hid_up[0], 1)
                        dve.wait_ge(hid_up[0], q + 1)
                    else:
                        dve.wait_ge(hid_act[1], M1 * b + m + 1)
                    src = act_up if l == 0 else act_out
                    if m == 0 and b:
                        dve.wait_ge(down_mm[l], 2 * b)
                    dve.wait_ge(side_mm[l], first + m + 1)
                    V.tensor_tensor(hidden[:, m, :], psum[:, SIDE_BANK, :], src[:, q % 2, :], ALU.mult).then_inc(hid_done[l], 1)

            V.memset(k_stack[96:P, :, :, :], 1.0).then_inc(const_dve, 1)
            V.memset(mx[:, :, :, :], NEG).then_inc(const_dve, 1)
            dve.wait_ge(small_in, 16 * SMALL)
            V.tensor_scalar(bcol4[:, :, :, :], bcol[:, :, :, :], 0.25, None, ALU.mult).then_inc(const_dve, 1)
            V.tensor_copy(merge_f[:, :], merge_i[:, :]).then_inc(const_dve, 1)
            dve.wait_ge(const_pool, CONST_POOL)
            V.tensor_scalar(slope_q, zero_rows, slope_c[:, 0:1], None, ALU.add).then_inc(const_dve, 1)
            V.tensor_scalar(slope_k, zero_rows, slope_c[:, 0:1], None, ALU.subtract).then_inc(const_dve, 1)
            dve.wait_ge(const_dve, 6)
            V.tensor_scalar(spread1[:, :], iota_e.rearrange("p e c -> p (e c)"), erow[:, 0:1], None, ALU.is_equal).then_inc(const_dve, 1)
            V.tensor_scalar(spread0[:, :], iota_g.rearrange("p e c -> p (e c)"), merge_f[:, 0:1], None, ALU.is_equal).then_inc(const_dve, 1)

            for l in range(2):
                layer_norm(2 * l, 0)
                for b in range(NB):
                    if b + 1 < NB:
                        layer_norm(2 * l, b + 1)
                    project(l, b)
                dve.sem_inc(at_ofree[l], 1)
                for n, st in enumerate(A_STEPS[:NHEAD]):
                    a_step_max(l, (n, n), st, st[1] if st[0] == "row" else 0)
                with dve.Fori(0, NG // 2) as it:
                    for half in range(2):
                        grp = it * 2 + half
                        for u, (b, j, w) in enumerate(UNITS):
                            if b and j == 0:
                                output(l, grp, b - 1)
                            for off, k, st in SLOTS[u]:
                                a_step_max(l, (NHEAD + k, grp * NA + NHEAD + k), st,
                                           (grp + off) * NB + st[1] if st[0] == "row" else 0)
                        output(l, grp, NB - 1)
                route = (route0, route1)[l]
                add_acc(l, "out", 0)
                add_acc(l, "out", 1)
                layer_norm(2 * l + 1, 0)
                add_acc(l, "out", 2)
                add_acc(l, "out", 3)
                route(0)
                for b in range(NB):
                    if b + 1 < NB:
                        layer_norm(2 * l + 1, b + 1)
                    mixture(l, b)
                    if b + 1 < NB:
                        if b + 2 < NB:
                            add_acc(l, "out", 2 * b + 4)
                            add_acc(l, "out", 2 * b + 5)
                        route(b + 1)
                    add_acc(l, "down", 2 * b)
                    add_acc(l, "down", 2 * b + 1)


def slope_constants():
    import math

    import numpy as np

    start = 2 ** (-2 ** (-(math.log2(H) - 3)))
    s = np.array([start * start ** i for i in range(H)], np.float32)
    parts = []
    for _ in range(3):
        top = (s.view(np.uint32) & np.uint32(0xFFFF0000)).view(np.float32)
        parts.append(top)
        s = s - top
    return np.stack(parts, 0).reshape(3 * H, 1).copy()


def kernel(**inputs):
    import numpy as _np
    import concourse.bacc as _bacc
    from concourse import mybir as _mybir
    from concourse.bass_utils import run_bass_kernel_spmd as _run

    def a(name):
        return _np.asarray(inputs[name])

    def column(v):
        return v.reshape(-1, P).T

    def heads_in(w):
        return w.transpose(1, 0, 2).reshape(D, D)

    arrays = [
        ("x", a("L0_attn_x")),
        ("wq0", heads_in(a("L0_attn_Wq"))), ("bq0", column(a("L0_attn_bq"))),
        ("wk0", heads_in(a("L0_attn_Wk"))), ("bk0", column(a("L0_attn_bk"))),
        ("wv0", heads_in(a("L0_attn_Wv"))), ("bv0", a("L0_attn_bv").reshape(-1)),
        ("wo0", a("L0_attn_Wo")), ("bo0", a("L0_attn_bo")),
        ("router0", a("L0_ffn_gate_weight").T),
        ("gate_up0", a("L0_ffn_gate_up_proj").transpose(0, 2, 1)),
        ("down0", a("L0_ffn_down_proj").transpose(0, 2, 1)),
        ("merge0", a("L0_ffn_merge_groups")), ("dominant0", a("L0_ffn_dominant_experts")),
        ("wq1", a("L1_attn_Wq").T), ("bq1", column(a("L1_attn_bq"))),
        ("wk1", a("L1_attn_Wk").T), ("bk1", column(a("L1_attn_bk"))),
        ("wv1", a("L1_attn_Wv").T), ("bv1", a("L1_attn_bv")),
        ("wo1", a("L1_attn_Wo").T), ("bo1", a("L1_attn_bo")),
        ("router1", a("L1_ffn_gate_w")),
        ("w1", a("L1_ffn_w1")), ("b1", column(a("L1_ffn_b1"))), ("w2", a("L1_ffn_w2")), ("b2", a("L1_ffn_b2")),
        ("sw1", a("L1_ffn_shared_w1")), ("sb1", column(a("L1_ffn_shared_b1"))),
        ("sw2", a("L1_ffn_shared_w2")), ("sb2", a("L1_ffn_shared_b2")),
        ("slope_parts", slope_constants()),
        ("expert_of_row", (_np.arange(3 * E1) % E1).astype(_np.float32).reshape(-1, 1)),
    ]
    nc = _bacc.Bacc("TRN2", target_bir_lowering=False, num_devices=1)
    sent, args = {}, []
    for name, v in arrays:
        v = _np.ascontiguousarray(v)
        sent[name] = v
        args.append(nc.dram_tensor(name, v.shape, _mybir.dt.from_np(v.dtype), kind="ExternalInput").ap())
    args.append(nc.dram_tensor("out", (1, T, D), _mybir.dt.float32, kind="ExternalOutput").ap())
    two_layers(nc, *args)
    r = _run(nc, [sent], core_ids=[0])
    return r.results[0]["out"]
```

```python
from contextlib import ExitStack

import concourse.bass as bass
from concourse import mybir

F32 = mybir.dt.float32
BF16 = mybir.dt.bfloat16
I32 = mybir.dt.int32
U32 = mybir.dt.uint32
ALU = mybir.AluOpType
ACT = mybir.ActivationFunctionType
AX = mybir.AxisListType

P = 128
T = 2048
D = 256
KD = D // P
NT = T // P
TB = 512
NB = T // TB
TPB = TB // P
H = 16
HD = D // H
G = 4
NG = H // G
EPS = 1e-5
NEG = -3.0e38

R_SLOPE = 0
R_POS = 6
R_QK = 12
R_MAX = R_QK + 6 * HD
KA = R_MAX
KB = R_MAX + 3
Q_PARTS = (0, 0, 0, 1, 1, 2)
K_PARTS = (0, 1, 2, 0, 1, 0)

E0 = 32
G0 = 8
I0 = 96
M0 = G0 * I0 // P
E1 = 8
H1 = 128
M1 = E1 + 2
MMAX = max(M0, M1)

ACC_BANKS = (0, 1)
TR_BANK = 2
SIDE_BANK = 3
HID_BANKS = (4, 5, 6, 7)
O_BANK = 4
A_BANKS = (5, 6, 7)


def pass_a_items():
    blocks = []
    for b in range(NB):
        items = []
        for i in range(TPB * b, TPB * b + TPB):
            keys = (i + 1) * P
            for c in range(keys // TB):
                items += [(i, h, 1, c * TB, TB) for h in range(G)]
            w = keys % TB
            if w:
                n = min(G, TB // w)
                items += [(i, h, n, keys - w, w) for h in range(0, G, n)]
        blocks.append(items)
    return blocks


def pass_b_units():
    return [(b, j, TB - max(0, j - TPB * b) * P) for b in range(NB) for j in range(TPB * (b + 1))]


STACK_DMAS = 18
UNITS = pass_b_units()
NU = len(UNITS)
A_BLOCKS = pass_a_items()
A_STEPS = [s for b in range(NB) for s in [("max", it) for it in A_BLOCKS[b]] + [("row", b)]]
NA = len(A_STEPS)
assert NA % len(A_BANKS) == 0 and NU % 2 == 0


NSTEP = NG * NA
NBLK = NG * NB
ROWS_NS = 6500
OUT_NS = 2000


def schedule():
    order, step_end, exp_end, pv_end, rows_at = [], [], {}, [], []
    pe = dve = act = out_free = 0.0

    def step_ready(n):
        grp, kind = n // NA, A_STEPS[n % NA][0]
        if grp >= 2 and len(pv_end) < (grp - 1) * NU:
            return None
        if kind == "row":
            return step_end[n - 1] + 400
        return step_end[n - 3] + 100 if n >= 3 else 0.0

    segments = [("scores", 0, 0), ("scores", 0, 1)]
    for k in range(NG * NU):
        segments += [("scores", k + 1, 0), ("scores", k + 1, 1)] if k + 1 < NG * NU else []
        segments.append(("values", k))
    for seg in segments:
        k = seg[1]
        b, j, w = UNITS[k % NU]
        blk = k // NU * NB + b
        while True:
            if seg[0] == "scores":
                ready = exp_end[k - 1, seg[2]] if k else 0.0
                if j == 0:
                    ready = max(ready, rows_at[blk]) if len(rows_at) > blk else None
            else:
                ready = max(exp_end[k, 1], out_free if j == 0 else 0.0)
            n = len(step_end)
            a = step_ready(n) if n < NSTEP else None
            if a is not None and (a <= pe or ready is None or a < ready):
                kind, what = A_STEPS[n % NA]
                cols = what[2] * what[4] if kind == "max" else P
                pe = max(pe, a) + cols * 0.44
                dve = max(dve, pe + 150) + cols * 1.05 + (55 if kind == "max" else 300)
                step_end.append(dve)
                if kind == "row":
                    rows_at.append(dve + ROWS_NS)
                order.append(("step", n))
                continue
            break
        pe = max(pe, ready)
        if seg[0] == "scores":
            pe += 2 * w * 0.44
            act = max(act, pe + 150) + 2 * w * 0.83 + 80
            exp_end[k, seg[2]] = act + 100
        else:
            pe += 4 * w * 0.46
            pv_end.append(pe)
            if j == TPB * (b + 1) - 1:
                dve = max(dve, pe + 150) + OUT_NS
                out_free = dve - OUT_NS + 800
        order.append(seg)
    assert len(step_end) == NSTEP
    return order, pe


SCHEDULE, _ = schedule()


def side_order():
    order, waiting = [], None
    for event in SCHEDULE:
        if event[0] == "values":
            if waiting is not None:
                order.append(waiting)
                waiting = None
            k = event[1]
            b, j, _ = UNITS[k % NU]
            if j == TPB * (b + 1) - 1:
                waiting = ("output", k // NU * NB + b)
        elif event[0] == "step":
            order.append(event)
            if waiting is not None:
                order.append(waiting)
                waiting = None
    order.append(waiting)
    return order


SIDE_ORDER = side_order()


ACC_ORDER = [("out", p) for p in range(4)]
for _b in range(NB):
    ACC_ORDER += [("out", p) for p in (2 * _b + 4, 2 * _b + 5) if p < NT // 2]
    ACC_ORDER += [("down", 2 * _b), ("down", 2 * _b + 1)]


def two_layers(nc, x, wq0, bq0, wk0, bk0, wv0, bv0, wo0, bo0, router0, gate_up0, down0, merge0, dominant0,
               wq1, bq1, wk1, bk1, wv1, bv1, wo1, bo1, router1, w1, b1, w2, b2, sw1, sb1, sw2, sb2,
               slope_parts, expert_of_row, out):
    with ExitStack() as ctx:
        def sb(name, shape, dt=F32):
            return ctx.enter_context(nc.sbuf_tensor(name, shape, dt))

        def sem(name):
            return ctx.enter_context(nc.semaphore(name))

        def sems(name, n):
            return [sem(f"{name}{i}") for i in range(n)]

        psum = ctx.enter_context(nc.psum_tensor("psum", [P, 8, TB], F32))

        xs = sb("xs", [P, NT, D])
        xT = sb("xT", [P, KD, T])
        yT = xT
        q_stack = sb("q_stack", [P, 2, NB, G, TB], BF16)
        k_stack = sb("k_stack", [P, 2, G, T], BF16)
        v_stage = sb("v_stage", [P, 2, NT, G, HD, 2])
        work = sb("work", [P, 8192])
        v_all = work[:, 0:NT * D].rearrange("p (i c) -> p i c", i=NT)
        probs = work[:, 4096:8192].rearrange("p (s k c) -> p s k c", s=4, k=2)
        qk_f = work[:, 4096:5120].rearrange("p (s c) -> p s c", s=2)
        qk_p = work[:, 5120:8192].bitcast(BF16).rearrange("p (s r c) -> p s r c", s=4, r=3)
        hidden = work[:, 0:MMAX * TB].rearrange("p (m c) -> p m c", m=MMAX)
        act_out = work[:, 5120:5120 + 2 * TB].rearrange("p (s c) -> p s c", s=2)
        act_up = work[:, 6144:6144 + 2 * TB].rearrange("p (s c) -> p s c", s=2)
        w_attn = sb("w_attn", [P, 4, KD, D])
        w_mix = sb("w_mix", [P, 5120])
        gate_w = w_mix[:, 0:KD * G0 * I0].rearrange("p (k c) -> p k c", k=KD)
        up_w = w_mix[:, 1536:1536 + KD * G0 * I0].rearrange("p (k c) -> p k c", k=KD)
        down_w = w_mix[:, 3072:3072 + M0 * D].rearrange("p (m c) -> p m c", m=M0)
        w1_s = w_mix[:, 0:KD * E1 * H1].rearrange("p (k e c) -> p k e c", k=KD, e=E1)
        sw1_s = w_mix[:, 2048:2048 + KD * D].rearrange("p (k c) -> p k c", k=KD)
        w2_s = w_mix[:, 2560:2560 + M1 * D].rearrange("p (m c) -> p m c", m=M1)
        area = sb("area", [P, 2560])
        xn = area[:, 0:2 * TPB * D].rearrange("p (s q c) -> p s q c", s=2, q=TPB)
        y_n = area[:, 0:2 * TB].rearrange("p (s c) -> p s c", s=2)
        o_t = area[:, 1024:1024 + TB]
        mt = area[0:G * TPB, 1536:1536 + 2 * P].rearrange("p (s c) -> p s c", s=2)
        mr = area[0:G * TPB, 1792:1792 + 2 * P].rearrange("p (s c) -> p s c", s=2)
        mrow = area[0:G * TPB, 2048:2048 + 3 * P].bitcast(BF16).rearrange("p (s r c) -> p s r c", s=2, r=3)
        stats = sb("stats", [P, TPB, 6])
        mv = sb("mv", [P, TPB, 2])
        lnt = sb("lnt", [P, 4, TPB])
        rstd = sb("rstd", [P, TPB])
        ident = sb("ident", [P, P])
        ident_bf = sb("ident_bf", [P, P], BF16)
        tri = sb("tri", [P, P], BF16)
        zeros = sb("zeros", [G * TPB, P])
        bcol = sb("bcol", [P, 2, 2, KD])
        bcol4 = sb("bcol4", [P, 2, 2, KD])
        brow = sb("brow", [P, 5, D])
        hb = sb("hb", [P, M1])
        b2_s = sb("b2_s", [E1, D])
        r0_s = sb("r0_s", [P, KD, E0])
        r1_s = sb("r1_s", [P, KD, E1])
        dom = sb("dom", [1, G0], I32)
        merge_i = sb("merge_i", [3 * E0, 1], I32)
        merge_f = sb("merge_f", [3 * E0, 1])
        erow = sb("erow", [3 * E1, 1])
        slope_c = sb("slope_c", [3 * H, 1])
        spread0 = sb("spread0", [3 * E0, G0 * I0], BF16)
        spread1 = sb("spread1", [3 * E1, E1 * H1], BF16)
        iota8 = sb("iota8", [P, TPB, E1])
        qk_r = sb("qk_r", [P, 2, TB])
        mx = sb("mx", [P, G, NT, NB])
        nmax = sb("nmax", [P, G, TPB])
        o_r = sb("o_r", [P, TB // 32])
        o_n = sb("o_n", [P, TB])
        rt = sb("rt", [P, 6, TPB, E0])
        rmax = sb("rmax", [P, TPB, 8])
        ridx = sb("ridx", [P, TPB, 8], U32)
        rsmall = sb("rsmall", [P, 8, TPB])
        gparts = sb("gparts", [P, TPB, 3 * E0], BF16)
        gT = sb("gT", [3 * E0, TB], BF16)
        gTf = work[0:E1, 7168:7168 + TB]
        iota_g = work[0:3 * E0, 0:G0 * I0].rearrange("p (g c) -> p g c", g=G0)
        iota_e = work[0:3 * E1, 1024:1024 + E1 * H1].rearrange("p (e c) -> p e c", e=E1)
        slope_q = k_stack[0:3 * H, 0, 0, :]
        slope_k = k_stack[0:3 * H, 0, 1, :]
        zero_rows = k_stack[0:3 * H, 0, 2, :]
        pos_hi = k_stack[0:1, 1, 0, :]
        pos_lo = k_stack[0:1, 1, 1, :]

        q_parts = nc.dram_tensor("q_parts", [3, NG, NB, G, HD, TB], BF16, kind="Internal").ap()
        k_parts = nc.dram_tensor("k_parts", [3, D, T], BF16, kind="Internal").ap()
        slopes_q = nc.dram_tensor("slopes_q", [2, 3, H, TB], BF16, kind="Internal").ap()
        slopes_k = nc.dram_tensor("slopes_k", [2, 3, H, T], BF16, kind="Internal").ap()
        positions = nc.dram_tensor("positions", [2, T], BF16, kind="Internal").ap()

        x_in = sems("x_in", NB)
        wattn_in = sems("wattn_in", 2)
        wmix_in = sems("wmix_in", 2)
        small_in = sem("small_in")
        dom_in = sem("dom_in")
        const_pool = sem("const_pool")
        const_dve = sem("const_dve")
        table_out = sem("table_out")
        fixed_in = sem("fixed_in")
        ln_stat = sems("ln_stat", 4)
        ln_var = sems("ln_var", 4)
        ln_root = sems("ln_root", 4)
        ln_xn = sems("ln_xn", 4)
        ln_tr = sems("ln_tr", 4)
        ln_xT = sems("ln_xT", 4)
        pj_mm = sems("pj_mm", 2)
        pj_act = sems("pj_act", 2)
        pj_dve = sems("pj_dve", 2)
        pj_cut = sems("pj_cut", 2)
        pj_parts = sems("pj_parts", 2)
        pj_out = [sems(f"pj_out{l}_", 4) for l in range(2)]
        pj_v = sems("pj_v", 2)
        xb_done = sems("xb_done", 3)
        at_stack = sems("at_stack", 2)
        at_ones = sems("at_ones", 2)
        at_vst = sems("at_vst", 2)
        at_score = sems("at_score", 2)
        at_exp = sems("at_exp", 2)
        at_pv = sems("at_pv", 2)
        at_ofree = sems("at_ofree", 2)
        at_dve = sems("at_dve", 2)
        at_yn = sems("at_yn", 2)
        at_y = [sems(f"at_y{l}_", 2) for l in range(2)]
        a_mm = sems("a_mm", 2)
        a_max = sems("a_max", 2)
        a_nm = sems("a_nm", 2)
        a_cut = sems("a_cut", 2)
        a_split = sems("a_split", 2)
        a_row = [sems(f"a_row{l}_", 2) for l in range(2)]
        acc_mm = sems("acc_mm", 2)
        x_add = sems("x_add", 2)
        side_mm = sems("side_mm", 2)
        side_free = sems("side_free", 2)
        r_dve = sems("r_dve", 2)
        r_soft = sems("r_soft", 2)
        r_exp = sems("r_exp", 2)
        r_gates = sems("r_gates", 2)
        hid_mm = sems("hid_mm", 2)
        hid_act = sems("hid_act", 2)
        hid_up = sems("hid_up", 2)
        hid_done = sems("hid_done", 2)
        down_mm = sems("down_mm", 2)
        x_out = sem("x_out")

        SMALL = 19
        MIX_DMAS = 3 * G0 + sum(I0 * g % P + I0 > P for g in range(G0))
        CONST_POOL = 14
        CONST_DVE = 8
        A_W = ((wq0, wk0, wv0, wo0), (wq1, wk1, wv1, wo1))
        SIDE = (2 + M0, 3 + E1)
        GATE_ITEMS = (2, 3)

        block = ctx.enter_context(nc.Block())

        @block.sync
        def _(sp):
            xv = x.rearrange("a (i p) c -> p (a i) c", p=P)
            for b in range(NB):
                sp.dma_start(xs[:, b * TPB:(b + 1) * TPB, :], xv[:, b * TPB:(b + 1) * TPB, :]).then_inc(x_in[b], 16)

            def load_attn(l):
                for n, w in enumerate(A_W[l]):
                    sp.dma_start(w_attn[:, n, :, :], w.rearrange("(k p) c -> p k c", p=P)).then_inc(wattn_in[l], 16)

            load_attn(0)
            sp.wait_ge(const_dve, CONST_DVE)
            sp.wait_ge(const_pool, CONST_POOL)
            for l, (tq, tk) in enumerate(((zero_rows, zero_rows), (slope_q, slope_k))):
                sp.dma_start(slopes_q[l].rearrange("r h t -> (r h) t"), tq[:, 0:TB]).then_inc(table_out, 16)
                sp.dma_start(slopes_k[l].rearrange("r h t -> (r h) t"), tk).then_inc(table_out, 16)
            sp.dma_start(positions[0:1, :], pos_hi).then_inc(table_out, 16)
            sp.dma_start(positions[1:2, :], pos_lo).then_inc(table_out, 16)
            sp.wait_ge(table_out, 16 * 6)
            for par in range(2):
                for r in range(3):
                    for h in range(G):
                        sp.dma_start(k_stack[R_SLOPE + 2 * r:R_SLOPE + 2 * r + 2, par, h, :], positions).then_inc(fixed_in, 16)
                        sp.dma_start(q_stack[R_POS + 2 * r:R_POS + 2 * r + 2, par, :, h, :],
                                     positions.rearrange("a (b t) -> a b t", b=NB)).then_inc(fixed_in, 16)

            def load_mix(l):
                if l == 0:
                    sp.wait_ge(dom_in, 16)
                    for g in range(G0):
                        e = sp.value_load(dom[0:1, g:g + 1], min_val=0, max_val=E0 - 1)
                        gu = gate_up0[bass.ds(e, 1), :, :].rearrange("a (k p) o -> p (a k) o", p=P)
                        sp.dma_start(gate_w[:, :, I0 * g:I0 * g + I0], gu[:, :, 0:I0]).then_inc(wmix_in[0], 16)
                        sp.dma_start(up_w[:, :, I0 * g:I0 * g + I0], gu[:, :, I0:2 * I0]).then_inc(wmix_in[0], 16)
                        dn = down0[bass.ds(e, 1), :, :].rearrange("a i c -> (a i) c")
                        r0 = I0 * g
                        n = min(I0, P - r0 % P)
                        sp.dma_start(down_w[r0 % P:r0 % P + n, r0 // P, :], dn[0:n, :]).then_inc(wmix_in[0], 16)
                        if n < I0:
                            sp.dma_start(down_w[0:I0 - n, r0 // P + 1, :], dn[n:I0, :]).then_inc(wmix_in[0], 16)
                else:
                    for k in range(KD):
                        sp.dma_start(w1_s[:, k, :, :], w1[:, k * P:(k + 1) * P, :].rearrange("e p c -> p e c")).then_inc(wmix_in[1], 16)
                    sp.dma_start(sw1_s, sw1.rearrange("(k p) c -> p k c", p=P)).then_inc(wmix_in[1], 16)
                    sp.dma_start(w2_s[:, 0:E1, :], w2.rearrange("e p c -> p e c")).then_inc(wmix_in[1], 16)
                    sp.dma_start(w2_s[:, E1:M1, :], sw2.rearrange("(k p) c -> p k c", p=P)).then_inc(wmix_in[1], 16)

            def load_stack(l, group):
                hs = slice(group * G, (group + 1) * G)
                par = group % 2
                for r in range(3):
                    sq = slopes_q[l, r, hs, :].rearrange("(a b h) t -> a b (h t)", a=1, b=1).broadcast_to([2, NB, G * TB])
                    sp.dma_start(q_stack[R_SLOPE + 2 * r:R_SLOPE + 2 * r + 2, par, :, :, :].rearrange("a b h t -> a b (h t)"), sq)\
                        .then_inc(at_stack[l], 16)
                    sk = slopes_k[l, r, hs, :].rearrange("(a h) t -> a (h t)", a=1).broadcast_to([2, G * T])
                    sp.dma_start(k_stack[R_POS + 2 * r:R_POS + 2 * r + 2, par, :, :].rearrange("a h t -> a (h t)"), sk)\
                        .then_inc(at_stack[l], 16)
                for n in range(6):
                    rows = slice(R_QK + HD * n, R_QK + HD * n + HD)
                    qv = q_parts[Q_PARTS[n], group:group + 1].rearrange("g b h d t -> d (g b h) t")
                    kv = k_parts[K_PARTS[n]].rearrange("(h d) t -> d h t", d=HD)
                    sp.dma_start(q_stack[rows, par, :, :, :].rearrange("d b h t -> d (b h) t"), qv).then_inc(at_stack[l], 16)
                    sp.dma_start(k_stack[rows, par, :, :], kv[:, hs, :]).then_inc(at_stack[l], 16)

            def store_max(l, blk):
                grp, b = blk // NB, blk % NB
                sp.wait_ge(a_split[l], blk + 1)
                for r in range(3):
                    dst = q_stack[R_MAX + r:R_MAX + r + 1, grp % 2, b, :, :].rearrange("a h c -> a (h c)")
                    sp.dma_start(dst, mrow[:, b % 2, r, :]).then_inc(a_row[l][b % 2], 16)

            def store_y(l, blk):
                grp, b = blk // NB, blk % NB
                r0 = 64 * (grp % 2)
                sp.wait_ge(at_yn[l], blk + 1)
                sp.dma_start(yT[r0:r0 + 64, grp // 2, b * TB:(b + 1) * TB], y_n[0:P:2, b % 2, :]).then_inc(at_y[l][b % 2], 16)

            for l in range(2):
                for n in range(4 * NB):
                    b, which, m = n // 4, n % 4 // 2, n % 2
                    sp.wait_ge(pj_parts[l], n + 1)
                    if which:
                        sp.dma_start(k_parts[:, m * P:(m + 1) * P, b * TB:(b + 1) * TB].rearrange("r p t -> p r t"),
                                     qk_p[:, n % 4, :, :]).then_inc(pj_out[l][n % 4], 16)
                    else:
                        for g in range(2):
                            sp.dma_start(q_parts[:, 2 * m + g, b].rearrange("r h d t -> (h d) r t"),
                                         qk_p[64 * g:64 * g + 64, n % 4, :, :]).then_inc(pj_out[l][n % 4], 16)
                for n in range(4):
                    sp.wait_ge(pj_out[l][n], 16 * (2, 2, 1, 1)[n] * NB)
                load_stack(l, 0)
                for what, n in SIDE_ORDER:
                    if what == "output":
                        store_y(l, n)
                        if n % NB == NB - 1 and n // NB + 2 < NG:
                            load_stack(l, n // NB + 2)
                    elif A_STEPS[n % NA][0] == "row":
                        blk = n // NA * NB + A_STEPS[n % NA][1]
                        store_max(l, blk)
                        if blk == 0:
                            load_stack(l, 1)
                        elif blk == 2:
                            if l == 1:
                                sp.wait_ge(down_mm[0], NT // 2)
                            load_mix(l)
                if l == 0:
                    sp.wait_ge(acc_mm[0], NT // 2)
                    load_attn(1)
            for b in range(NB):
                sp.wait_ge(x_add[1], ACC_ORDER.index(("down", 2 * b + 1)) + 1)
                sp.dma_start(out.rearrange("a (i p) c -> p (a i) c", p=P)[:, b * TPB:(b + 1) * TPB, :],
                             xs[:, b * TPB:(b + 1) * TPB, :]).then_inc(x_out, 16)
            sp.wait_ge(x_out, 16 * NB)

        @block.gpsimd
        def _(pool):
            pool.memset(ident[:, :], 0.0).then_inc(const_pool, 1)
            pool.memset(tri[:, :], 0.0).then_inc(const_pool, 1)
            pool.memset(zeros[:, :], 0.0).then_inc(const_pool, 1)
            pool.wait_ge(const_pool, 3)
            pool.affine_select(out=ident[:, :], in_=ident[:, :], compare_op=ALU.not_equal, fill=1.0, base=0,
                               pattern=[[-1, P]], channel_multiplier=1).then_inc(const_pool, 1)
            pool.affine_select(out=tri[:, :], in_=tri[:, :], compare_op=ALU.is_ge, fill=NEG, base=0,
                               pattern=[[-1, P]], channel_multiplier=1).then_inc(const_pool, 1)
            pool.iota(pos_hi.rearrange("p (a c) -> p a c", c=8), pattern=[[8, T // 8], [0, 8]], base=0,
                      channel_multiplier=0, allow_small_or_imprecise_dtypes=True).then_inc(const_pool, 1)
            pool.iota(pos_lo.rearrange("p (a c) -> p a c", c=8), pattern=[[0, T // 8], [1, 8]], base=0,
                      channel_multiplier=0, allow_small_or_imprecise_dtypes=True).then_inc(const_pool, 1)
            pool.iota(iota8[:, :, :], pattern=[[0, TPB], [1, E1]], base=0, channel_multiplier=0,
                      allow_small_or_imprecise_dtypes=True).then_inc(const_pool, 1)
            pool.memset(zero_rows, 0.0).then_inc(const_pool, 1)
            pool.memset(v_stage[:, :, :, :, :, :], 1.0).then_inc(const_pool, 1)
            pool.iota(iota_g, pattern=[[1, G0], [0, I0]], base=0, channel_multiplier=0,
                      allow_small_or_imprecise_dtypes=True).then_inc(const_pool, 1)
            pool.iota(iota_e, pattern=[[1, E1], [0, H1]], base=0, channel_multiplier=0,
                      allow_small_or_imprecise_dtypes=True).then_inc(const_pool, 1)
            pool.wait_ge(const_pool, 12)
            pool.tensor_copy(ident_bf[:, :], ident[:, :]).then_inc(const_pool, 1)
            pool.memset(o_n[:, :], 0.0).then_inc(const_pool, 1)

            def add_row(n, row, b, after, value):
                pool.wait_ge(after, value)
                xv = xs[:, b * TPB:(b + 1) * TPB, :]
                pool.tensor_tensor(xv, xv, brow[:, row:row + 1, :].broadcast_to([P, TPB, D]), ALU.add).then_inc(xb_done[n], 1)

            def stage_v(l, grp):
                pool.tensor_copy(v_stage[:, grp % 2, :, :, :, 0],
                                 v_all[:, :, grp * G * HD:(grp + 1) * G * HD].rearrange("p i (h d) -> p i h d", d=HD)).then_inc(at_vst[l], 1)

            def split_max(l, n):
                b = A_STEPS[n % NA][1]
                blk = n // NA * NB + b
                s = b % 2
                base = 4 * blk
                pool.wait_ge(a_max[l], n + 1)
                if blk >= 2:
                    pool.wait_ge(a_row[l][s], 48 * (blk // 2))
                pool.tensor_tensor(mrow[:, s, 0, :], mt[:, s, :], zeros[0:G * TPB, :], ALU.add).then_inc(a_cut[l], 1)
                pool.wait_ge(a_cut[l], base + 1)
                pool.tensor_tensor(mr[:, s, :], mt[:, s, :], mrow[:, s, 0, :], ALU.subtract).then_inc(a_cut[l], 1)
                pool.wait_ge(a_cut[l], base + 2)
                pool.tensor_tensor(mrow[:, s, 1, :], mr[:, s, :], zeros[0:G * TPB, :], ALU.add).then_inc(a_cut[l], 1)
                pool.wait_ge(a_cut[l], base + 3)
                pool.tensor_tensor(mr[:, s, :], mr[:, s, :], mrow[:, s, 1, :], ALU.subtract).then_inc(a_cut[l], 1)
                pool.wait_ge(a_cut[l], base + 4)
                pool.tensor_tensor(mrow[:, s, 2, :], mr[:, s, :], zeros[0:G * TPB, :], ALU.add).then_inc(a_split[l], 1)

            for l in range(2):
                if l == 0:
                    pool.wait_ge(small_in, 16 * SMALL)
                for b in range(NB):
                    add_row(l, 2 * l + 1, b, ln_xn[2 * l], TPB * (b + 1))
                pool.wait_ge(pj_v[l], NT)
                stage_v(l, 0)
                stage_v(l, 1)
                for what, n in SIDE_ORDER:
                    if what == "output":
                        grp = n // NB + 2
                        if n % NB == NB - 1 and grp < NG:
                            pool.wait_ge(at_pv[l], (grp - 1) * NU)
                            stage_v(l, grp)
                    elif A_STEPS[n % NA][0] == "row":
                        split_max(l, n)
                if l == 1:
                    for b in range(NB):
                        add_row(2, 4, b, ln_xn[3], TPB * (b + 1))

        @block.scalar
        def _(act):
            for l, (bq, bk, bv, bo) in enumerate(((bq0, bk0, bv0, bo0), (bq1, bk1, bv1, bo1))):
                for n, v in enumerate((bq, bk)):
                    act.dma_start(bcol[:, l, n, :], v).then_inc(small_in, 16)
                for n, v in enumerate((bv, bo)):
                    act.dma_start(brow[:, 2 * l + n, :], v.rearrange("(a c) -> a c", a=1).broadcast_to([P, D])).then_inc(small_in, 16)
            act.dma_start(brow[:, 4, :], sb2.rearrange("(a c) -> a c", a=1).broadcast_to([P, D])).then_inc(small_in, 16)
            act.dma_start(hb[:, 0:E1], b1).then_inc(small_in, 16)
            act.dma_start(hb[:, E1:M1], sb1).then_inc(small_in, 16)
            act.dma_start(b2_s[:, :], b2).then_inc(small_in, 16)
            act.dma_start(r0_s[:, :, :], router0.rearrange("(k p) e -> p k e", p=P)).then_inc(small_in, 16)
            act.dma_start(r1_s[:, :, :], router1.rearrange("(k p) e -> p k e", p=P)).then_inc(small_in, 16)
            for r in range(3):
                act.dma_start(merge_i[r * E0:(r + 1) * E0, :], merge0.rearrange("(e a) -> e a", a=1)).then_inc(small_in, 16)
            act.dma_start(erow[:, :], expert_of_row).then_inc(small_in, 16)
            act.dma_start(slope_c[:, :], slope_parts).then_inc(small_in, 16)
            act.dma_start(dom[:, :], dominant0.rearrange("(a g) -> a g", a=1)).then_inc(dom_in, 16)

            def ln_block(n, b):
                act.wait_ge(ln_var[n], b + 1)
                act.activation(lnt[:, 1, :], lnt[:, 0, :], ACT.Sqrt).then_inc(ln_root[n], 1)

            def ln_evac(n, b):
                for k in range(KD):
                    act.wait_ge(ln_tr[n], KD * b + k + 1)
                    act.activation(xT[:, k, b * TB:(b + 1) * TB], psum[:, TR_BANK, :], ACT.Copy).then_inc(ln_xT[n], 1)

            def project(l, b):
                for n in range(4):
                    which, m = n // 2, n % 2
                    item = 6 * b + n
                    count = 4 * b + n
                    bank = psum[:, HID_BANKS[item % 4], :]
                    bias = (bcol4 if which == 0 else bcol)[:, l, which, m:m + 1]
                    scale = 0.25 if which == 0 else 1.0
                    act.wait_ge(pj_mm[l], item + 1)
                    if count >= 2:
                        act.wait_ge(pj_dve[l], count - 1)
                    if count >= 4:
                        act.wait_ge(pj_out[l][n], 16 * (2, 2, 1, 1)[n] * b)
                    act.activation(qk_p[:, count % 4, 0, :], bank, ACT.Identity, bias=bias, scale=scale).then_inc(pj_act[l], 1)
                    act.activation(qk_f[:, count % 2, :], bank, ACT.Identity, bias=bias, scale=scale).then_inc(pj_act[l], 1)

            act.wait_ge(const_dve, CONST_DVE)
            for l in range(2):
                ln_block(2 * l, 0)
                ln_evac(2 * l, 0)
                for b in range(NB):
                    if b + 1 < NB:
                        ln_block(2 * l, b + 1)
                        ln_evac(2 * l, b + 1)
                    project(l, b)
                for k in range(NG * NU):
                    w = UNITS[k % NU][2]
                    for hh in range(2):
                        act.wait_ge(at_score[l], 2 * k + hh + 1)
                        if hh == 0 and k >= 2:
                            act.wait_ge(at_pv[l], k - 1)
                        act.activation(probs[:, (2 * k + hh) % 4, :, 0:w], psum[:, 2 * hh:2 * hh + 2, 0:w], ACT.Exp).then_inc(at_exp[l], 1)

                def hidden_rows(b):
                    if l == 0:
                        for m in range(M0):
                            n = M0 * b + m
                            act.wait_ge(hid_mm[0], n + 1)
                            if n >= 2:
                                act.wait_ge(hid_up[0], n - 1)
                            act.activation(act_out[:, n % 2, :], psum[:, HID_BANKS[2 * (n % 2)], :], ACT.Silu).then_inc(hid_act[0], 1)
                    else:
                        for m in range(M1):
                            n = M1 * b + m
                            act.wait_ge(hid_mm[1], n + 1)
                            bank = psum[:, HID_BANKS[n % 4], :]
                            if m < E1:
                                q = E1 * b + m
                                if q >= 2:
                                    act.wait_ge(hid_done[1], q - 1)
                                act.activation(act_out[:, q % 2, :], bank, ACT.Gelu, bias=hb[:, m:m + 1]).then_inc(hid_act[1], 1)
                            else:
                                act.activation(hidden[:, m, :], bank, ACT.Gelu, bias=hb[:, m:m + 1]).then_inc(hid_act[1], 1)

                def route(b):
                    if l == 0:
                        act.wait_ge(side_free[0], GATE_ITEMS[0] * b + 1)
                        act.activation(rt[:, 1, :, :], rt[:, 0, :, :], ACT.Exp).then_inc(r_exp[l], 1)
                    else:
                        act.wait_ge(r_soft[1], b + 1)
                        act.activation(rsmall[:, 1, :], rsmall[:, 0, :], ACT.Exp).then_inc(r_exp[l], 1)

                ln_block(2 * l + 1, 0)
                ln_evac(2 * l + 1, 0)
                route(0)
                for b in range(NB):
                    if b + 1 < NB:
                        ln_block(2 * l + 1, b + 1)
                    hidden_rows(b)
                    if b + 1 < NB:
                        ln_evac(2 * l + 1, b + 1)
                        route(b + 1)

        @block.tensor
        def _(pe):
            def transpose_rows(n, b):
                pe.wait_ge(ln_xn[n], TPB * (b + 1))
                for k in range(KD):
                    item = KD * b + k
                    if item:
                        pe.wait_ge(ln_xT[n], item)
                    for q in range(TPB):
                        last = pe.transpose(psum[:, TR_BANK, q * P:(q + 1) * P], xn[:, b % 2, q, k * P:(k + 1) * P], ident[:, :])
                    last.then_inc(ln_tr[n], 1)

            def bank_free(l, item):
                old = item - 4
                if old >= 0:
                    b, n = divmod(old, 6)
                    if n < 4:
                        pe.wait_ge(pj_act[l], 2 * (4 * b + n + 1))
                    else:
                        pe.wait_ge(pj_v[l], TPB * b + 2 * (n - 4) + 2)

            def project(l, b):
                if b == 0:
                    pe.wait_ge(wattn_in[l], 64)
                pe.wait_ge(ln_xT[2 * l], KD * (b + 1))
                for n in range(6):
                    item = 6 * b + n
                    bank_free(l, item)
                    bank = psum[:, HID_BANKS[item % 4], :]
                    if n < 4:
                        which, m = n // 2, n % 2
                        for k in range(KD):
                            last = pe.matmul(bank, w_attn[:, which, k, m * P:(m + 1) * P], xT[:, k, b * TB:(b + 1) * TB],
                                             start=(k == 0), stop=(k == KD - 1))
                    else:
                        for q in range(2):
                            i = TPB * b + 2 * (n - 4) + q
                            for k in range(KD):
                                last = pe.matmul(bank[:, q * D:(q + 1) * D], xT[:, k, i * P:(i + 1) * P], w_attn[:, 2, k, :],
                                                 start=(k == 0), stop=(k == KD - 1))
                    last.then_inc(pj_mm[l], 1)

            def step_mm(l, n):
                grp, (kind, what) = n // NA, A_STEPS[n % NA]
                slot = psum[:, A_BANKS[n % 3], :]
                par = grp % 2
                if n >= 3:
                    pe.wait_ge(a_max[l], n - 2)
                if kind == "row":
                    pe.wait_ge(a_nm[l], grp * NB + what + 1)
                    last = pe.transpose(slot[0:G * TPB, 0:P], nmax[:, :, :].rearrange("p h i -> p (h i)"), ident[:, :])
                    last.then_inc(a_mm[l], 1)
                    return
                if n % NA == 0:
                    pe.wait_ge(at_stack[l], (grp + 1) * STACK_DMAS * 16)
                i, h0, nh, s0, w = what
                for h in range(nh):
                    diag = s0 + w == (i + 1) * P
                    dst = slot[:, h * w:(h + 1) * w]
                    last = pe.matmul(dst, q_stack[0:KA, par, i // TPB, h0 + h, i % TPB * P:(i % TPB + 1) * P], k_stack[0:KA, par, h0 + h, s0:s0 + w],
                                     start=True, stop=not diag)
                    if diag:
                        last = pe.matmul(dst[:, w - P:w], ident_bf[:, :], tri[:, :], start=False, stop=True)
                last.then_inc(a_mm[l], 1)

            def scores(l, k, hh):
                grp, (b, j, w) = k // NU, UNITS[k % NU]
                if j == 0 and hh == 0:
                    pe.wait_ge(a_row[l][b % 2], 48 * (grp * 2 + b // 2 + 1))
                if k:
                    pe.wait_ge(at_exp[l], 2 * (k - 1) + hh + 1)
                for h in (2 * hh, 2 * hh + 1):
                    diag = j >= TPB * b
                    last = pe.matmul(psum[:, h, 0:w], k_stack[0:KB, grp % 2, h, j * P:(j + 1) * P], q_stack[0:KB, grp % 2, b, h, TB - w:TB],
                                     start=True, stop=not diag)
                    if diag:
                        last = pe.matmul(psum[:, h, 0:P], tri[:, :], ident_bf[:, :], start=False, stop=True)
                last.then_inc(at_score[l], 1)

            def values(l, k):
                grp, (b, j, w) = k // NU, UNITS[k % NU]
                blk = grp * NB + b
                if j == 0:
                    if blk:
                        pe.wait_ge(at_ofree[l], blk)
                    if b == 0:
                        pe.wait_ge(at_vst[l], grp + 1)
                pe.wait_ge(at_exp[l], 2 * k + 2)
                for h in range(G):
                    last = pe.matmul(psum[32 * h:32 * h + 32, O_BANK, TB - w:TB], v_stage[:, grp % 2, j, h, :, :].rearrange("p d a -> p (d a)"),
                                     probs[:, (2 * k + h // 2) % 4, h % 2, 0:w], start=(j == 0), stop=(j == TPB * (b + 1) - 1),
                                     skip_group_check=True)
                last.then_inc(at_pv[l], 1)

            def out_pair(l, pair):
                n = ACC_ORDER.index(("out", pair))
                if n >= 2:
                    pe.wait_ge(x_add[l], n - 1)
                for q in range(2):
                    i = 2 * pair + q
                    for k in range(KD):
                        last = pe.matmul(psum[:, ACC_BANKS[n % 2], q * D:(q + 1) * D], yT[:, k, i * P:(i + 1) * P], w_attn[:, 3, k, :],
                                         start=(k == 0), stop=(k == KD - 1))
                last.then_inc(acc_mm[l], 1)


            def logits(l, b):
                pe.wait_ge(ln_xT[2 * l + 1], KD * (b + 1))
                if b:
                    pe.wait_ge(hid_done[l], (M0 if l == 0 else E1) * b)
                ne, w = (E0, r0_s) if l == 0 else (E1, r1_s)
                for q in range(TPB):
                    i = TPB * b + q
                    for k in range(KD):
                        last = pe.matmul(psum[:, SIDE_BANK, q * ne:(q + 1) * ne], xT[:, k, i * P:(i + 1) * P], w[:, k, :],
                                         start=(k == 0), stop=(k == KD - 1))
                last.then_inc(side_mm[l], 1)

            def gate_rows(l, b):
                ne = 3 * (E0 if l == 0 else E1)
                pe.wait_ge(r_gates[l], b + 1)
                pe.wait_ge(side_free[l], GATE_ITEMS[l] * b + 1)
                bank = psum[:, SIDE_BANK, :].bitcast(BF16)
                for q in range(TPB):
                    last = pe.transpose(bank[0:ne, q * P:(q + 1) * P], gparts[:, q, 0:ne], ident_bf[:, :])
                last.then_inc(side_mm[l], 1)
                if l == 1:
                    pe.wait_ge(side_free[l], GATE_ITEMS[l] * b + 2)
                    for q in range(TPB):
                        last = pe.transpose(psum[0:E1, SIDE_BANK, q * P:(q + 1) * P], rt[:, 5, q, 0:E1], ident[:, :])
                    last.then_inc(side_mm[l], 1)

            def spread(l, b, m):
                if m == 0:
                    pe.wait_ge(side_free[l], GATE_ITEMS[l] * (b + 1))
                else:
                    pe.wait_ge(hid_done[l], (M0 if l == 0 else E1) * b + m)
                lhs = spread0[:, m * P:(m + 1) * P] if l == 0 else spread1[:, m * P:(m + 1) * P]
                ne = 3 * (E0 if l == 0 else E1)
                pe.matmul(psum[:, SIDE_BANK, :], lhs, gT[0:ne, :], start=True, stop=True).then_inc(side_mm[l], 1)

            def hidden_mm(l, b, m):
                xb = lambda k: xT[:, k, b * TB:(b + 1) * TB]
                if l == 0:
                    n = M0 * b + m
                    if n >= 2:
                        pe.wait_ge(hid_act[0], n - 1)
                        pe.wait_ge(hid_up[0], n - 1)
                    for s, w in enumerate((gate_w, up_w)):
                        for k in range(KD):
                            last = pe.matmul(psum[:, HID_BANKS[2 * (n % 2) + s], :], w[:, k, m * P:(m + 1) * P], xb(k),
                                             start=(k == 0), stop=(k == KD - 1))
                else:
                    n = M1 * b + m
                    if n >= 4:
                        pe.wait_ge(hid_act[1], n - 3)
                    for k in range(KD):
                        w = w1_s[:, k, m, :] if m < E1 else sw1_s[:, k, (m - E1) * P:(m - E1 + 1) * P]
                        last = pe.matmul(psum[:, HID_BANKS[n % 4], :], w, xb(k), start=(k == 0), stop=(k == KD - 1))
                last.then_inc(hid_mm[l], 1)

            def down_pair(l, b, s):
                pair = 2 * b + s
                pe.wait_ge(x_add[l], ACC_ORDER.index(("down", pair)) - 1)
                mm = M0 if l == 0 else M1
                w = down_w if l == 0 else w2_s
                for q in range(2):
                    c0 = (2 * s + q) * P
                    dst = psum[:, ACC_BANKS[pair % 2], q * D:(q + 1) * D]
                    if l == 1:
                        pe.matmul(dst, gTf[:, c0:c0 + P], b2_s[:, :], start=True, stop=False)
                    for m in range(mm):
                        last = pe.matmul(dst, hidden[:, m, c0:c0 + P], w[:, m, :], start=(m == 0 and l == 0), stop=(m == mm - 1))
                last.then_inc(down_mm[l], 1)

            pe.wait_ge(const_pool, CONST_POOL)
            pe.wait_ge(const_dve, CONST_DVE)
            for l in range(2):
                transpose_rows(2 * l, 0)
                for b in range(NB):
                    if b + 1 < NB:
                        transpose_rows(2 * l, b + 1)
                    project(l, b)
                pe.wait_ge(pj_act[l], 8 * NB)
                pe.wait_ge(pj_v[l], NT)
                if l == 0:
                    pe.wait_ge(fixed_in, 16 * 48)
                for event in SCHEDULE:
                    if event[0] == "step":
                        step_mm(l, event[1])
                    elif event[0] == "scores":
                        scores(l, event[1], event[2])
                    else:
                        values(l, event[1])
                for par in range(2):
                    pe.wait_ge(at_y[l][par], 16 * NBLK // 2)
                pe.wait_ge(a_max[l], NSTEP)
                out_pair(l, 0)
                out_pair(l, 1)
                out_pair(l, 2)
                out_pair(l, 3)
                pe.wait_ge(wmix_in[l], 16 * (MIX_DMAS if l == 0 else 5))
                transpose_rows(2 * l + 1, 0)
                logits(l, 0)
                for b in range(NB):
                    mm = M0 if l == 0 else M1
                    me = M0 if l == 0 else E1
                    hidden_mm(l, b, 0)
                    hidden_mm(l, b, 1)
                    gate_rows(l, b)
                    for m in range(mm):
                        if m < me:
                            spread(l, b, m)
                        if m + 2 < mm:
                            hidden_mm(l, b, m + 2)
                    if b + 1 < NB:
                        if b + 2 < NB:
                            out_pair(l, 2 * b + 4)
                            out_pair(l, 2 * b + 5)
                        transpose_rows(2 * l + 1, b + 1)
                        logits(l, b + 1)
                    pe.wait_ge(hid_done[l], me * (b + 1))
                    if l == 1:
                        pe.wait_ge(hid_act[1], M1 * (b + 1))
                    down_pair(l, b, 0)
                    down_pair(l, b, 1)

        @block.vector
        def _(dve):
            V = nc.vector

            def layer_norm(n, b):
                if n == 0:
                    dve.wait_ge(x_in[b], 16)
                else:
                    kind, l = ("out", n // 2) if n % 2 else ("down", n // 2 - 1)
                    dve.wait_ge(x_add[l], ACC_ORDER.index((kind, 2 * b + 1)) + 1)
                for q in range(TPB):
                    V.bn_stats(stats[:, q, :], xs[:, b * TPB + q, :]).then_inc(ln_stat[n], 1)
                base = b * 13
                for q in range(TPB):
                    dve.wait_ge(ln_stat[n], base + q + 1)
                    V.bn_aggr(mv[:, q, :], stats[:, q, :]).then_inc(ln_stat[n], 1)
                dve.wait_ge(ln_stat[n], base + 8)
                V.tensor_scalar(lnt[:, 0, :], mv[:, :, 1], EPS, None, ALU.add).then_inc(ln_var[n], 1)
                dve.wait_ge(ln_root[n], b + 1)
                V.reciprocal(rstd[:, :], lnt[:, 1, :]).then_inc(ln_stat[n], 1)
                dve.wait_ge(ln_stat[n], base + 9)
                V.tensor_tensor(lnt[:, 2, :], rstd[:, :], rstd[:, :], ALU.mult).then_inc(ln_stat[n], 1)
                dve.wait_ge(ln_stat[n], base + 10)
                V.tensor_tensor(lnt[:, 3, :], lnt[:, 2, :], lnt[:, 0, :], ALU.mult).then_inc(ln_stat[n], 1)
                dve.wait_ge(ln_stat[n], base + 11)
                V.tensor_scalar(lnt[:, 2, :], lnt[:, 3, :], -0.5, 1.5, ALU.mult, ALU.add).then_inc(ln_stat[n], 1)
                dve.wait_ge(ln_stat[n], base + 12)
                V.tensor_tensor(lnt[:, 3, :], lnt[:, 2, :], rstd[:, :], ALU.mult).then_inc(ln_stat[n], 1)
                dve.wait_ge(ln_stat[n], base + 13)
                if b >= 2:
                    dve.wait_ge(ln_tr[n], KD * (b - 1))
                for q in range(TPB):
                    V.tensor_scalar(xn[:, b % 2, q, :], xs[:, b * TPB + q, :], mv[:, q, 0:1], lnt[:, 3, q:q + 1],
                                    ALU.subtract, ALU.mult).then_inc(ln_xn[n], 1)

            def project(l, b):
                for n in range(4):
                    count = 4 * b + n
                    s, r = count % 4, count % 2
                    dve.wait_ge(pj_act[l], 2 * count + 2)
                    V.tensor_tensor(qk_r[:, 0, :], qk_f[:, r, :], qk_p[:, s, 0, :], ALU.subtract).then_inc(pj_dve[l], 1)
                    dve.wait_ge(pj_dve[l], count + 1)
                    V.tensor_copy(qk_p[:, s, 1, :], qk_r[:, 0, :]).then_inc(pj_cut[l], 1)
                    dve.wait_ge(pj_cut[l], count + 1)
                    V.tensor_tensor(qk_p[:, s, 2, :], qk_r[:, 0, :], qk_p[:, s, 1, :], ALU.subtract).then_inc(pj_parts[l], 1)
                    dve.wait_ge(pj_parts[l], count + 1)
                for n in range(2):
                    item = 6 * b + 4 + n
                    dve.wait_ge(pj_mm[l], item + 1)
                    for q in range(2):
                        i = TPB * b + 2 * n + q
                        V.tensor_tensor(v_all[:, i, :], psum[:, HID_BANKS[item % 4], q * D:(q + 1) * D], brow[:, 2 * l, :],
                                        ALU.add).then_inc(pj_v[l], 1)

            def step_max(l, n):
                kind, what = A_STEPS[n % NA]
                slot = psum[:, A_BANKS[n % 3], :]
                if kind == "max":
                    i, h0, nh, s0, w = what
                    dve.wait_ge(a_mm[l], n + 1)
                    V.tensor_reduce(mx[:, h0:h0 + nh, i, s0 // TB], slot[:, 0:nh * w].rearrange("p (h c) -> p h c", h=nh),
                                    AX.X, ALU.max).then_inc(a_max[l], 1)
                else:
                    blk = n // NA * NB + what
                    dve.wait_ge(a_max[l], n)
                    V.tensor_reduce(nmax[:, :, :], mx[:, :, what * TPB:(what + 1) * TPB, :], AX.X, ALU.max,
                                    negate=True).then_inc(a_nm[l], 1)
                    dve.wait_ge(a_mm[l], n + 1)
                    if blk >= 2:
                        dve.wait_ge(a_split[l], blk - 1)
                    V.tensor_copy(mt[:, what % 2, :], slot[0:G * TPB, 0:P]).then_inc(a_max[l], 1)

            def output(l, blk):
                grp, b = blk // NB, blk % NB
                dve.wait_ge(at_pv[l], grp * NU + sum(1 for v in UNITS if v[0] <= b))
                V.transpose(o_t, psum[:, O_BANK, :]).then_inc(at_ofree[l], 1)
                dve.wait_ge(at_ofree[l], blk + 1)
                ov = o_t.rearrange("p (k d a) -> p k d a", d=HD, a=2)
                nv = o_n[:, :].rearrange("p (k d a) -> p k d a", d=HD, a=2)
                V.reciprocal(o_r[:, :], ov[:, :, 0, 1]).then_inc(at_dve[l], 1)
                dve.wait_ge(at_dve[l], 2 * blk + 1)
                V.tensor_tensor(nv[:, :, :, 0], ov[:, :, :, 0], o_r[:, :].rearrange("p (k a) -> p k a", a=1).broadcast_to([P, TB // 32, HD]),
                                ALU.mult).then_inc(at_dve[l], 1)
                dve.wait_ge(at_dve[l], 2 * blk + 2)
                if blk >= 2:
                    dve.wait_ge(at_y[l][b % 2], 16 * (blk // 2))
                V.transpose(y_n[:, b % 2, :], o_n[:, :]).then_inc(at_yn[l], 1)

            def add_acc(l, kind, pair):
                n = ACC_ORDER.index((kind, pair))
                if kind == "out":
                    dve.wait_ge(acc_mm[l], pair + 1)
                    dve.wait_ge(xb_done[l], NB)
                else:
                    dve.wait_ge(down_mm[l], pair + 1)
                    if l == 1:
                        dve.wait_ge(xb_done[2], pair // 2 + 1)
                xv = xs[:, 2 * pair:2 * pair + 2, :]
                V.tensor_tensor(xv, psum[:, ACC_BANKS[n % 2], :].rearrange("p (i c) -> p i c", i=2), xv, ALU.add).then_inc(x_add[l], 1)

            def bc(a, w):
                return a.rearrange("p (q a) -> p q a", a=1).broadcast_to([P, TPB, w])

            def step(l, ins):
                count[l] += 1
                ins.then_inc(r_dve[l], 1)
                dve.wait_ge(r_dve[l], count[l])

            count = [0, 0]

            def cut_gates(l, b, src, ne):
                rest = rt[:, 4, :, 0:ne]
                gp = lambda r: gparts[:, :, r * ne:(r + 1) * ne]
                step(l, V.tensor_copy(gp(0), src))
                step(l, V.tensor_tensor(rest, src, gp(0), ALU.subtract))
                step(l, V.tensor_copy(gp(1), rest))
                step(l, V.tensor_tensor(rest, rest, gp(1), ALU.subtract))
                V.tensor_copy(gp(2), rest).then_inc(r_gates[l], 1)

            def route0(b):
                lg = psum[:, SIDE_BANK, 0:TPB * E0].rearrange("p (q e) -> p q e", q=TPB)
                dve.wait_ge(side_mm[0], SIDE[0] * b + 1)
                step(0, V.tensor_reduce(rsmall[:, 0, :], lg, AX.X, ALU.max))
                V.tensor_tensor(rt[:, 0, :, :], lg, bc(rsmall[:, 0, :], E0), ALU.subtract).then_inc(side_free[0], 1)
                dve.wait_ge(r_exp[0], b + 1)
                for q in range(TPB):
                    V.max(rmax[:, q, :], rt[:, 1, q, :]).then_inc(r_dve[0], 1)
                count[0] += TPB
                dve.wait_ge(r_dve[0], count[0])
                for q in range(TPB):
                    V.match_replace(rt[:, 2, q, :], rmax[:, q, :], rt[:, 1, q, :], 0.0).then_inc(r_dve[0], 1)
                count[0] += TPB
                dve.wait_ge(r_dve[0], count[0])
                step(0, V.tensor_reduce(rsmall[:, 1, :], rmax[:, :, :], AX.X, ALU.add))
                step(0, V.reciprocal(rsmall[:, 2, :], rsmall[:, 1, :]))
                step(0, V.tensor_tensor(rt[:, 3, :, :], rt[:, 1, :, :], rt[:, 2, :, :], ALU.subtract))
                step(0, V.tensor_tensor(rt[:, 5, :, :], rt[:, 3, :, :], bc(rsmall[:, 2, :], E0), ALU.mult))
                if b:
                    dve.wait_ge(side_mm[0], SIDE[0] * (b - 1) + 2)
                cut_gates(0, b, rt[:, 5, :, :], E0)

            def route1(b):
                lg = rt[:, 0, :, 0:E1]
                dve.wait_ge(side_mm[1], SIDE[1] * b + 1)
                V.tensor_copy(lg, psum[:, SIDE_BANK, 0:TPB * E1].rearrange("p (q e) -> p q e", q=TPB)).then_inc(side_free[1], 1)
                dve.wait_ge(side_free[1], GATE_ITEMS[1] * b + 1)
                for q in range(TPB):
                    V.max(rmax[:, q, :], lg[:, q, :]).then_inc(r_dve[1], 1)
                count[1] += TPB
                dve.wait_ge(r_dve[1], count[1])
                V.tensor_tensor(rsmall[:, 0, :], rmax[:, :, 1], rmax[:, :, 0], ALU.subtract).then_inc(r_soft[1], 1)
                for q in range(TPB):
                    V.max_index(ridx[:, q, :], rmax[:, q, :], lg[:, q, :]).then_inc(r_dve[1], 1)
                count[1] += TPB
                dve.wait_ge(r_dve[1], count[1])
                step(1, V.tensor_copy(rsmall[:, 4, :], ridx[:, :, 0]))
                step(1, V.tensor_copy(rsmall[:, 5, :], ridx[:, :, 1]))
                dve.wait_ge(r_exp[1], b + 1)
                step(1, V.tensor_scalar(rsmall[:, 2, :], rsmall[:, 1, :], 1.0, None, ALU.add))
                step(1, V.reciprocal(rsmall[:, 3, :], rsmall[:, 2, :]))
                step(1, V.tensor_tensor(rsmall[:, 6, :], rsmall[:, 1, :], rsmall[:, 3, :], ALU.mult))
                first, second = rt[:, 1, :, 0:E1], rt[:, 2, :, 0:E1]
                step(1, V.tensor_tensor(first, iota8[:, :, :], bc(rsmall[:, 4, :], E1), ALU.is_equal))
                step(1, V.tensor_tensor(second, iota8[:, :, :], bc(rsmall[:, 5, :], E1), ALU.is_equal))
                step(1, V.tensor_tensor(first, first, bc(rsmall[:, 3, :], E1), ALU.mult))
                step(1, V.tensor_tensor(second, second, bc(rsmall[:, 6, :], E1), ALU.mult))
                if b:
                    dve.wait_ge(side_mm[1], SIDE[1] * (b - 1) + 3)
                step(1, V.tensor_tensor(rt[:, 5, :, 0:E1], first, second, ALU.add))
                cut_gates(1, b, rt[:, 5, :, 0:E1], E1)

            def mixture(l, b):
                me = M0 if l == 0 else E1
                ne = 3 * (E0 if l == 0 else E1)
                n0 = SIDE[l] * b + 1
                if b:
                    dve.wait_ge(side_mm[l], SIDE[l] * b)
                dve.wait_ge(side_mm[l], n0 + 1)
                V.tensor_copy(gT[0:ne, :], psum[:, SIDE_BANK, :].bitcast(BF16)[0:ne, 0:TB]).then_inc(side_free[l], 1)
                if l == 1:
                    dve.wait_ge(side_mm[1], n0 + 2)
                    V.tensor_copy(gTf, psum[0:E1, SIDE_BANK, :]).then_inc(side_free[1], 1)
                first = n0 + (1 if l == 0 else 2)
                for m in range(me):
                    q = me * b + m
                    if l == 0:
                        dve.wait_ge(hid_act[0], q + 1)
                        V.tensor_tensor(act_up[:, q % 2, :], psum[:, HID_BANKS[2 * (q % 2) + 1], :], act_out[:, q % 2, :],
                                        ALU.mult).then_inc(hid_up[0], 1)
                        dve.wait_ge(hid_up[0], q + 1)
                    else:
                        dve.wait_ge(hid_act[1], M1 * b + m + 1)
                    src = act_up if l == 0 else act_out
                    if m == 0 and b:
                        dve.wait_ge(down_mm[l], 2 * b)
                    dve.wait_ge(side_mm[l], first + m + 1)
                    V.tensor_tensor(hidden[:, m, :], psum[:, SIDE_BANK, :], src[:, q % 2, :], ALU.mult).then_inc(hid_done[l], 1)

            V.memset(k_stack[96:P, :, :, :], 1.0).then_inc(const_dve, 1)
            V.memset(mx[:, :, :, :], NEG).then_inc(const_dve, 1)
            dve.wait_ge(small_in, 16 * SMALL)
            V.tensor_scalar(bcol4[:, :, :, :], bcol[:, :, :, :], 0.25, None, ALU.mult).then_inc(const_dve, 1)
            V.tensor_copy(merge_f[:, :], merge_i[:, :]).then_inc(const_dve, 1)
            dve.wait_ge(const_pool, CONST_POOL)
            V.tensor_scalar(slope_q, zero_rows, slope_c[:, 0:1], None, ALU.add).then_inc(const_dve, 1)
            V.tensor_scalar(slope_k, zero_rows, slope_c[:, 0:1], None, ALU.subtract).then_inc(const_dve, 1)
            dve.wait_ge(const_dve, 6)
            V.tensor_scalar(spread1[:, :], iota_e.rearrange("p e c -> p (e c)"), erow[:, 0:1], None, ALU.is_equal).then_inc(const_dve, 1)
            V.tensor_scalar(spread0[:, :], iota_g.rearrange("p e c -> p (e c)"), merge_f[:, 0:1], None, ALU.is_equal).then_inc(const_dve, 1)

            for l in range(2):
                layer_norm(2 * l, 0)
                for b in range(NB):
                    if b + 1 < NB:
                        layer_norm(2 * l, b + 1)
                    project(l, b)
                for what, n in SIDE_ORDER:
                    if what == "step":
                        step_max(l, n)
                    else:
                        output(l, n)
                route = (route0, route1)[l]
                add_acc(l, "out", 0)
                add_acc(l, "out", 1)
                layer_norm(2 * l + 1, 0)
                add_acc(l, "out", 2)
                add_acc(l, "out", 3)
                route(0)
                for b in range(NB):
                    if b + 1 < NB:
                        layer_norm(2 * l + 1, b + 1)
                    mixture(l, b)
                    if b + 1 < NB:
                        if b + 2 < NB:
                            add_acc(l, "out", 2 * b + 4)
                            add_acc(l, "out", 2 * b + 5)
                        route(b + 1)
                    add_acc(l, "down", 2 * b)
                    add_acc(l, "down", 2 * b + 1)


def slope_constants():
    import math

    import numpy as np

    start = 2 ** (-2 ** (-(math.log2(H) - 3)))
    s = np.array([start * start ** i for i in range(H)], np.float32)
    parts = []
    for _ in range(3):
        top = (s.view(np.uint32) & np.uint32(0xFFFF0000)).view(np.float32)
        parts.append(top)
        s = s - top
    return np.stack(parts, 0).reshape(3 * H, 1).copy()


def kernel(**inputs):
    import numpy as _np
    import concourse.bacc as _bacc
    from concourse import mybir as _mybir
    from concourse.bass_utils import run_bass_kernel_spmd as _run

    def a(name):
        return _np.asarray(inputs[name])

    def column(v):
        return v.reshape(-1, P).T

    def heads_in(w):
        return w.transpose(1, 0, 2).reshape(D, D)

    arrays = [
        ("x", a("L0_attn_x")),
        ("wq0", heads_in(a("L0_attn_Wq"))), ("bq0", column(a("L0_attn_bq"))),
        ("wk0", heads_in(a("L0_attn_Wk"))), ("bk0", column(a("L0_attn_bk"))),
        ("wv0", heads_in(a("L0_attn_Wv"))), ("bv0", a("L0_attn_bv").reshape(-1)),
        ("wo0", a("L0_attn_Wo")), ("bo0", a("L0_attn_bo")),
        ("router0", a("L0_ffn_gate_weight").T),
        ("gate_up0", a("L0_ffn_gate_up_proj").transpose(0, 2, 1)),
        ("down0", a("L0_ffn_down_proj").transpose(0, 2, 1)),
        ("merge0", a("L0_ffn_merge_groups")), ("dominant0", a("L0_ffn_dominant_experts")),
        ("wq1", a("L1_attn_Wq").T), ("bq1", column(a("L1_attn_bq"))),
        ("wk1", a("L1_attn_Wk").T), ("bk1", column(a("L1_attn_bk"))),
        ("wv1", a("L1_attn_Wv").T), ("bv1", a("L1_attn_bv")),
        ("wo1", a("L1_attn_Wo").T), ("bo1", a("L1_attn_bo")),
        ("router1", a("L1_ffn_gate_w")),
        ("w1", a("L1_ffn_w1")), ("b1", column(a("L1_ffn_b1"))), ("w2", a("L1_ffn_w2")), ("b2", a("L1_ffn_b2")),
        ("sw1", a("L1_ffn_shared_w1")), ("sb1", column(a("L1_ffn_shared_b1"))),
        ("sw2", a("L1_ffn_shared_w2")), ("sb2", a("L1_ffn_shared_b2")),
        ("slope_parts", slope_constants()),
        ("expert_of_row", (_np.arange(3 * E1) % E1).astype(_np.float32).reshape(-1, 1)),
    ]
    nc = _bacc.Bacc("TRN2", target_bir_lowering=False, num_devices=1)
    sent, args = {}, []
    for name, v in arrays:
        v = _np.ascontiguousarray(v)
        sent[name] = v
        args.append(nc.dram_tensor(name, v.shape, _mybir.dt.from_np(v.dtype), kind="ExternalInput").ap())
    args.append(nc.dram_tensor("out", (1, T, D), _mybir.dt.float32, kind="ExternalOutput").ap())
    two_layers(nc, *args)
    r = _run(nc, [sent], core_ids=[0])
    return r.results[0]["out"]
```

```python
from contextlib import ExitStack

import concourse.bass as bass
from concourse import mybir

F32 = mybir.dt.float32
BF16 = mybir.dt.bfloat16
I32 = mybir.dt.int32
U32 = mybir.dt.uint32
ALU = mybir.AluOpType
ACT = mybir.ActivationFunctionType
AX = mybir.AxisListType

P = 128
T = 2048
D = 256
KD = D // P
NT = T // P
TB = 512
NB = T // TB
TPB = TB // P
H = 16
HD = D // H
G = 4
NG = H // G
EPS = 1e-5
NEG = -3.0e38
ONES_PAIR = 1.0019378662109375

R_SLOPE = 0
R_POS = 6
R_QK = 12
R_MAX = R_QK + 6 * HD
KA = R_MAX
KB = R_MAX + 3
Q_PARTS = (0, 0, 0, 1, 1, 2)
K_PARTS = (0, 1, 2, 0, 1, 0)

E0 = 32
G0 = 8
I0 = 96
M0 = G0 * I0 // P
E1 = 8
H1 = 128
M1 = E1 + 2
MMAX = max(M0, M1)

ACC_BANKS = (5, 6)
TR_BANK = 7
SIDE_BANK = 0
HID_BANKS = (1, 2, 3, 4)
O_BANK = 4
A_BANKS = (5, 6, 7)


def pass_a_items():
    blocks = []
    for b in range(NB):
        items = []
        for i in range(TPB * b, TPB * b + TPB):
            keys = (i + 1) * P
            for c in range(keys // TB):
                items += [(i, h, 1, c * TB, TB) for h in range(G)]
            w = keys % TB
            if w:
                n = min(G, TB // w)
                items += [(i, h, n, keys - w, w) for h in range(0, G, n)]
        blocks.append(items)
    return blocks


def pass_b_units():
    return [(b, j, TB - max(0, j - TPB * b) * P) for b in range(NB) for j in range(TPB * (b + 1))]


STACK_DMAS = 18
REST_DMAS = 12
UNITS = pass_b_units()
NU = len(UNITS)
A_BLOCKS = pass_a_items()
A_STEPS = [s for b in range(NB) for s in [("max", it) for it in A_BLOCKS[b]] + [("row", b)]]
NA = len(A_STEPS)
assert NA % len(A_BANKS) == 0 and NU % 2 == 0


EARLY = len(A_BLOCKS[0])
assert EARLY <= 12


def early_steps(n):
    return range(3 * (n - 3), min(3 * (n - 3) + 3, EARLY)) if 3 <= n <= 6 else ()


NSTEP = NG * NA
NBLK = NG * NB
ROWS_NS = 8500
OUT_NS = 2000


def schedule():
    order, step_end, exp_end, pv_end, rows_at = [], [], {}, [], []
    pe = dve = act = out_free = 0.0

    def step_ready(n):
        grp, kind = n // NA, A_STEPS[n % NA][0]
        if grp >= 2 and len(pv_end) < (grp - 1) * NU:
            return None
        if kind == "row":
            return step_end[n - 1] + 400
        return step_end[n - 3] if n >= 3 else 0.0

    segments = [("scores", 0, 0), ("scores", 0, 1)]
    for k in range(NG * NU):
        segments += [("scores", k + 1, 0), ("scores", k + 1, 1)] if k + 1 < NG * NU else []
        segments.append(("values", k))
    for seg in segments:
        k = seg[1]
        b, j, w = UNITS[k % NU]
        blk = k // NU * NB + b
        while True:
            if seg[0] == "scores":
                ready = exp_end[k - 1, seg[2]] if k else 0.0
                if j == 0:
                    ready = max(ready, rows_at[blk]) if len(rows_at) > blk else None
            else:
                ready = max(exp_end[k, 1], out_free if j == 0 else 0.0)
            n = len(step_end)
            a = step_ready(n) if n < NSTEP else None
            if a is not None and (a <= pe or ready is None or a < ready):
                kind, what = A_STEPS[n % NA]
                cols = 0 if n < EARLY else what[2] * what[4] if kind == "max" else P
                pe = max(pe, a) + cols * 0.44
                dve = max(dve, pe + 150) + cols * 1.05 + (55 if kind == "max" else 300)
                step_end.append(dve)
                if kind == "row":
                    rows_at.append(dve + ROWS_NS)
                order.append(("step", n))
                continue
            break
        pe = max(pe, ready)
        if seg[0] == "scores":
            pe += 2 * w * 0.44
            act = max(act, pe + 150) + 2 * w * 0.83 + 80
            exp_end[k, seg[2]] = act + 100
        else:
            pe += 4 * w * 0.46
            pv_end.append(pe)
            if j == TPB * (b + 1) - 1:
                dve = max(dve, pe + 150) + OUT_NS
                out_free = dve - OUT_NS + 800
        order.append(seg)
    assert len(step_end) == NSTEP
    return order, pe


SCHEDULE, _ = schedule()


def side_order():
    order, waiting = [], None
    for event in SCHEDULE:
        if event[0] == "values":
            if waiting is not None:
                order.append(waiting)
                waiting = None
            k = event[1]
            b, j, _ = UNITS[k % NU]
            if j == TPB * (b + 1) - 1:
                waiting = ("output", k // NU * NB + b)
        elif event[0] == "step":
            order.append(event)
            if waiting is not None:
                order.append(waiting)
                waiting = None
    order.append(waiting)
    return order


SIDE_ORDER = side_order()


ACC_ORDER = [("out", p) for p in range(NT // 2)] + [("down", p) for p in range(NT // 2)]
EARLY_OUTS = NT // 2 - 2
TAIL_UNIT = NG * NU - TPB * NB + 2
assert all(e[0] != "step" for e in SCHEDULE[SCHEDULE.index(("values", TAIL_UNIT)):])


TR_AFTER = (0, 2)


LN_ORDER = [(0, b) for b in range(NB)] + [(1, 0), (1, 1), (1, 2), (2, 0), (1, 3), (2, 1), (2, 2), (2, 3)] + [(3, b) for b in range(NB)]


def xn_buffer(n, b):
    def buffer(m, c):
        at = LN_ORDER.index((m, c)) - NB * (1 if m else 0)
        return c % 2 if m == 0 else (2, 0, 1)[(at if m < 3 else c) % 3]
    mine = buffer(n, b)
    before = [x for x in LN_ORDER[:LN_ORDER.index((n, b))] if buffer(*x) == mine]
    return mine, before[-1] if before else None


def two_layers(nc, x, wq0, bq0, wk0, bk0, wv0, bv0, wo0, bo0, router0, gate_up0, down0, merge0, dominant0,
               wq1, bq1, wk1, bk1, wv1, bv1, wo1, bo1, router1, w1, b1, w2, b2, sw1, sb1, sw2, sb2,
               slope_parts, expert_of_row, out):
    with ExitStack() as ctx:
        def sb(name, shape, dt=F32):
            return ctx.enter_context(nc.sbuf_tensor(name, shape, dt))

        def sem(name):
            return ctx.enter_context(nc.semaphore(name))

        def sems(name, n):
            return [sem(f"{name}{i}") for i in range(n)]

        psum = ctx.enter_context(nc.psum_tensor("psum", [P, 8, TB], F32))

        xs = sb("xs", [P, NT, D])
        xT = sb("xT", [P, KD, T])
        yT = xT
        q_stack = sb("q_stack", [P, 2, NB, G, TB], BF16)
        k_stack = sb("k_stack", [P, 2, G, T], BF16)
        v_stage = sb("v_stage", [P, 2, NT, G, HD, 2])
        work = sb("work", [P, 8192])
        v_all = work[:, 0:NT * D].rearrange("p (i c) -> p i c", i=NT)
        probs = work[:, 4096:8192].rearrange("p (s k c) -> p s k c", s=4, k=2)
        qk_f = work[:, 4096:5120].rearrange("p (s c) -> p s c", s=2)
        qk_p = work[:, 5120:8192].bitcast(BF16).rearrange("p (s r c) -> p s r c", s=4, r=3)
        hidden = work[:, 0:MMAX * TB].rearrange("p (m c) -> p m c", m=MMAX)
        act_out = work[:, 5120:5120 + 2 * TB].rearrange("p (s c) -> p s c", s=2)
        act_up = work[:, 6144:6144 + 2 * TB].rearrange("p (s c) -> p s c", s=2)
        w_attn = sb("w_attn", [P, 4, KD, D])
        w_mix = sb("w_mix", [P, 5120])
        gate_w = w_mix[:, 0:KD * G0 * I0].rearrange("p (k c) -> p k c", k=KD)
        up_w = w_mix[:, 1536:1536 + KD * G0 * I0].rearrange("p (k c) -> p k c", k=KD)
        down_w = w_mix[:, 3072:3072 + M0 * D].rearrange("p (m c) -> p m c", m=M0)
        w1_s = w_mix[:, 0:KD * E1 * H1].rearrange("p (k e c) -> p k e c", k=KD, e=E1)
        sw1_s = w_mix[:, 2048:2048 + KD * D].rearrange("p (k c) -> p k c", k=KD)
        w2_s = w_mix[:, 2560:2560 + M1 * D].rearrange("p (m c) -> p m c", m=M1)
        area = sb("area", [P, 2560])
        y_n = area[:, 0:2 * TB].rearrange("p (s c) -> p s c", s=2)
        o_t = area[:, 1024:1024 + TB]
        mt = area[0:G * TPB, 1536:1536 + 2 * P].rearrange("p (s c) -> p s c", s=2)
        mr = area[0:G * TPB, 1792:1792 + 2 * P].rearrange("p (s c) -> p s c", s=2)
        mrow = area[0:G * TPB, 2048:2048 + 3 * P].bitcast(BF16).rearrange("p (s r c) -> p s r c", s=2, r=3)
        stats = sb("stats", [P, TPB, 6])
        mv = sb("mv", [P, TPB, 2])
        lnt = sb("lnt", [P, 4, TPB])
        rstd = sb("rstd", [P, TPB])
        ident = sb("ident", [P, P])
        ident_bf = sb("ident_bf", [P, P], BF16)
        tri = sb("tri", [P, P], BF16)
        zeros = sb("zeros", [G * TPB, P])
        bcol = sb("bcol", [P, 2, 2, KD])
        bcol4 = sb("bcol4", [P, 2, 2, KD])
        brow = sb("brow", [P, 5, D])
        hb = sb("hb", [P, M1])
        b2_s = sb("b2_s", [E1, D])
        r0_s = sb("r0_s", [P, KD, E0])
        r1_s = sb("r1_s", [P, KD, E1])
        dom = sb("dom", [1, G0], I32)
        merge_i = sb("merge_i", [3 * E0, 1], I32)
        merge_f = sb("merge_f", [3 * E0, 1])
        erow = sb("erow", [3 * E1, 1])
        slope_c = sb("slope_c", [3 * H, 1])
        spread0 = sb("spread0", [3 * E0, G0 * I0], BF16)
        spread1 = sb("spread1", [3 * E1, E1 * H1], BF16)
        iota8 = sb("iota8", [P, TPB, E1])
        qk_r = sb("qk_r", [P, 2, TB])
        xn = [area[:, 0:TPB * D].rearrange("p (q c) -> p q c", q=TPB),
              area[:, TPB * D:2 * TPB * D].rearrange("p (q c) -> p q c", q=TPB),
              qk_r.rearrange("p (s q) c -> p (s q c)", q=1).rearrange("p (q c) -> p q c", q=TPB)]
        mx = sb("mx", [P, G, NT, NB])
        nmax = sb("nmax", [P, G, TPB])
        o_r = sb("o_r", [P, TB // 32])
        o_n = sb("o_n", [P, TB])
        rt = sb("rt", [P, 6, TPB, E0])
        rmax = sb("rmax", [P, TPB, 8])
        ridx = sb("ridx", [P, TPB, 8], U32)
        rsmall = sb("rsmall", [P, 8, TPB])
        gparts = sb("gparts", [P, TPB, 3 * E0], BF16)
        gT = sb("gT", [3 * E0, TB], BF16)
        gTf = work[0:E1, 7168:7168 + TB]
        iota_g = work[0:3 * E0, 0:G0 * I0].rearrange("p (g c) -> p g c", g=G0)
        iota_e = work[0:3 * E1, 1024:1024 + E1 * H1].rearrange("p (e c) -> p e c", e=E1)
        slope_q = k_stack[0:3 * H, 0, 0, :]
        slope_k = k_stack[0:3 * H, 0, 1, :]
        zero_rows = k_stack[0:3 * H, 0, 2, :]
        pos_hi = k_stack[0:1, 1, 0, :]
        pos_lo = k_stack[0:1, 1, 1, :]

        q_parts = nc.dram_tensor("q_parts", [3, NG, NB, G, HD, TB], BF16, kind="Internal").ap()
        k_parts = nc.dram_tensor("k_parts", [3, D, T], BF16, kind="Internal").ap()
        slopes_q = nc.dram_tensor("slopes_q", [2, 3, H, TB], BF16, kind="Internal").ap()
        slopes_k = nc.dram_tensor("slopes_k", [2, 3, H, T], BF16, kind="Internal").ap()
        positions = nc.dram_tensor("positions", [2, T], BF16, kind="Internal").ap()

        x_in = sems("x_in", NB)
        wattn_in = sems("wattn_in", 2)
        wmix_in = sems("wmix_in", 2)
        small_in = sem("small_in")
        dom_in = sem("dom_in")
        const_pool = sem("const_pool")
        const_dve = sem("const_dve")
        table_out = sem("table_out")
        fixed_in = sem("fixed_in")
        ln_stat = sems("ln_stat", 4)
        ln_var = sems("ln_var", 4)
        ln_root = sems("ln_root", 4)
        ln_xn = sems("ln_xn", 4)
        ln_tr = sems("ln_tr", 4)
        ln_xT = sems("ln_xT", 4)
        pj_mm = sems("pj_mm", 2)
        pj_act = sems("pj_act", 2)
        pj_dve = sems("pj_dve", 2)
        pj_cut = sems("pj_cut", 2)
        pj_parts = sems("pj_parts", 2)
        pj_out = [sems(f"pj_out{l}_", 4) for l in range(2)]
        pj_v = sems("pj_v", 2)
        xb_done = sems("xb_done", 3)
        at_first = sems("at_first", 2)
        at_rest = sems("at_rest", 2)
        at_stack = sems("at_stack", 2)
        at_vst = sems("at_vst", 2)
        at_score = sems("at_score", 2)
        at_exp = sems("at_exp", 2)
        at_pv = sems("at_pv", 2)
        at_ofree = sems("at_ofree", 2)
        at_dve = sems("at_dve", 2)
        at_yn = sems("at_yn", 2)
        at_y = [sems(f"at_y{l}_", 2) for l in range(2)]
        a_mm = sems("a_mm", 2)
        a_max = sems("a_max", 2)
        a_nm = sems("a_nm", 2)
        a_cut = sems("a_cut", 2)
        a_split = sems("a_split", 2)
        a_row = [sems(f"a_row{l}_", 2) for l in range(2)]
        acc_mm = sems("acc_mm", 2)
        x_add = sems("x_add", 2)
        side_mm = sems("side_mm", 2)
        side_free = sems("side_free", 2)
        r_dve = sems("r_dve", 2)
        r_soft = sems("r_soft", 2)
        r_exp = sems("r_exp", 2)
        r_gates = sems("r_gates", 2)
        hid_mm = sems("hid_mm", 2)
        hid_act = sems("hid_act", 2)
        hid_up = sems("hid_up", 2)
        hid_done = sems("hid_done", 2)
        down_mm = sems("down_mm", 2)
        x_out = sem("x_out")

        SMALL = 19
        MIX_DMAS = 3 * G0 + sum(I0 * g % P + I0 > P for g in range(G0))
        CONST_POOL_1, CONST_POOL = 9, 15
        CONST_POOL_ONES = 10
        CONST_DVE_1, CONST_DVE = 3, 7
        A_W = ((wq0, wk0, wv0, wo0), (wq1, wk1, wv1, wo1))
        SIDE = (2 + M0, 3 + E1)
        GATE_ITEMS = (2, 3)

        block = ctx.enter_context(nc.Block())

        @block.sync
        def _(sp):
            xv = x.rearrange("a (i p) c -> p (a i) c", p=P)
            for b in range(NB):
                sp.dma_start(xs[:, b * TPB:(b + 1) * TPB, :], xv[:, b * TPB:(b + 1) * TPB, :]).then_inc(x_in[b], 16)

            def load_attn(l):
                for n, w in enumerate(A_W[l]):
                    sp.dma_start(w_attn[:, n, :, :], w.rearrange("(k p) c -> p k c", p=P)).then_inc(wattn_in[l], 16)

            load_attn(0)
            for l, (bq, bk, bv, bo) in enumerate(((bq0, bk0, bv0, bo0), (bq1, bk1, bv1, bo1))):
                for n, v in enumerate((bq, bk)):
                    sp.dma_start(bcol[:, l, n, :], v).then_inc(small_in, 16)
                for n, v in enumerate((bv, bo)):
                    sp.dma_start(brow[:, 2 * l + n, :], v.rearrange("(a c) -> a c", a=1).broadcast_to([P, D])).then_inc(small_in, 16)
            sp.dma_start(brow[:, 4, :], sb2.rearrange("(a c) -> a c", a=1).broadcast_to([P, D])).then_inc(small_in, 16)
            sp.dma_start(hb[:, 0:E1], b1).then_inc(small_in, 16)
            sp.dma_start(hb[:, E1:M1], sb1).then_inc(small_in, 16)
            sp.dma_start(b2_s[:, :], b2).then_inc(small_in, 16)
            sp.dma_start(r0_s[:, :, :], router0.rearrange("(k p) e -> p k e", p=P)).then_inc(small_in, 16)
            sp.dma_start(r1_s[:, :, :], router1.rearrange("(k p) e -> p k e", p=P)).then_inc(small_in, 16)
            for r in range(3):
                sp.dma_start(merge_i[r * E0:(r + 1) * E0, :], merge0.rearrange("(e a) -> e a", a=1)).then_inc(small_in, 16)
            sp.dma_start(erow[:, :], expert_of_row).then_inc(small_in, 16)
            sp.dma_start(slope_c[:, :], slope_parts).then_inc(small_in, 16)
            sp.dma_start(dom[:, :], dominant0.rearrange("(a g) -> a g", a=1)).then_inc(dom_in, 16)
            sp.wait_ge(const_dve, CONST_DVE_1)
            sp.wait_ge(const_pool, CONST_POOL_1)
            for l, (tq, tk) in enumerate(((zero_rows, zero_rows), (slope_q, slope_k))):
                sp.dma_start(slopes_q[l].rearrange("r h t -> (r h) t"), tq[:, 0:TB]).then_inc(table_out, 16)
                sp.dma_start(slopes_k[l].rearrange("r h t -> (r h) t"), tk).then_inc(table_out, 16)
            sp.dma_start(positions[0:1, :], pos_hi).then_inc(table_out, 16)
            sp.dma_start(positions[1:2, :], pos_lo).then_inc(table_out, 16)
            def load_positions(n):
                r, third = divmod(n, 3)
                if third == 0:
                    sp.dma_start(k_stack[R_SLOPE + 2 * r:R_SLOPE + 2 * r + 2, :, :, :].rearrange("a s h t -> a (s h) t"),
                                 positions.rearrange("a (b t) -> a b t", b=1).broadcast_to([2, 2 * G, T])).then_inc(fixed_in, 16)
                for at in ((0, 1), (2, 3, 4), (5, 6, 7))[third]:
                    par, b = divmod(at, NB)
                    pos = positions[:, b * TB:(b + 1) * TB].rearrange("a (h t) -> a h t", h=1)
                    sp.dma_start(q_stack[R_POS + 2 * r:R_POS + 2 * r + 2, par, b, :, :], pos.broadcast_to([2, G, TB])).then_inc(fixed_in, 16)

            def load_mix(l):
                if l == 0:
                    sp.wait_ge(dom_in, 16)
                    for g in range(G0):
                        e = sp.value_load(dom[0:1, g:g + 1], min_val=0, max_val=E0 - 1)
                        gu = gate_up0[bass.ds(e, 1), :, :].rearrange("a (k p) o -> p (a k) o", p=P)
                        sp.dma_start(gate_w[:, :, I0 * g:I0 * g + I0], gu[:, :, 0:I0]).then_inc(wmix_in[0], 16)
                        sp.dma_start(up_w[:, :, I0 * g:I0 * g + I0], gu[:, :, I0:2 * I0]).then_inc(wmix_in[0], 16)
                        dn = down0[bass.ds(e, 1), :, :].rearrange("a i c -> (a i) c")
                        r0 = I0 * g
                        n = min(I0, P - r0 % P)
                        sp.dma_start(down_w[r0 % P:r0 % P + n, r0 // P, :], dn[0:n, :]).then_inc(wmix_in[0], 16)
                        if n < I0:
                            sp.dma_start(down_w[0:I0 - n, r0 // P + 1, :], dn[n:I0, :]).then_inc(wmix_in[0], 16)
                else:
                    for k in range(KD):
                        sp.dma_start(w1_s[:, k, :, :], w1[:, k * P:(k + 1) * P, :].rearrange("e p c -> p e c")).then_inc(wmix_in[1], 16)
                    sp.dma_start(sw1_s, sw1.rearrange("(k p) c -> p k c", p=P)).then_inc(wmix_in[1], 16)
                    sp.dma_start(w2_s[:, 0:E1, :], w2.rearrange("e p c -> p e c")).then_inc(wmix_in[1], 16)
                    sp.dma_start(w2_s[:, E1:M1, :], sw2.rearrange("(k p) c -> p k c", p=P)).then_inc(wmix_in[1], 16)

            def load_slopes(l, group, signal):
                hs = slice(group * G, (group + 1) * G)
                par = group % 2
                for r in range(3):
                    sq = slopes_q[l, r, hs, :].rearrange("(a b h) t -> a b (h t)", a=1, b=1).broadcast_to([2, NB, G * TB])
                    sp.dma_start(q_stack[R_SLOPE + 2 * r:R_SLOPE + 2 * r + 2, par, :, :, :].rearrange("a b h t -> a b (h t)"), sq)\
                        .then_inc(signal, 16)
                    sk = slopes_k[l, r, hs, :].rearrange("(a h) t -> a (h t)", a=1).broadcast_to([2, G * T])
                    sp.dma_start(k_stack[R_POS + 2 * r:R_POS + 2 * r + 2, par, :, :].rearrange("a h t -> a (h t)"), sk)\
                        .then_inc(signal, 16)

            def load_parts(group, b0, b1, signal, products=range(6)):
                hs = slice(group * G, (group + 1) * G)
                par = group % 2
                for n in products:
                    rows = slice(R_QK + HD * n, R_QK + HD * n + HD)
                    qv = q_parts[Q_PARTS[n], group, b0:b1].rearrange("b h d t -> d (b h) t")
                    kv = k_parts[K_PARTS[n]].rearrange("(h d) t -> d h t", d=HD)
                    sp.dma_start(q_stack[rows, par, b0:b1, :, :].rearrange("d b h t -> d (b h) t"), qv).then_inc(signal, 16)
                    sp.dma_start(k_stack[rows, par, :, b0 * TB:b1 * TB], kv[:, hs, b0 * TB:b1 * TB]).then_inc(signal, 16)

            def load_stack(l, group):
                load_slopes(l, group, at_stack[l])
                load_parts(group, 0, NB, at_stack[l])

            def store_max(l, blk):
                grp, b = blk // NB, blk % NB
                sp.wait_ge(a_split[l], blk + 1)
                for r in range(3):
                    dst = q_stack[R_MAX + r:R_MAX + r + 1, grp % 2, b, :, :].rearrange("a h c -> a (h c)")
                    sp.dma_start(dst, mrow[:, b % 2, r, :]).then_inc(a_row[l][b % 2], 16)

            def store_y(l, blk):
                grp, b = blk // NB, blk % NB
                r0 = 64 * (grp % 2)
                sp.wait_ge(at_yn[l], blk + 1)
                sp.dma_start(yT[r0:r0 + 64, grp // 2, b * TB:(b + 1) * TB], y_n[0:P:2, b % 2, :]).then_inc(at_y[l][b % 2], 16)

            for l in range(2):
                for n in range(4 * NB):
                    b, which, m = n // 4, n % 4 // 2, n % 2
                    if b == 1:
                        sp.wait_ge(pj_out[l][n - 4], 16 * (2, 2, 1, 1)[n - 4])
                    sp.wait_ge(pj_parts[l], n + 1)
                    if which:
                        sp.dma_start(k_parts[:, m * P:(m + 1) * P, b * TB:(b + 1) * TB].rearrange("r p t -> p r t"),
                                     qk_p[:, n % 4, :, :]).then_inc(pj_out[l][n % 4], 16)
                    else:
                        for g in range(2):
                            sp.dma_start(q_parts[:, 2 * m + g, b].rearrange("r h d t -> (h d) r t"),
                                         qk_p[64 * g:64 * g + 64, n % 4, :, :]).then_inc(pj_out[l][n % 4], 16)
                    if l == 0 and 1 <= n <= 9:
                        if n == 1:
                            sp.wait_ge(table_out, 16 * 6)
                        load_positions(n - 1)
                    first = 8 if l == 0 else 7
                    if n == first:
                        if l == 0:
                            sp.wait_ge(const_pool, CONST_POOL_ONES)
                        load_slopes(l, 0, at_first[l])
                    elif first < n <= first + 3:
                        load_parts(0, 0, 1, at_first[l], (2 * (n - first) - 2, 2 * (n - first) - 1))
                for n in range(4):
                    sp.wait_ge(pj_out[l][n], 16 * (2, 2, 1, 1)[n] * NB)
                load_parts(0, 1, NB, at_rest[l])
                for what, n in SIDE_ORDER:
                    if what == "output":
                        store_y(l, n)
                        if n % NB == NB - 1 and n // NB + 2 < NG:
                            load_stack(l, n // NB + 2)
                    elif A_STEPS[n % NA][0] == "row":
                        blk = n // NA * NB + A_STEPS[n % NA][1]
                        store_max(l, blk)
                        if blk == 0:
                            load_stack(l, 1)
                        elif blk == 2:
                            if l == 1:
                                sp.wait_ge(down_mm[0], NT // 2)
                            load_mix(l)
                if l == 0:
                    sp.wait_ge(acc_mm[0], NT // 2)
                    load_attn(1)
            for b in range(NB):
                sp.wait_ge(x_add[1], ACC_ORDER.index(("down", 2 * b + 1)) + 1)
                sp.dma_start(out.rearrange("a (i p) c -> p (a i) c", p=P)[:, b * TPB:(b + 1) * TPB, :],
                             xs[:, b * TPB:(b + 1) * TPB, :]).then_inc(x_out, 16)
            sp.wait_ge(x_out, 16 * NB)

        @block.gpsimd
        def _(pool):
            pool.memset(ident[:, :], 0.0).then_inc(const_pool, 1)
            pool.memset(tri[:, :], 0.0).then_inc(const_pool, 1)
            pool.memset(zeros[:, :], 0.0).then_inc(const_pool, 1)
            pool.wait_ge(const_pool, 3)
            pool.affine_select(out=ident[:, :], in_=ident[:, :], compare_op=ALU.not_equal, fill=1.0, base=0,
                               pattern=[[-1, P]], channel_multiplier=1).then_inc(const_pool, 1)
            pool.affine_select(out=tri[:, :], in_=tri[:, :], compare_op=ALU.is_ge, fill=NEG, base=0,
                               pattern=[[-1, P]], channel_multiplier=1).then_inc(const_pool, 1)
            pool.iota(pos_hi.rearrange("p (a c) -> p a c", c=8), pattern=[[8, T // 8], [0, 8]], base=0,
                      channel_multiplier=0, allow_small_or_imprecise_dtypes=True).then_inc(const_pool, 1)
            pool.iota(pos_lo.rearrange("p (a c) -> p a c", c=8), pattern=[[0, T // 8], [1, 8]], base=0,
                      channel_multiplier=0, allow_small_or_imprecise_dtypes=True).then_inc(const_pool, 1)
            pool.memset(zero_rows, 0.0).then_inc(const_pool, 1)
            pool.wait_ge(const_pool, 4)
            pool.tensor_copy(ident_bf[:, :], ident[:, :]).then_inc(const_pool, 1)

            pool.wait_ge(const_pool, CONST_POOL_1)
            pool.memset(k_stack[96:P, :, :, :].rearrange("p s h t -> p (s h t)").bitcast(F32), ONES_PAIR).then_inc(const_pool, 1)
            pool.wait_ge(const_pool, CONST_POOL_ONES)

            def later_constants(b):
                if b == 1:
                    pool.iota(iota8[:, :, :], pattern=[[0, TPB], [1, E1]], base=0, channel_multiplier=0,
                              allow_small_or_imprecise_dtypes=True).then_inc(const_pool, 1)
                    pool.memset(v_stage[:, :, :, :, :, :], 1.0).then_inc(const_pool, 1)
                elif b == 2:
                    pool.iota(iota_g, pattern=[[1, G0], [0, I0]], base=0, channel_multiplier=0,
                              allow_small_or_imprecise_dtypes=True).then_inc(const_pool, 1)
                    pool.wait_ge(const_pool, CONST_POOL_1 + 4)
                    pool.iota(iota_e, pattern=[[1, E1], [0, H1]], base=0, channel_multiplier=0,
                              allow_small_or_imprecise_dtypes=True).then_inc(const_pool, 1)
                elif b == 3:
                    pool.memset(o_n[:, :], 0.0).then_inc(const_pool, 1)

            def add_row(n, row, b, after, value):
                pool.wait_ge(after, value)
                xv = xs[:, b * TPB:(b + 1) * TPB, :]
                pool.tensor_tensor(xv, xv, brow[:, row:row + 1, :].broadcast_to([P, TPB, D]), ALU.add).then_inc(xb_done[n], 1)

            def stage_v(l, grp):
                pool.tensor_copy(v_stage[:, grp % 2, :, :, :, 0],
                                 v_all[:, :, grp * G * HD:(grp + 1) * G * HD].rearrange("p i (h d) -> p i h d", d=HD)).then_inc(at_vst[l], 1)

            def split_max(l, n):
                b = A_STEPS[n % NA][1]
                blk = n // NA * NB + b
                s = b % 2
                base = 4 * blk
                pool.wait_ge(a_max[l], n + 1)
                if blk >= 2:
                    pool.wait_ge(a_row[l][s], 48 * (blk // 2))
                pool.tensor_tensor(mrow[:, s, 0, :], mt[:, s, :], zeros[0:G * TPB, :], ALU.add).then_inc(a_cut[l], 1)
                pool.wait_ge(a_cut[l], base + 1)
                pool.tensor_tensor(mr[:, s, :], mt[:, s, :], mrow[:, s, 0, :], ALU.subtract).then_inc(a_cut[l], 1)
                pool.wait_ge(a_cut[l], base + 2)
                pool.tensor_tensor(mrow[:, s, 1, :], mr[:, s, :], zeros[0:G * TPB, :], ALU.add).then_inc(a_cut[l], 1)
                pool.wait_ge(a_cut[l], base + 3)
                pool.tensor_tensor(mr[:, s, :], mr[:, s, :], mrow[:, s, 1, :], ALU.subtract).then_inc(a_cut[l], 1)
                pool.wait_ge(a_cut[l], base + 4)
                pool.tensor_tensor(mrow[:, s, 2, :], mr[:, s, :], zeros[0:G * TPB, :], ALU.add).then_inc(a_split[l], 1)

            for l in range(2):
                if l == 0:
                    pool.wait_ge(small_in, 16 * SMALL)
                for b in range(NB):
                    for n in range(4 * b, 4 * b + 4):
                        pool.wait_ge(pj_cut[l], n + 1)
                        pool.tensor_tensor(qk_p[:, n % 4, 2, :], qk_r[:, n % 2, :], qk_p[:, n % 4, 1, :], ALU.subtract).then_inc(pj_parts[l], 1)
                    if l == 0:
                        pool.wait_ge(pj_parts[0], 4 * (b + 1))
                        later_constants(b)
                        pool.wait_ge(const_pool, CONST_POOL_1 + (1, 3, 5, 6)[b])
                pool.wait_ge(pj_v[l], NT)
                stage_v(l, 0)
                for what, n in SIDE_ORDER:
                    if what == "output":
                        grp = n // NB + 2
                        if n % NB == NB - 1 and grp < NG:
                            pool.wait_ge(at_pv[l], (grp - 1) * NU)
                            stage_v(l, grp)
                    elif A_STEPS[n % NA][0] == "row":
                        split_max(l, n)
                        if n // NA == 0 and A_STEPS[n][1] == 1:
                            stage_v(l, 1)
                        elif n // NA == 0 and A_STEPS[n][1] == NB - 1:
                            for b in range(NB):
                                add_row(l, 2 * l + 1, b, ln_xn[2 * l], TPB * (b + 1))
                if l == 1:
                    for b in range(NB):
                        add_row(2, 4, b, ln_xn[3], TPB * (b + 1))

        @block.scalar
        def _(act):
            def ln_block(n, b):
                act.wait_ge(ln_var[n], b + 1)
                act.activation(lnt[:, 1, :], lnt[:, 0, :], ACT.Sqrt).then_inc(ln_root[n], 1)

            def ln_evac_part(n, b, k):
                act.wait_ge(ln_tr[n], KD * b + k + 1)
                act.activation(xT[:, k, b * TB:(b + 1) * TB], psum[:, TR_BANK, :], ACT.Copy).then_inc(ln_xT[n], 1)

            def ln_evac(n, b):
                for k in range(KD):
                    ln_evac_part(n, b, k)

            def project(l, b):
                for n in range(4):
                    which, m = n // 2, n % 2
                    count = 4 * b + n
                    bank = psum[:, HID_BANKS[n], :]
                    bias = (bcol4 if which == 0 else bcol)[:, l, which, m:m + 1]
                    scale = 0.25 if which == 0 else 1.0
                    act.wait_ge(pj_mm[l], count + 1)
                    if count >= 2:
                        act.wait_ge(pj_dve[l], count - 1)
                    if count >= 4:
                        act.wait_ge(pj_out[l][n], 16 * (2, 2, 1, 1)[n] * b)
                    act.activation(qk_p[:, count % 4, 0, :], bank, ACT.Identity, bias=bias, scale=scale).then_inc(pj_act[l], 1)
                    act.activation(qk_f[:, count % 2, :], bank, ACT.Identity, bias=bias, scale=scale).then_inc(pj_act[l], 1)

            for l in range(2):
                if l == 0:
                    ln_block(0, 0)
                    ln_block(0, 1)
                    ln_evac(0, 0)
                    act.wait_ge(const_dve, CONST_DVE_1)
                for b in range(NB):
                    if l == 0 and b + 1 < NB:
                        ln_evac(0, b + 1)
                    if l == 0 and b + 2 < NB:
                        ln_block(0, b + 2)
                    if l == 1 and b == 0:
                        ln_block(2, NB - 1)
                    if l == 1 and b == 1:
                        ln_evac(2, NB - 1)
                    project(l, b)
                for k in range(NG * NU):
                    w = UNITS[k % NU][2]
                    for hh in range(2):
                        act.wait_ge(at_score[l], 2 * k + hh + 1)
                        if hh == 0 and k >= 2:
                            act.wait_ge(at_pv[l], k - 1)
                        act.activation(probs[:, (2 * k + hh) % 4, :, 0:w], psum[:, 2 * hh:2 * hh + 2, 0:w], ACT.Exp).then_inc(at_exp[l], 1)

                def hidden_rows(b):
                    if l == 0:
                        for m in range(M0):
                            n = M0 * b + m
                            act.wait_ge(hid_mm[0], n + 1)
                            if n >= 2:
                                act.wait_ge(hid_up[0], n - 1)
                            act.activation(act_out[:, n % 2, :], psum[:, HID_BANKS[2 * (n % 2)], :], ACT.Silu).then_inc(hid_act[0], 1)
                            if b + 1 < NB and m - 2 in TR_AFTER:
                                ln_evac_part(1, b + 1, TR_AFTER.index(m - 2))
                    else:
                        for m in range(M1):
                            n = M1 * b + m
                            act.wait_ge(hid_mm[1], n + 1)
                            bank = psum[:, HID_BANKS[n % 4], :]
                            if m < E1:
                                q = E1 * b + m
                                if q >= 2:
                                    act.wait_ge(hid_done[1], q - 1)
                                act.activation(act_out[:, q % 2, :], bank, ACT.Gelu, bias=hb[:, m:m + 1]).then_inc(hid_act[1], 1)
                            else:
                                act.activation(hidden[:, m, :], bank, ACT.Gelu, bias=hb[:, m:m + 1]).then_inc(hid_act[1], 1)
                            if b + 1 < NB and m - 2 in TR_AFTER:
                                ln_evac_part(3, b + 1, TR_AFTER.index(m - 2))

                def route(b):
                    if l == 0:
                        act.wait_ge(side_free[0], GATE_ITEMS[0] * b + 1)
                        act.activation(rt[:, 1, :, :], rt[:, 0, :, :], ACT.Exp).then_inc(r_exp[l], 1)
                    else:
                        act.wait_ge(r_soft[1], b + 1)
                        act.activation(rsmall[:, 1, :], rsmall[:, 0, :], ACT.Exp).then_inc(r_exp[l], 1)

                ln_block(2 * l + 1, 0)
                ln_evac(2 * l + 1, 0)
                route(0)
                for b in range(NB):
                    if b + 1 < NB:
                        ln_block(2 * l + 1, b + 1)
                    hidden_rows(b)
                    if b + 1 < NB:
                        route(b + 1)
                    if l == 0 and b:
                        ln_block(2, b - 1)
                        ln_evac(2, b - 1)

        @block.tensor
        def _(pe):
            def transpose_part(n, b, k):
                buf, _ = xn_buffer(n, b)
                at = LN_ORDER.index((n, b))
                if k == 0:
                    pe.wait_ge(ln_xn[n], TPB * (b + 1))
                    if at:
                        m, c = LN_ORDER[at - 1]
                        pe.wait_ge(ln_xT[m], KD * (c + 1))
                else:
                    pe.wait_ge(ln_xT[n], KD * b + k)
                for q in range(TPB):
                    last = pe.transpose(psum[:, TR_BANK, q * P:(q + 1) * P], xn[buf][:, q, k * P:(k + 1) * P], ident[:, :])
                last.then_inc(ln_tr[n], 1)

            def transpose_rows(n, b):
                for k in range(KD):
                    transpose_part(n, b, k)

            def project(l, b):
                if b == 0:
                    pe.wait_ge(wattn_in[l], 64)
                pe.wait_ge(ln_xT[2 * l], KD * (b + 1))
                for n in range(4):
                    which, m = n // 2, n % 2
                    if b:
                        pe.wait_ge(pj_act[l], 2 * (4 * (b - 1) + n + 1))
                    for k in range(KD):
                        last = pe.matmul(psum[:, HID_BANKS[n], :], w_attn[:, which, k, m * P:(m + 1) * P], xT[:, k, b * TB:(b + 1) * TB],
                                         start=(k == 0), stop=(k == KD - 1))
                    last.then_inc(pj_mm[l], 1)

            def project_values(l):
                for n in range(NT // 2):
                    if n < 4:
                        pe.wait_ge(pj_act[l], 2 * (4 * (NB - 1) + n + 1))
                    else:
                        pe.wait_ge(pj_v[l], 2 * (n - 4) + 2)
                    for q in range(2):
                        i = 2 * n + q
                        for k in range(KD):
                            last = pe.matmul(psum[:, HID_BANKS[n % 4], q * D:(q + 1) * D], xT[:, k, i * P:(i + 1) * P], w_attn[:, 2, k, :],
                                             start=(k == 0), stop=(k == KD - 1))
                    last.then_inc(pj_mm[l], 1)
                    for step in early_steps(n):
                        step_mm(l, step)

            def step_mm(l, n):
                grp, (kind, what) = n // NA, A_STEPS[n % NA]
                slot = psum[:, A_BANKS[n % 3], :]
                par = grp % 2
                if n >= 3:
                    pe.wait_ge(a_max[l], n - 2)
                if kind == "row":
                    pe.wait_ge(a_nm[l], grp * NB + what + 1)
                    last = pe.transpose(slot[0:G * TPB, 0:P], nmax[:, :, :].rearrange("p h i -> p (h i)"), ident[:, :])
                    last.then_inc(a_mm[l], 1)
                    return
                if n == 0:
                    pe.wait_ge(at_first[l], STACK_DMAS * 16)
                    if l == 0:
                        pe.wait_ge(const_pool, CONST_POOL_ONES)
                        pe.wait_ge(fixed_in, 16 * 3 * (1 + 2 * NB))
                elif n == EARLY + 1:
                    pe.wait_ge(at_rest[l], REST_DMAS * 16)
                elif n % NA == 0:
                    pe.wait_ge(at_stack[l], grp * STACK_DMAS * 16)
                i, h0, nh, s0, w = what
                for h in range(nh):
                    diag = s0 + w == (i + 1) * P
                    dst = slot[:, h * w:(h + 1) * w]
                    last = pe.matmul(dst, q_stack[0:KA, par, i // TPB, h0 + h, i % TPB * P:(i % TPB + 1) * P], k_stack[0:KA, par, h0 + h, s0:s0 + w],
                                     start=True, stop=not diag)
                    if diag:
                        last = pe.matmul(dst[:, w - P:w], ident_bf[:, :], tri[:, :], start=False, stop=True)
                last.then_inc(a_mm[l], 1)

            def scores(l, k, hh):
                grp, (b, j, w) = k // NU, UNITS[k % NU]
                if j == 0 and hh == 0:
                    pe.wait_ge(a_row[l][b % 2], 48 * (grp * 2 + b // 2 + 1))
                if k:
                    pe.wait_ge(at_exp[l], 2 * (k - 1) + hh + 1)
                for h in (2 * hh, 2 * hh + 1):
                    diag = j >= TPB * b
                    last = pe.matmul(psum[:, h, 0:w], k_stack[0:KB, grp % 2, h, j * P:(j + 1) * P], q_stack[0:KB, grp % 2, b, h, TB - w:TB],
                                     start=True, stop=not diag)
                    if diag:
                        last = pe.matmul(psum[:, h, 0:P], tri[:, :], ident_bf[:, :], start=False, stop=True)
                last.then_inc(at_score[l], 1)

            def values(l, k):
                grp, (b, j, w) = k // NU, UNITS[k % NU]
                blk = grp * NB + b
                if j == 0:
                    if blk:
                        pe.wait_ge(at_ofree[l], blk)
                    if b == 0:
                        pe.wait_ge(at_vst[l], grp + 1)
                pe.wait_ge(at_exp[l], 2 * k + 2)
                for h in range(G):
                    last = pe.matmul(psum[32 * h:32 * h + 32, O_BANK, TB - w:TB], v_stage[:, grp % 2, j, h, :, :].rearrange("p d a -> p (d a)"),
                                     probs[:, (2 * k + h // 2) % 4, h % 2, 0:w], start=(j == 0), stop=(j == TPB * (b + 1) - 1),
                                     skip_group_check=True)
                last.then_inc(at_pv[l], 1)

            def out_pair(l, pair):
                if pair % 2 == 0:
                    b = pair // 2
                    blk = NBLK - NB + b
                    pe.wait_ge(at_y[l][b % 2], 16 * (blk // 2 + 1))
                if pair >= 2:
                    pe.wait_ge(x_add[l], pair - 1)
                elif pair == 0:
                    pe.wait_ge(a_max[l], NSTEP)
                for q in range(2):
                    i = 2 * pair + q
                    for k in range(KD):
                        last = pe.matmul(psum[:, ACC_BANKS[pair % 2], q * D:(q + 1) * D], yT[:, k, i * P:(i + 1) * P], w_attn[:, 3, k, :],
                                         start=(k == 0), stop=(k == KD - 1))
                last.then_inc(acc_mm[l], 1)


            def logits(l, b):
                pe.wait_ge(ln_xT[2 * l + 1], KD * (b + 1))
                if b:
                    pe.wait_ge(hid_done[l], (M0 if l == 0 else E1) * b)
                ne, w = (E0, r0_s) if l == 0 else (E1, r1_s)
                for q in range(TPB):
                    i = TPB * b + q
                    for k in range(KD):
                        last = pe.matmul(psum[:, SIDE_BANK, q * ne:(q + 1) * ne], xT[:, k, i * P:(i + 1) * P], w[:, k, :],
                                         start=(k == 0), stop=(k == KD - 1))
                last.then_inc(side_mm[l], 1)

            def gate_rows(l, b):
                ne = 3 * (E0 if l == 0 else E1)
                pe.wait_ge(r_gates[l], b + 1)
                pe.wait_ge(side_free[l], GATE_ITEMS[l] * b + 1)
                bank = psum[:, SIDE_BANK, :].bitcast(BF16)
                for q in range(TPB):
                    last = pe.transpose(bank[0:ne, q * P:(q + 1) * P], gparts[:, q, 0:ne], ident_bf[:, :])
                last.then_inc(side_mm[l], 1)

            def gate_rows_exact(b):
                pe.wait_ge(side_free[1], GATE_ITEMS[1] * b + 2)
                for q in range(TPB):
                    last = pe.transpose(psum[0:E1, SIDE_BANK, q * P:(q + 1) * P], rt[:, 5, q, 0:E1], ident[:, :])
                last.then_inc(side_mm[1], 1)

            def spread(l, b, m):
                if m == 0:
                    pe.wait_ge(side_free[l], GATE_ITEMS[l] * (b + 1))
                else:
                    pe.wait_ge(hid_done[l], (M0 if l == 0 else E1) * b + m)
                lhs = spread0[:, m * P:(m + 1) * P] if l == 0 else spread1[:, m * P:(m + 1) * P]
                ne = 3 * (E0 if l == 0 else E1)
                pe.matmul(psum[:, SIDE_BANK, :], lhs, gT[0:ne, :], start=True, stop=True).then_inc(side_mm[l], 1)

            def hidden_mm(l, b, m):
                xb = lambda k: xT[:, k, b * TB:(b + 1) * TB]
                if l == 0:
                    n = M0 * b + m
                    if n >= 2:
                        pe.wait_ge(hid_act[0], n - 1)
                        pe.wait_ge(hid_up[0], n - 1)
                    for s, w in enumerate((gate_w, up_w)):
                        for k in range(KD):
                            last = pe.matmul(psum[:, HID_BANKS[2 * (n % 2) + s], :], w[:, k, m * P:(m + 1) * P], xb(k),
                                             start=(k == 0), stop=(k == KD - 1))
                else:
                    n = M1 * b + m
                    if n >= 4:
                        pe.wait_ge(hid_act[1], n - 3)
                    for k in range(KD):
                        w = w1_s[:, k, m, :] if m < E1 else sw1_s[:, k, (m - E1) * P:(m - E1 + 1) * P]
                        last = pe.matmul(psum[:, HID_BANKS[n % 4], :], w, xb(k), start=(k == 0), stop=(k == KD - 1))
                last.then_inc(hid_mm[l], 1)

            def down_pair(l, b, s):
                pair = 2 * b + s
                pe.wait_ge(x_add[l], ACC_ORDER.index(("down", pair)) - 1)
                mm = M0 if l == 0 else M1
                w = down_w if l == 0 else w2_s
                for q in range(2):
                    c0 = (2 * s + q) * P
                    dst = psum[:, ACC_BANKS[pair % 2], q * D:(q + 1) * D]
                    if l == 1:
                        pe.matmul(dst, gTf[:, c0:c0 + P], b2_s[:, :], start=True, stop=False)
                    for m in range(mm):
                        last = pe.matmul(dst, hidden[:, m, c0:c0 + P], w[:, m, :], start=(m == 0 and l == 0), stop=(m == mm - 1))
                last.then_inc(down_mm[l], 1)

            pe.wait_ge(const_pool, 4)
            for l in range(2):
                if l == 0:
                    transpose_rows(0, 0)
                for b in range(NB):
                    if l == 0 and b + 1 < NB:
                        transpose_rows(0, b + 1)
                    if l == 1 and b == 1:
                        transpose_rows(2, NB - 1)
                    project(l, b)
                project_values(l)
                pe.wait_ge(pj_act[l], 8 * NB)
                pe.wait_ge(pj_v[l], NT)
                if l == 0:
                    pe.wait_ge(const_pool, CONST_POOL)
                    pe.wait_ge(const_dve, CONST_DVE)
                for event in SCHEDULE:
                    if event[0] == "step":
                        if event[1] >= EARLY:
                            step_mm(l, event[1])
                    elif event[0] == "scores":
                        scores(l, event[1], event[2])
                    else:
                        values(l, event[1])
                        pair = event[1] - TAIL_UNIT
                        if 0 <= pair < EARLY_OUTS:
                            out_pair(l, pair)
                transpose_rows(2 * l + 1, 0)
                pe.wait_ge(at_exp[l], 2 * NG * NU)
                logits(l, 0)
                pe.wait_ge(at_ofree[l], NBLK)
                pe.wait_ge(wmix_in[l], 16 * (MIX_DMAS if l == 0 else 5))
                for b in range(NB):
                    mm = M0 if l == 0 else M1
                    me = M0 if l == 0 else E1
                    hidden_mm(l, b, 0)
                    if l == 0 and b >= 2:
                        transpose_part(2, b - 2, 1)
                    hidden_mm(l, b, 1)
                    gate_rows(l, b)
                    ahead = 2
                    if l == 1:
                        hidden_mm(l, b, 2)
                        gate_rows_exact(b)
                        ahead = 3
                    for m in range(mm):
                        if m < me:
                            spread(l, b, m)
                        if m + ahead < mm:
                            hidden_mm(l, b, m + ahead)
                        if b + 1 < NB and m in TR_AFTER:
                            transpose_part(2 * l + 1, b + 1, TR_AFTER.index(m))
                    if b + 1 < NB:
                        if b == 0:
                            out_pair(l, EARLY_OUTS)
                            out_pair(l, EARLY_OUTS + 1)
                        logits(l, b + 1)
                    pe.wait_ge(hid_done[l], me * (b + 1))
                    if l == 1:
                        pe.wait_ge(hid_act[1], M1 * (b + 1))
                    down_pair(l, b, 0)
                    down_pair(l, b, 1)
                    if l == 0 and b:
                        transpose_part(2, b - 1, 0)
                        if b == NB - 1:
                            transpose_part(2, b - 1, 1)

        @block.vector
        def _(dve):
            V = nc.vector

            def ln_statistics(n, b):
                if n == 0:
                    dve.wait_ge(x_in[b], 16)
                else:
                    kind, l = ("out", n // 2) if n % 2 else ("down", n // 2 - 1)
                    dve.wait_ge(x_add[l], ACC_ORDER.index((kind, 2 * b + 1)) + 1)
                for q in range(TPB):
                    V.bn_stats(stats[:, q, :], xs[:, b * TPB + q, :]).then_inc(ln_stat[n], 1)
                base = b * 13
                for q in range(TPB):
                    dve.wait_ge(ln_stat[n], base + q + 1)
                    V.bn_aggr(mv[:, q, :], stats[:, q, :]).then_inc(ln_stat[n], 1)
                dve.wait_ge(ln_stat[n], base + 8)
                V.tensor_scalar(lnt[:, 0, :], mv[:, :, 1], EPS, None, ALU.add).then_inc(ln_var[n], 1)

            def ln_rows(n, b):
                base = b * 13
                dve.wait_ge(ln_root[n], b + 1)
                V.reciprocal(rstd[:, :], lnt[:, 1, :]).then_inc(ln_stat[n], 1)
                dve.wait_ge(ln_stat[n], base + 9)
                V.tensor_tensor(lnt[:, 2, :], rstd[:, :], rstd[:, :], ALU.mult).then_inc(ln_stat[n], 1)
                dve.wait_ge(ln_stat[n], base + 10)
                V.tensor_tensor(lnt[:, 3, :], lnt[:, 2, :], lnt[:, 0, :], ALU.mult).then_inc(ln_stat[n], 1)
                dve.wait_ge(ln_stat[n], base + 11)
                V.tensor_scalar(lnt[:, 2, :], lnt[:, 3, :], -0.5, 1.5, ALU.mult, ALU.add).then_inc(ln_stat[n], 1)
                dve.wait_ge(ln_stat[n], base + 12)
                V.tensor_tensor(lnt[:, 3, :], lnt[:, 2, :], rstd[:, :], ALU.mult).then_inc(ln_stat[n], 1)
                dve.wait_ge(ln_stat[n], base + 13)
                buf, before = xn_buffer(n, b)
                if before is not None:
                    dve.wait_ge(ln_tr[before[0]], KD * (before[1] + 1))
                if n % 2 and b == 1:
                    for par in range(2):
                        dve.wait_ge(at_y[n // 2][par], 16 * NBLK // 2)
                for q in range(TPB):
                    V.tensor_scalar(xn[buf][:, q, :], xs[:, b * TPB + q, :], mv[:, q, 0:1], lnt[:, 3, q:q + 1],
                                    ALU.subtract, ALU.mult).then_inc(ln_xn[n], 1)

            def layer_norm(n, b):
                ln_statistics(n, b)
                ln_rows(n, b)

            def project(l, b):
                for n in range(4):
                    count = 4 * b + n
                    s, r = count % 4, count % 2
                    dve.wait_ge(pj_act[l], 2 * count + 2)
                    if count >= 2:
                        dve.wait_ge(pj_parts[l], count - 1)
                    V.tensor_tensor(qk_r[:, r, :], qk_f[:, r, :], qk_p[:, s, 0, :], ALU.subtract).then_inc(pj_dve[l], 1)
                    dve.wait_ge(pj_dve[l], count + 1)
                    V.tensor_copy(qk_p[:, s, 1, :], qk_r[:, r, :]).then_inc(pj_cut[l], 1)

            def project_values(l):
                for i in range(NT):
                    if i and i % 2 == 0:
                        for step in early_steps(i // 2 - 1):
                            step_max(l, step)
                    dve.wait_ge(pj_mm[l], 4 * NB + i // 2 + 1)
                    V.tensor_tensor(v_all[:, i, :], psum[:, HID_BANKS[i // 2 % 4], i % 2 * D:(i % 2 + 1) * D], brow[:, 2 * l, :],
                                    ALU.add).then_inc(pj_v[l], 1)

            def step_max(l, n):
                kind, what = A_STEPS[n % NA]
                slot = psum[:, A_BANKS[n % 3], :]
                if kind == "max":
                    i, h0, nh, s0, w = what
                    dve.wait_ge(a_mm[l], n + 1)
                    V.tensor_reduce(mx[:, h0:h0 + nh, i, s0 // TB], slot[:, 0:nh * w].rearrange("p (h c) -> p h c", h=nh),
                                    AX.X, ALU.max).then_inc(a_max[l], 1)
                else:
                    blk = n // NA * NB + what
                    dve.wait_ge(a_max[l], n)
                    V.tensor_reduce(nmax[:, :, :], mx[:, :, what * TPB:(what + 1) * TPB, :], AX.X, ALU.max,
                                    negate=True).then_inc(a_nm[l], 1)
                    dve.wait_ge(a_mm[l], n + 1)
                    if blk >= 2:
                        dve.wait_ge(a_split[l], blk - 1)
                    V.tensor_copy(mt[:, what % 2, :], slot[0:G * TPB, 0:P]).then_inc(a_max[l], 1)

            def output(l, blk):
                grp, b = blk // NB, blk % NB
                dve.wait_ge(at_pv[l], grp * NU + sum(1 for v in UNITS if v[0] <= b))
                V.transpose(o_t, psum[:, O_BANK, :]).then_inc(at_ofree[l], 1)
                dve.wait_ge(at_ofree[l], blk + 1)
                ov = o_t.rearrange("p (k d a) -> p k d a", d=HD, a=2)
                nv = o_n[:, :].rearrange("p (k d a) -> p k d a", d=HD, a=2)
                V.reciprocal(o_r[:, :], ov[:, :, 0, 1]).then_inc(at_dve[l], 1)
                dve.wait_ge(at_dve[l], 2 * blk + 1)
                V.tensor_tensor(nv[:, :, :, 0], ov[:, :, :, 0], o_r[:, :].rearrange("p (k a) -> p k a", a=1).broadcast_to([P, TB // 32, HD]),
                                ALU.mult).then_inc(at_dve[l], 1)
                dve.wait_ge(at_dve[l], 2 * blk + 2)
                if blk >= 2:
                    dve.wait_ge(at_y[l][b % 2], 16 * (blk // 2))
                V.transpose(y_n[:, b % 2, :], o_n[:, :]).then_inc(at_yn[l], 1)

            def add_acc(l, kind, pair):
                if kind == "out":
                    dve.wait_ge(acc_mm[l], pair + 1)
                    dve.wait_ge(xb_done[l], NB)
                else:
                    dve.wait_ge(down_mm[l], pair + 1)
                    if l == 1:
                        dve.wait_ge(xb_done[2], pair // 2 + 1)
                xv = xs[:, 2 * pair:2 * pair + 2, :]
                V.tensor_tensor(xv, psum[:, ACC_BANKS[pair % 2], :].rearrange("p (i c) -> p i c", i=2), xv, ALU.add).then_inc(x_add[l], 1)

            def bc(a, w):
                return a.rearrange("p (q a) -> p q a", a=1).broadcast_to([P, TPB, w])

            def step(l, ins):
                count[l] += 1
                ins.then_inc(r_dve[l], 1)
                dve.wait_ge(r_dve[l], count[l])

            count = [0, 0]

            def cut_gates(l, b, src, ne):
                rest = rt[:, 4, :, 0:ne]
                gp = lambda r: gparts[:, :, r * ne:(r + 1) * ne]
                step(l, V.tensor_copy(gp(0), src))
                step(l, V.tensor_tensor(rest, src, gp(0), ALU.subtract))
                step(l, V.tensor_copy(gp(1), rest))
                step(l, V.tensor_tensor(rest, rest, gp(1), ALU.subtract))
                V.tensor_copy(gp(2), rest).then_inc(r_gates[l], 1)

            def route0(b):
                lg = psum[:, SIDE_BANK, 0:TPB * E0].rearrange("p (q e) -> p q e", q=TPB)
                dve.wait_ge(side_mm[0], SIDE[0] * b + 1)
                step(0, V.tensor_reduce(rsmall[:, 0, :], lg, AX.X, ALU.max))
                V.tensor_tensor(rt[:, 0, :, :], lg, bc(rsmall[:, 0, :], E0), ALU.subtract).then_inc(side_free[0], 1)
                dve.wait_ge(r_exp[0], b + 1)
                for q in range(TPB):
                    V.max(rmax[:, q, :], rt[:, 1, q, :]).then_inc(r_dve[0], 1)
                count[0] += TPB
                dve.wait_ge(r_dve[0], count[0])
                for q in range(TPB):
                    V.match_replace(rt[:, 2, q, :], rmax[:, q, :], rt[:, 1, q, :], 0.0).then_inc(r_dve[0], 1)
                count[0] += TPB
                dve.wait_ge(r_dve[0], count[0])
                step(0, V.tensor_reduce(rsmall[:, 1, :], rmax[:, :, :], AX.X, ALU.add))
                step(0, V.reciprocal(rsmall[:, 2, :], rsmall[:, 1, :]))
                step(0, V.tensor_tensor(rt[:, 3, :, :], rt[:, 1, :, :], rt[:, 2, :, :], ALU.subtract))
                step(0, V.tensor_tensor(rt[:, 5, :, :], rt[:, 3, :, :], bc(rsmall[:, 2, :], E0), ALU.mult))
                if b:
                    dve.wait_ge(side_mm[0], SIDE[0] * (b - 1) + 2)
                cut_gates(0, b, rt[:, 5, :, :], E0)

            def route1(b):
                lg = rt[:, 0, :, 0:E1]
                dve.wait_ge(side_mm[1], SIDE[1] * b + 1)
                V.tensor_copy(lg, psum[:, SIDE_BANK, 0:TPB * E1].rearrange("p (q e) -> p q e", q=TPB)).then_inc(side_free[1], 1)
                dve.wait_ge(side_free[1], GATE_ITEMS[1] * b + 1)
                for q in range(TPB):
                    V.max(rmax[:, q, :], lg[:, q, :]).then_inc(r_dve[1], 1)
                count[1] += TPB
                dve.wait_ge(r_dve[1], count[1])
                V.tensor_tensor(rsmall[:, 0, :], rmax[:, :, 1], rmax[:, :, 0], ALU.subtract).then_inc(r_soft[1], 1)
                for q in range(TPB):
                    V.max_index(ridx[:, q, :], rmax[:, q, :], lg[:, q, :]).then_inc(r_dve[1], 1)
                count[1] += TPB
                dve.wait_ge(r_dve[1], count[1])
                step(1, V.tensor_copy(rsmall[:, 4, :], ridx[:, :, 0]))
                step(1, V.tensor_copy(rsmall[:, 5, :], ridx[:, :, 1]))
                dve.wait_ge(r_exp[1], b + 1)
                step(1, V.tensor_scalar(rsmall[:, 2, :], rsmall[:, 1, :], 1.0, None, ALU.add))
                step(1, V.reciprocal(rsmall[:, 3, :], rsmall[:, 2, :]))
                step(1, V.tensor_tensor(rsmall[:, 6, :], rsmall[:, 1, :], rsmall[:, 3, :], ALU.mult))
                first, second = rt[:, 1, :, 0:E1], rt[:, 2, :, 0:E1]
                step(1, V.tensor_tensor(first, iota8[:, :, :], bc(rsmall[:, 4, :], E1), ALU.is_equal))
                step(1, V.tensor_tensor(second, iota8[:, :, :], bc(rsmall[:, 5, :], E1), ALU.is_equal))
                step(1, V.tensor_tensor(first, first, bc(rsmall[:, 3, :], E1), ALU.mult))
                step(1, V.tensor_tensor(second, second, bc(rsmall[:, 6, :], E1), ALU.mult))
                if b:
                    dve.wait_ge(side_mm[1], SIDE[1] * (b - 1) + 3)
                step(1, V.tensor_tensor(rt[:, 5, :, 0:E1], first, second, ALU.add))
                cut_gates(1, b, rt[:, 5, :, 0:E1], E1)

            def mixture(l, b):
                me = M0 if l == 0 else E1
                ne = 3 * (E0 if l == 0 else E1)
                n0 = SIDE[l] * b + 1
                if b:
                    dve.wait_ge(side_mm[l], SIDE[l] * b)
                dve.wait_ge(side_mm[l], n0 + 1)
                V.tensor_copy(gT[0:ne, :], psum[:, SIDE_BANK, :].bitcast(BF16)[0:ne, 0:TB]).then_inc(side_free[l], 1)
                if l == 1:
                    dve.wait_ge(side_mm[1], n0 + 2)
                    V.tensor_copy(gTf, psum[0:E1, SIDE_BANK, :]).then_inc(side_free[1], 1)
                first = n0 + (1 if l == 0 else 2)
                for m in range(me):
                    q = me * b + m
                    if l == 0:
                        dve.wait_ge(hid_act[0], q + 1)
                        V.tensor_tensor(act_up[:, q % 2, :], psum[:, HID_BANKS[2 * (q % 2) + 1], :], act_out[:, q % 2, :],
                                        ALU.mult).then_inc(hid_up[0], 1)
                        dve.wait_ge(hid_up[0], q + 1)
                    else:
                        dve.wait_ge(hid_act[1], M1 * b + m + 1)
                    src = act_up if l == 0 else act_out
                    if m == 0 and b:
                        dve.wait_ge(down_mm[l], 2 * b)
                    dve.wait_ge(side_mm[l], first + m + 1)
                    V.tensor_tensor(hidden[:, m, :], psum[:, SIDE_BANK, :], src[:, q % 2, :], ALU.mult).then_inc(hid_done[l], 1)

            def first_constants():
                dve.wait_ge(small_in, 16 * SMALL)
                V.tensor_scalar(bcol4[:, :, :, :], bcol[:, :, :, :], 0.25, None, ALU.mult).then_inc(const_dve, 1)
                dve.wait_ge(const_pool, CONST_POOL_1)
                V.tensor_scalar(slope_q, zero_rows, slope_c[:, 0:1], None, ALU.add).then_inc(const_dve, 1)
                V.tensor_scalar(slope_k, zero_rows, slope_c[:, 0:1], None, ALU.subtract).then_inc(const_dve, 1)

            def later_constants():
                V.memset(mx[:, :, :, :], NEG).then_inc(const_dve, 1)
                V.tensor_copy(merge_f[:, :], merge_i[:, :]).then_inc(const_dve, 1)
                dve.wait_ge(const_pool, CONST_POOL)
                dve.wait_ge(const_dve, CONST_DVE_1 + 2)
                V.tensor_scalar(spread1[:, :], iota_e.rearrange("p e c -> p (e c)"), erow[:, 0:1], None, ALU.is_equal).then_inc(const_dve, 1)
                V.tensor_scalar(spread0[:, :], iota_g.rearrange("p e c -> p (e c)"), merge_f[:, 0:1], None, ALU.is_equal).then_inc(const_dve, 1)
                dve.wait_ge(const_dve, CONST_DVE)

            for l in range(2):
                if l == 0:
                    layer_norm(0, 0)
                    layer_norm(0, 1)
                    first_constants()
                else:
                    layer_norm(2, NB - 1)
                for b in range(NB):
                    if l == 0 and b + 2 < NB:
                        layer_norm(0, b + 2)
                    project(l, b)
                if l == 0:
                    later_constants()
                project_values(l)
                for what, n in SIDE_ORDER:
                    if what == "step":
                        if n >= EARLY:
                            step_max(l, n)
                        continue
                    if n == NBLK - 1:
                        for pair in range(EARLY_OUTS):
                            add_acc(l, "out", pair)
                        layer_norm(2 * l + 1, 0)
                    output(l, n)
                route = (route0, route1)[l]
                route(0)
                for b in range(NB):
                    if b + 1 < NB:
                        layer_norm(2 * l + 1, b + 1)
                    mixture(l, b)
                    if b == 0:
                        add_acc(l, "out", EARLY_OUTS)
                        add_acc(l, "out", EARLY_OUTS + 1)
                    if b + 1 < NB:
                        route(b + 1)
                    if l == 0 and b:
                        layer_norm(2, b - 1)
                    add_acc(l, "down", 2 * b)
                    add_acc(l, "down", 2 * b + 1)


def slope_constants():
    import math

    import numpy as np

    start = 2 ** (-2 ** (-(math.log2(H) - 3)))
    s = np.array([start * start ** i for i in range(H)], np.float32)
    parts = []
    for _ in range(3):
        top = (s.view(np.uint32) & np.uint32(0xFFFF0000)).view(np.float32)
        parts.append(top)
        s = s - top
    return np.stack(parts, 0).reshape(3 * H, 1).copy()


def kernel(**inputs):
    import numpy as _np
    import concourse.bacc as _bacc
    from concourse import mybir as _mybir
    from concourse.bass_utils import run_bass_kernel_spmd as _run

    def a(name):
        return _np.asarray(inputs[name])

    def column(v):
        return v.reshape(-1, P).T

    def heads_in(w):
        return w.transpose(1, 0, 2).reshape(D, D)

    arrays = [
        ("x", a("L0_attn_x")),
        ("wq0", heads_in(a("L0_attn_Wq"))), ("bq0", column(a("L0_attn_bq"))),
        ("wk0", heads_in(a("L0_attn_Wk"))), ("bk0", column(a("L0_attn_bk"))),
        ("wv0", heads_in(a("L0_attn_Wv"))), ("bv0", a("L0_attn_bv").reshape(-1)),
        ("wo0", a("L0_attn_Wo")), ("bo0", a("L0_attn_bo")),
        ("router0", a("L0_ffn_gate_weight").T),
        ("gate_up0", a("L0_ffn_gate_up_proj").transpose(0, 2, 1)),
        ("down0", a("L0_ffn_down_proj").transpose(0, 2, 1)),
        ("merge0", a("L0_ffn_merge_groups")), ("dominant0", a("L0_ffn_dominant_experts")),
        ("wq1", a("L1_attn_Wq").T), ("bq1", column(a("L1_attn_bq"))),
        ("wk1", a("L1_attn_Wk").T), ("bk1", column(a("L1_attn_bk"))),
        ("wv1", a("L1_attn_Wv").T), ("bv1", a("L1_attn_bv")),
        ("wo1", a("L1_attn_Wo").T), ("bo1", a("L1_attn_bo")),
        ("router1", a("L1_ffn_gate_w")),
        ("w1", a("L1_ffn_w1")), ("b1", column(a("L1_ffn_b1"))), ("w2", a("L1_ffn_w2")), ("b2", a("L1_ffn_b2")),
        ("sw1", a("L1_ffn_shared_w1")), ("sb1", column(a("L1_ffn_shared_b1"))),
        ("sw2", a("L1_ffn_shared_w2")), ("sb2", a("L1_ffn_shared_b2")),
        ("slope_parts", slope_constants()),
        ("expert_of_row", (_np.arange(3 * E1) % E1).astype(_np.float32).reshape(-1, 1)),
    ]
    nc = _bacc.Bacc("TRN2", target_bir_lowering=False, num_devices=1)
    sent, args = {}, []
    for name, v in arrays:
        v = _np.ascontiguousarray(v)
        sent[name] = v
        args.append(nc.dram_tensor(name, v.shape, _mybir.dt.from_np(v.dtype), kind="ExternalInput").ap())
    args.append(nc.dram_tensor("out", (1, T, D), _mybir.dt.float32, kind="ExternalOutput").ap())
    two_layers(nc, *args)
    r = _run(nc, [sent], core_ids=[0])
    return r.results[0]["out"]
```
